# Optimizing a Trainium2 kernel written in Bass

```python
import numpy as np
import jax
import jax.numpy as jnp

def _softmax(x, axis=-1):
    return jax.nn.softmax(x, axis=axis)

def _gelu(x):
    return jax.nn.gelu(x, approximate=True)

def _silu(x):
    return jax.nn.silu(x)

def _sigmoid(x):
    return jax.nn.sigmoid(x)

def _layernorm(x, axis=-1, eps=1e-05):
    m = jnp.mean(x, axis=axis, keepdims=True)
    v = jnp.var(x, axis=axis, keepdims=True)
    return (x - m) / jnp.sqrt(v + eps)

def _scatter_add(tgt, idx, src, axis=0):
    return tgt.at[idx].add(src)

def _segment_sum(src, seg, n):
    return jax.ops.segment_sum(src, seg, n)
kernel_name = 'mk_gps_d1_gnn_r32_6dd17e'

def setup_inputs(seed: int=0):
    np.random.seed(seed)
    _w = jnp.asarray

    def _rec_inputs():
        import jax
        import jax.numpy as jnp
        _gk = jax.random.key(seed)
        x = -8.776e-05 + 1 * jax.random.normal(jax.random.fold_in(_gk, 1), (3125, 256), jnp.float32)
        _s = jax.random.randint(jax.random.fold_in(_gk, 2), (25000,), 0, 3125, jnp.int32)
        _d = jax.random.randint(jax.random.fold_in(_gk, 3), (25000,), 0, 3125, jnp.int32)
        _loop = jnp.arange(3125, dtype=jnp.int32)
        src = jnp.concatenate([_s, _d, _loop])
        dst = jnp.concatenate([_d, _s, _loop])
        _o = jnp.argsort(dst, stable=True)
        src = src[_o]
        dst = dst[_o]
        edge_attr_64 = 0.000151818 + 1.00006 * jax.random.normal(jax.random.fold_in(_gk, 11), (53125, 64), jnp.float32)
        edge_weight = jax.random.uniform(jax.random.fold_in(_gk, 13), (53125,), jnp.float32, 0.0, 4.99999)
        return (x, src, dst, edge_attr_64, edge_weight)
    x, src, dst, edge_attr_64, edge_weight = _rec_inputs()

    def _L0_gnn_setup():
        import jax, jax.numpy as jnp
        import numpy as np
        H = 256
        R = 64
        N = 625
        E = 10000
        CUTOFF_LO = 0.0
        CUTOFF_UP = 5.0
        LN_EPS = 1e-05

        def _layernorm(x, g, b):
            mu = jnp.mean(x, axis=-1, keepdims=True)
            var = jnp.var(x, axis=-1, keepdims=True)
            return (x - mu) * jax.lax.rsqrt(var + LN_EPS) * g + b

        def _cosine_cutoff(r):
            c = 0.5 * (jnp.cos(r * (jnp.pi / CUTOFF_UP)) + 1.0)
            return c * (r < CUTOFF_UP).astype(r.dtype)
        key = jax.random.key(seed)
        ks = jax.random.split(key, 16)

        def xavier(k, shape):
            fan_in, fan_out = (shape[1], shape[0])
            lim = np.sqrt(6.0 / (fan_in + fan_out))
            return jax.random.uniform(k, shape, jnp.float32, -lim, lim)
        x = jax.random.normal(ks[0], (N, H), jnp.float32)
        edge_index = jax.random.randint(ks[1], (2, E), 0, N, jnp.int64)
        edge_weight = jax.random.uniform(ks[2], (E,), jnp.float32, 0.0, CUTOFF_UP)
        edge_attr = jax.random.normal(ks[3], (E, R), jnp.float32)
        return {'x': x, 'edge_index': edge_index, 'edge_weight': edge_weight, 'edge_attr': edge_attr, 'ln_g': jnp.ones((H,), jnp.float32), 'ln_b': jnp.zeros((H,), jnp.float32), 'Wq': xavier(ks[4], (H, H)), 'bq': jnp.zeros((H,), jnp.float32), 'Wk': xavier(ks[5], (H, H)), 'bk': jnp.zeros((H,), jnp.float32), 'Wv': xavier(ks[6], (H, H)), 'bv': jnp.zeros((H,), jnp.float32), 'Wo': xavier(ks[7], (H, H)), 'bo': jnp.zeros((H,), jnp.float32), 'Wdk': xavier(ks[8], (H, R)), 'bdk': jnp.zeros((H,), jnp.float32), 'Wdv': xavier(ks[9], (H, R)), 'bdv': jnp.zeros((H,), jnp.float32)}
    _L0_gnn_all = _L0_gnn_setup()
    _L0_gnn_in = {k: v for k, v in _L0_gnn_all.items() if k in ('ln_g', 'ln_b', 'Wq', 'bq', 'Wk', 'bk', 'Wv', 'bv', 'Wo', 'bo', 'Wdk', 'bdk', 'Wdv', 'bdv')}
    del _L0_gnn_all

    def _L0_mix_setup():
        import jax, jax.numpy as jnp
        import numpy as np
        NHEAD = 8
        ATT_EPS = 1e-06
        LN_EPS = 1e-05

        def _layernorm(x, g, b):
            mu = jnp.mean(x, axis=-1, keepdims=True)
            var = jnp.mean(jnp.square(x - mu), axis=-1, keepdims=True)
            return (x - mu) * jax.lax.rsqrt(var + LN_EPS) * g + b
        key = jax.random.key(seed)
        ks = jax.random.split(key, 7)
        N, L, C = (4, 512, 256)
        s = 1.0 / np.sqrt(C)
        return {'x': jax.random.normal(ks[0], (N, L, C), jnp.float32), 'Wq': jax.random.normal(ks[1], (C, C), jnp.float32) * s, 'Wk': jax.random.normal(ks[2], (C, C), jnp.float32) * s, 'Wv': jax.random.normal(ks[3], (C, C), jnp.float32) * s, 'Wm': jax.random.normal(ks[4], (C, C), jnp.float32) * s, 'W1': jax.random.normal(ks[5], (2 * C, 2 * C), jnp.float32) * (1.0 / np.sqrt(2 * C)), 'W2': jax.random.normal(ks[6], (2 * C, C), jnp.float32) * (1.0 / np.sqrt(2 * C)), 'g1': jnp.ones((C,), jnp.float32), 'b1': jnp.zeros((C,), jnp.float32), 'g2': jnp.ones((C,), jnp.float32), 'b2': jnp.zeros((C,), jnp.float32)}
    _L0_mix_all = _L0_mix_setup()
    _L0_mix_in = {k: v for k, v in _L0_mix_all.items() if k in ('Wq', 'Wk', 'Wv', 'Wm', 'W1', 'W2', 'g1', 'b1', 'g2', 'b2')}
    del _L0_mix_all

    def _L0_ffn_setup():
        import math
        import jax, jax.numpy as jnp
        import numpy as np
        CAPACITY_FACTOR = 1.25
        key = jax.random.key(seed)
        ks = jax.random.split(key, 5)
        B, L, D, F, E = (8, 256, 256, 1024, 8)
        h = jax.random.normal(ks[0], (B, L, D), dtype=jnp.float32)
        gate_w = jax.random.normal(ks[1], (D, E), dtype=jnp.float32) * 0.02
        gate_b = jnp.zeros((E,), dtype=jnp.float32)
        w1 = jax.random.normal(ks[2], (E, D, F), dtype=jnp.float32) * (1.0 / math.sqrt(D))
        b1 = jnp.zeros((E, F), dtype=jnp.float32)
        w2 = jax.random.normal(ks[3], (E, F, D), dtype=jnp.float32) * (1.0 / math.sqrt(F))
        b2 = jnp.zeros((E, D), dtype=jnp.float32)
        return {'h': h, 'gate_w': gate_w, 'gate_b': gate_b, 'w1': w1, 'b1': b1, 'w2': w2, 'b2': b2}
    _L0_ffn_all = _L0_ffn_setup()
    _L0_ffn_in = {k: v for k, v in _L0_ffn_all.items() if k in ('gate_w', 'gate_b', 'w1', 'b1', 'w2', 'b2')}
    del _L0_ffn_all
    return {'x': x, 'src': src, 'dst': dst, 'edge_attr_64': edge_attr_64, 'edge_weight': edge_weight, 'L0_gnn_ln_g': _L0_gnn_in['ln_g'], 'L0_gnn_ln_b': _L0_gnn_in['ln_b'], 'L0_gnn_Wq': _L0_gnn_in['Wq'], 'L0_gnn_bq': _L0_gnn_in['bq'], 'L0_gnn_Wk': _L0_gnn_in['Wk'], 'L0_gnn_bk': _L0_gnn_in['bk'], 'L0_gnn_Wv': _L0_gnn_in['Wv'], 'L0_gnn_bv': _L0_gnn_in['bv'], 'L0_gnn_Wo': _L0_gnn_in['Wo'], 'L0_gnn_bo': _L0_gnn_in['bo'], 'L0_gnn_Wdk': _L0_gnn_in['Wdk'], 'L0_gnn_bdk': _L0_gnn_in['bdk'], 'L0_gnn_Wdv': _L0_gnn_in['Wdv'], 'L0_gnn_bdv': _L0_gnn_in['bdv'], 'L0_mix_Wq': _L0_mix_in['Wq'], 'L0_mix_Wk': _L0_mix_in['Wk'], 'L0_mix_Wv': _L0_mix_in['Wv'], 'L0_mix_Wm': _L0_mix_in['Wm'], 'L0_mix_W1': _L0_mix_in['W1'], 'L0_mix_W2': _L0_mix_in['W2'], 'L0_mix_g1': _L0_mix_in['g1'], 'L0_mix_b1': _L0_mix_in['b1'], 'L0_mix_g2': _L0_mix_in['g2'], 'L0_mix_b2': _L0_mix_in['b2'], 'L0_ffn_gate_w': _L0_ffn_in['gate_w'], 'L0_ffn_gate_b': _L0_ffn_in['gate_b'], 'L0_ffn_w1': _L0_ffn_in['w1'], 'L0_ffn_b1': _L0_ffn_in['b1'], 'L0_ffn_w2': _L0_ffn_in['w2'], 'L0_ffn_b2': _L0_ffn_in['b2']}

def reference(x, src, dst, edge_attr_64, edge_weight, L0_gnn_ln_g, L0_gnn_ln_b, L0_gnn_Wq, L0_gnn_bq, L0_gnn_Wk, L0_gnn_bk, L0_gnn_Wv, L0_gnn_bv, L0_gnn_Wo, L0_gnn_bo, L0_gnn_Wdk, L0_gnn_bdk, L0_gnn_Wdv, L0_gnn_bdv, L0_mix_Wq, L0_mix_Wk, L0_mix_Wv, L0_mix_Wm, L0_mix_W1, L0_mix_W2, L0_mix_g1, L0_mix_b1, L0_mix_g2, L0_mix_b2, L0_ffn_gate_w, L0_ffn_gate_b, L0_ffn_w1, L0_ffn_b1, L0_ffn_w2, L0_ffn_b2):
    import jax
    import jax.numpy as jnp

    def _L0_gnn_ref(x, edge_index, edge_weight, edge_attr, ln_g, ln_b, Wq, bq, Wk, bk, Wv, bv, Wo, bo, Wdk, bdk, Wdv, bdv):
        import jax, jax.numpy as jnp
        import numpy as np
        H = 256
        R = 64
        N = 625
        E = 10000
        CUTOFF_LO = 0.0
        CUTOFF_UP = 5.0
        LN_EPS = 1e-05

        def _layernorm(x, g, b):
            mu = jnp.mean(x, axis=-1, keepdims=True)
            var = jnp.var(x, axis=-1, keepdims=True)
            return (x - mu) * jax.lax.rsqrt(var + LN_EPS) * g + b

        def _cosine_cutoff(r):
            c = 0.5 * (jnp.cos(r * (jnp.pi / CUTOFF_UP)) + 1.0)
            return c * (r < CUTOFF_UP).astype(r.dtype)
        src = edge_index[0]
        dst = edge_index[1]
        x_norm = _layernorm(x, ln_g, ln_b)
        q = x_norm @ Wq.T + bq
        k = x_norm @ Wk.T + bk
        v = x_norm @ Wv.T + bv
        dk = jax.nn.silu(edge_attr @ Wdk.T + bdk)
        dv = jax.nn.silu(edge_attr @ Wdv.T + bdv)
        q_i = q[dst]
        k_j = k[src]
        v_j = v[src]
        attn = jnp.sum(q_i * k_j * dk, axis=1)
        attn = jax.nn.silu(attn) * _cosine_cutoff(edge_weight)
        msg = v_j * dv * attn[:, None]
        agg = jax.ops.segment_sum(msg, dst, num_segments=x.shape[0])
        out = agg @ Wo.T + bo
        return x + out

    def _L0_mix_ref(x, Wq, Wk, Wv, Wm, W1, W2, g1, b1, g2, b2):
        import jax, jax.numpy as jnp
        import numpy as np
        NHEAD = 8
        ATT_EPS = 1e-06
        LN_EPS = 1e-05

        def _layernorm(x, g, b):
            mu = jnp.mean(x, axis=-1, keepdims=True)
            var = jnp.mean(jnp.square(x - mu), axis=-1, keepdims=True)
            return (x - mu) * jax.lax.rsqrt(var + LN_EPS) * g + b
        N, L, C = x.shape
        H = NHEAD
        D = C // H
        q = (x @ Wq).reshape(N, L, H, D)
        k = (x @ Wk).reshape(N, L, H, D)
        v = (x @ Wv).reshape(N, L, H, D)
        Q = jax.nn.elu(q) + 1.0
        K = jax.nn.elu(k) + 1.0
        v = v / L
        KV = jnp.einsum('nshd,nshv->nhdv', K, v)
        Z = 1.0 / (jnp.einsum('nlhd,nhd->nlh', Q, K.sum(axis=1)) + ATT_EPS)
        msg = jnp.einsum('nlhd,nhdv,nlh->nlhv', Q, KV, Z) * L
        msg = msg.reshape(N, L, C) @ Wm
        msg = _layernorm(msg, g1, b1)
        h = jnp.concatenate([x, msg], axis=-1) @ W1
        h = jax.nn.relu(h) @ W2
        msg = _layernorm(h, g2, b2)
        return x + msg

    def _L0_ffn_ref(h, gate_w, gate_b, w1, b1, w2, b2):
        import math
        import jax, jax.numpy as jnp
        import numpy as np
        CAPACITY_FACTOR = 1.25
        B, L, D = h.shape
        E = gate_w.shape[1]
        T = B * L
        C = max(1, math.ceil(CAPACITY_FACTOR * T / E))
        x = h.reshape(T, D)
        logits = x @ gate_w + gate_b
        probs = jax.nn.softmax(logits, axis=-1)
        idx = jnp.argmax(probs, axis=-1)
        prb = jnp.take_along_axis(probs, idx[:, None], axis=1)[:, 0]
        one_hot = jax.nn.one_hot(idx, E, dtype=jnp.float32)
        pos = (jnp.cumsum(one_hot, axis=0) * one_hot).sum(-1).astype(jnp.int32) - 1
        kept = pos < C
        pos_safe = jnp.where(kept, pos, C)
        buf = jnp.zeros((E, C, D), dtype=h.dtype).at[idx, pos_safe].set(x, mode='drop')
        hmid = jax.nn.relu(jnp.einsum('ecd,edf->ecf', buf, w1) + b1[:, None, :])
        ybuf = jnp.einsum('ecf,efd->ecd', hmid, w2) + b2[:, None, :]
        pos_g = jnp.minimum(pos, C - 1)
        y_tok = ybuf[idx, pos_g] * (prb * kept)[:, None]
        y = y_tok.reshape(B, L, D)
        y = jnp.nan_to_num(y, nan=0.0, posinf=10000.0, neginf=-10000.0)
        return y
    edge_index = jnp.stack([src, dst])
    xn = _layernorm(x, axis=-1)
    x = x + _L0_gnn_ref(xn, edge_index, edge_weight, edge_attr_64, L0_gnn_ln_g, L0_gnn_ln_b, L0_gnn_Wq, L0_gnn_bq, L0_gnn_Wk, L0_gnn_bk, L0_gnn_Wv, L0_gnn_bv, L0_gnn_Wo, L0_gnn_bo, L0_gnn_Wdk, L0_gnn_bdk, L0_gnn_Wdv, L0_gnn_bdv) + _L0_mix_ref(xn[None], L0_mix_Wq, L0_mix_Wk, L0_mix_Wv, L0_mix_Wm, L0_mix_W1, L0_mix_W2, L0_mix_g1, L0_mix_b1, L0_mix_g2, L0_mix_b2)[0]
    x = x + _L0_ffn_ref(_layernorm(x, axis=-1)[None], L0_ffn_gate_w, L0_ffn_gate_b, L0_ffn_w1, L0_ffn_b1, L0_ffn_w2, L0_ffn_b2)[0]
    return x

_drawn_inputs = setup_inputs


def setup_inputs(seed=0):
    import zlib

    import numpy as np

    out = dict(_drawn_inputs(seed))
    spreads = {'L0_gnn_ln_g': (1.0, 0.2),
     'L0_gnn_ln_b': (0.0, 0.1),
     'L0_gnn_bq': (0.0, 0.1),
     'L0_gnn_bk': (0.0, 0.1),
     'L0_gnn_bv': (0.0, 0.1),
     'L0_gnn_bo': (0.0, 0.411),
     'L0_gnn_bdk': (0.0, 0.1),
     'L0_gnn_bdv': (0.0, 0.1),
     'L0_mix_g1': (1.0, 0.2),
     'L0_mix_b1': (0.0, 0.585),
     'L0_mix_g2': (1.0, 0.2),
     'L0_mix_b2': (0.0, 0.413),
     'L0_ffn_gate_b': (0.0, 0.444),
     'L0_ffn_b1': (0.0, 2.0),
     'L0_ffn_b2': (0.0, 2.0)}
    factors = {'L0_ffn_w1': 2.751}
    for name, (base, spread) in spreads.items():
        noise = np.random.default_rng([zlib.crc32(name.encode()), seed]).standard_normal(out[name].shape)
        drawn = base * np.exp(spread * noise) if base else spread * noise
        out[name] = jnp.asarray(drawn.astype(out[name].dtype))
    for name, factor in factors.items():
        out[name] = (out[name] * factor).astype(out[name].dtype)
    return out
```

```python
import math

import concourse.bass as bass
from concourse import mybir
from contextlib import ExitStack

P = 128
NODES, EDGES, D, R = 3125, 53125, 256, 64
TILES = 26
ROWS = TILES * P
REAL_TILES = -(-NODES // P)
PAIR = 2
PAIRS = TILES // PAIR
QUAD, QUADS = 4, 4
CH = QUAD * QUADS
ROUNDS = 26
HALF = CH // 2
SLOTS = 8
NACC = 2
KE = R + 1
HEADS, HD = 8, D // 8
EXPERTS, FF = 8, 1024
FC = FF // P
CAP = max(1, math.ceil(1.25 * NODES / EXPERTS))
CT = 4
CPAD = CT * P
LN_EPS, ATT_EPS, CUTOFF = 1e-5, 1e-6, 5.0
KB = D // P
HB = HEADS // KB
ZW = P + HB
FAR = 1 << 20
BIG = 3.4028234e38

fp32, i32, u32 = mybir.dt.float32, mybir.dt.int32, mybir.dt.uint32
ALU = mybir.AluOpType
ACT = mybir.ActivationFunctionType
AX = mybir.AxisListType


class Own:

    def __init__(self, eng, sem, before=0, per=0, r=0):
        self.eng, self.sem, self.per, self.r = eng, sem, per, r
        self.start = self.n = before

    def link(self, ins):
        ins.then_inc(self.sem, 1)
        self.n += 1
        self.eng.wait_ge(self.sem, self.r * self.per + self.n)

    def rest(self, idle):
        self.eng.sem_inc(idle, 1)

    def closed(self):
        assert self.n - self.start == self.per, (self.n - self.start, self.per)


def tile_of(all_, t):
    return all_[:, bass.ds(t, 1), :].rearrange("p a c -> p (a c)")


def rows_of(table, t):
    return table.rearrange("(t p) c -> t p c", p=P)[bass.ds(t, 1), :, :].rearrange("a p c -> (a p) c")


def build_nodes(nc, sem, sb, banks, v):
    x_all, xn_all, ident, before, upto, ones = v["x_all"], v["xn_all"], v["ident"], v["before"], v["upto"], v["ones"]
    kv_sum, consts_made = v["kv_sum"], v["consts_made"]
    q_table, kv_table, acc, slots = v["q_table"], v["kv_table"], v["acc"], v["slots"]
    ctx = ExitStack()
    with ctx:
        def s(name): return sem("n_" + name, ctx)

        idle = s("idle")

        def b(name, shape, dt=fp32): return sb("n_" + name, shape, dt, ctx)

        ln_gb, bias = b("ln_gb", [P, 2, D]), b("bias", [P, 3 * D])
        w_gnn, w_kv = b("w_gnn", [P, KB, 3 * D]), b("w_kv", [P, KB, 2 * D])
        mask, zeros = b("mask", [P, TILES]), b("zeros", [P, 2048])
        stats, mv, rs = b("stats", [P, 2, 6]), b("mv", [P, 2, 2]), b("rs", [P, 2])
        stats2, mv2, rs2 = b("stats2", [P, 2, 6]), b("mv2", [P, 2, 2]), b("rs2", [P, 2])
        xn, xg = b("xn", [P, PAIR, D]), b("xg", [P, PAIR, D])
        xt, gt = b("xt", [P, PAIR, D]), b("gt", [P, PAIR, D])
        q, kv = b("q", [P, PAIR, D]), b("kv", [P, PAIR, 2 * D])
        neg, kpos, vext = b("neg", [P, PAIR, D]), b("kpos", [P, PAIR, D]), b("vext", [P, PAIR, KB, P + 1])

        x_in, w_in, zeros_made, zero_out = s("x_in"), s("w_in"), s("zeros_made"), s("zero_out")
        p_own, d_own, a_own = s("p_own"), s("d_own"), s("a_own")
        var, std, var2, std2, normed, turned, copied = (s(n) for n in "var std var2 std2 normed turned copied".split())
        q_done, kv_done, mix_done, q_ready, kv_ready, neg_ready, exp_ready = (
            s(n) for n in "q_done kv_done mix_done q_ready kv_ready neg_ready exp_ready".split())
        k_ready, v_ready, sums_done, round_done = (s(n) for n in "k_ready v_ready sums_done round_done".split())
        rows_out = s("rows_out")
        block = ctx.enter_context(nc.Block())

        @block.sync
        def _(sp):
            xr = v["x"].rearrange("(t p) c -> p t c", p=P)
            sp.dma_start(x_all[:, :, :], xr).then_inc(x_in, 16)
            sp.dma_start(ln_gb[:, :, :], v["ln_gb"]).then_inc(w_in, 16)
            sp.dma_start(bias[:, :], v["b_gnn"]).then_inc(w_in, 16)
            sp.dma_start(w_gnn[:, :, :], v["w_gnn"].rearrange("(k p) c -> p k c", p=P)).then_inc(w_in, 16)
            sp.dma_start(w_kv[:, :, :], v["w_mix"][:, D:3 * D].rearrange("(k p) c -> p k c", p=P)).then_inc(w_in, 16)
            sp.dma_start(mask[:, :], v["row_mask"]).then_inc(w_in, 16)
            sp.wait_ge(zeros_made, 1)
            sent, span = 0, 2048 // D
            for table, tiles in [(a, TILES + 1) for a in acc] + [(slots, (EXPERTS + 2) * CT)]:
                for t in range(0, tiles, span):
                    m = min(span, tiles - t)
                    sp.dma_start(table[t * P:(t + m) * P, :].rearrange("(t p) c -> p t c", p=P),
                                 zeros[:, 0:m * D].rearrange("p (t c) -> p t c", c=D)).then_inc(zero_out, 16)
                    sent += 1
            with sp.Fori(0, PAIRS) as r:
                for h in range(PAIR):
                    sp.wait_ge(q_ready, r * 2 + (h + 1))
                    sp.dma_start(rows_of(q_table, r * 2 + h), q[:, h, :]).then_inc(rows_out, 16)
                    sp.wait_ge(kv_ready, r * 2 + (h + 1))
                    sp.dma_start(rows_of(kv_table, r * 2 + h), kv[:, h, :]).then_inc(rows_out, 16)
                sp.wait_ge(rows_out, r * 64 + 64)
                sp.sem_inc(round_done, 1)
            sp.wait_ge(zero_out, 16 * sent)

        @block.gpsimd
        def _(g):
            own = Own(g, p_own)
            own.link(g.memset(ident[:, :], 0.0))
            own.link(g.memset(ones[:, :], 1.0))
            g.affine_select(out=ident[:, :], in_=ident[:, :], compare_op=ALU.not_equal, fill=1.0, base=0,
                            pattern=[[-1, P]], channel_multiplier=1).then_inc(consts_made, 1)
            g.affine_select(out=before[:, :], in_=ones[:, :], compare_op=ALU.is_gt, fill=0.0, base=0,
                            pattern=[[-1, P]], channel_multiplier=1).then_inc(consts_made, 1)
            g.affine_select(out=upto[:, :], in_=ones[:, :], compare_op=ALU.is_ge, fill=0.0, base=0,
                            pattern=[[1, P]], channel_multiplier=-1).then_inc(consts_made, 1)
            g.wait_ge(consts_made, 3)

        @block.vector
        def _(d):
            d.memset(zeros[:, :], 0.0).then_inc(zeros_made, 1)
            first = Own(d, d_own)
            first.link(d.memset(kv_sum[:, :, :], 0.0))
            d.sem_inc(round_done, 2)
            d.wait_ge(x_in, 16)
            d.wait_ge(w_in, 80)
            with d.Fori(0, PAIRS) as r:
                d.wait_ge(round_done, r * 2 + 2)
                own = Own(d, d_own, 1, 20, r)
                for h in range(PAIR):
                    own.rest(idle)
                    own.link(d.bn_stats(stats[:, h, :], tile_of(x_all, r * 2 + h)))
                    own.rest(idle)
                    own.link(d.bn_aggr(mv[:, h, :], stats[:, h, :]))
                    d.tensor_scalar(rs[:, h:h + 1], mv[:, h, 1:2], LN_EPS, None, ALU.add).then_inc(var, 1)
                for h in range(PAIR):
                    d.wait_ge(std, r * 2 + (h + 1))
                    own.link(d.reciprocal(rs[:, h:h + 1], rs[:, h:h + 1]))
                    own.link(d.tensor_scalar(xn[:, h, :], tile_of(x_all, r * 2 + h), mv[:, h, 0:1], rs[:, h:h + 1],
                                             ALU.subtract, ALU.mult))
                    own.link(d.bn_stats(stats2[:, h, :], xn[:, h, :]))
                    own.rest(idle)
                    own.link(d.bn_aggr(mv2[:, h, :], stats2[:, h, :]))
                    d.tensor_scalar(rs2[:, h:h + 1], mv2[:, h, 1:2], LN_EPS, None, ALU.add).then_inc(var2, 1)
                for h in range(PAIR):
                    d.wait_ge(std2, r * 2 + (h + 1))
                    own.link(d.reciprocal(rs2[:, h:h + 1], rs2[:, h:h + 1]))
                    own.link(d.tensor_scalar(xg[:, h, :], xn[:, h, :], mv2[:, h, 0:1], rs2[:, h:h + 1],
                                             ALU.subtract, ALU.mult))
                    own.link(d.tensor_tensor(xg[:, h, :], xg[:, h, :], ln_gb[:, 0, :], ALU.mult))
                    d.tensor_tensor(xg[:, h, :], xg[:, h, :], ln_gb[:, 1, :], ALU.add).then_inc(normed, 1)
                for h in range(PAIR):
                    d.wait_ge(q_done, r * 2 + (h + 1))
                    d.tensor_tensor(q[:, h, :], banks[4 * h + 1][:, 0:D], bias[:, 0:D], ALU.add).then_inc(q_ready, 1)
                    d.wait_ge(kv_done, r * 2 + (h + 1))
                    d.tensor_tensor(kv[:, h, :], banks[4 * h + 2][:, :], bias[:, D:3 * D], ALU.add).then_inc(kv_ready, 1)
                    d.wait_ge(mix_done, r * 2 + (h + 1))
                    d.tensor_scalar(neg[:, h, :], banks[4 * h + 3][:, 0:D], 0.0, None, ALU.min).then_inc(neg_ready, 1)
                for h in range(PAIR):
                    d.wait_ge(exp_ready, r * 2 + (h + 1))
                    d.scalar_tensor_tensor(out=kpos[:, h, :], in0=banks[4 * h + 3][:, 0:D], scalar=0.0, in1=neg[:, h, :],
                                           op0=ALU.max, op1=ALU.add).then_inc(k_ready, 1)
                for h in range(PAIR):
                    d.wait_ge(sums_done, r * 2 + (h + 1))
                    own.link(d.tensor_tensor(kv_sum[:, :, :], kv_sum[:, :, :],
                                             banks[4 * h][:, 0:KB * (P + 1)].rearrange("p (k c) -> p k c", k=KB), ALU.add))
                own.closed()
                d.sem_inc(round_done, 1)

        @block.scalar
        def _(a):
            a.wait_ge(w_in, 80)
            with a.Fori(0, PAIRS) as r:
                for h in range(PAIR):
                    a.wait_ge(var, r * 2 + (h + 1))
                    a.activation(rs[:, h:h + 1], rs[:, h:h + 1], ACT.Sqrt).then_inc(std, 1)
                for h in range(PAIR):
                    a.wait_ge(var2, r * 2 + (h + 1))
                    a.activation(rs2[:, h:h + 1], rs2[:, h:h + 1], ACT.Sqrt).then_inc(std2, 1)
                    a.activation(tile_of(xn_all, r * 2 + h), xn[:, h, :], ACT.Copy).then_inc(a_own, 1)
                for h in range(PAIR):
                    a.wait_ge(turned, r * 2 + (h + 1))
                    a.activation(xt[:, h, :], banks[4 * h][:, 0:D], ACT.Copy).then_inc(copied, 1)
                    a.activation(gt[:, h, :], banks[4 * h][:, D:2 * D], ACT.Copy).then_inc(copied, 1)
                for h in range(PAIR):
                    a.wait_ge(neg_ready, r * 2 + (h + 1))
                    a.activation(neg[:, h, :], neg[:, h, :], ACT.Exp).then_inc(exp_ready, 1)
                for h in range(PAIR):
                    a.wait_ge(k_ready, r * 2 + (h + 1))
                    for k in range(KB):
                        a.activation(vext[:, h, k, 0:P], banks[4 * h + 3][:, D + k * P:D + (k + 1) * P], ACT.Copy,
                                     scale=1.0 / NODES).then_inc(v_ready, 1)
                        a.activation(vext[:, h, k, P:P + 1], mask[:, bass.ds(r * 2 + h, 1)], ACT.Copy).then_inc(v_ready, 1)

        @block.tensor
        def _(t):
            t.wait_ge(consts_made, 3)
            t.wait_ge(w_in, 80)
            with t.Fori(0, PAIRS) as r:
                for h in range(PAIR):
                    t.wait_ge(normed, r * 2 + (h + 1))
                    for k in range(2 * KB):
                        half = (xn if k < KB else xg)[:, h, (k % KB) * P:(k % KB + 1) * P]
                        last = nc.tensor.transpose(banks[4 * h][:, k * P:(k + 1) * P], half, ident[:, :])
                    last.then_inc(turned, 1)
                for h in range(PAIR):
                    t.wait_ge(copied, r * 4 + (2 * h + 2))
                    for out_, lhs, w, signal in (
                            (banks[4 * h + 1][:, 0:D], gt, w_gnn[:, :, 0:D], q_done),
                            (banks[4 * h + 2][:, :], gt, w_gnn[:, :, D:3 * D], kv_done),
                            (banks[4 * h + 3][:, :], xt, w_kv, mix_done)):
                        for k in range(KB):
                            last = nc.tensor.matmul(out_, lhs[:, h, k * P:(k + 1) * P], w[:, k, :],
                                                    start=(k == 0), stop=(k == KB - 1))
                        last.then_inc(signal, 1)
                for h in range(PAIR):
                    t.wait_ge(k_ready, r * 2 + (h + 1))
                    t.wait_ge(v_ready, r * 8 + (4 * h + 4))
                    for k in range(KB):
                        last = nc.tensor.matmul(banks[4 * h][:, k * (P + 1):(k + 1) * (P + 1)],
                                                kpos[:, h, k * P:(k + 1) * P], vext[:, h, k, :], start=True, stop=True)
                    last.then_inc(sums_done, 1)


def build_mixer(nc, sem, sb, banks, v):
    x_all, xn_all, ident, kv_sum = v["x_all"], v["xn_all"], v["ident"], v["kv_sum"]
    ctx = ExitStack()
    with ctx:
        def s(name): return sem("m_" + name, ctx)

        idle = s("idle")

        def b(name, shape, dt=fp32): return sb("m_" + name, shape, dt, ctx)

        wq, wm = b("wq", [P, KB, D]), b("wm", [P, KB, D])
        w1, w2 = b("w1", [P, 2 * KB, 2 * D]), b("w2", [P, 2 * KB, D])
        gb = b("gb", [P, 4, D])
        heads = b("heads", [P, HB])
        sums = b("sums", [P, KB, ZW])
        xt = b("xt", [P, PAIR, D])
        stage = b("stage", [P, PAIR, D])
        neg, qt = b("neg", [P, PAIR, D]), b("qt", [P, PAIR, D])
        z, msg, mt = b("z", [P, PAIR, HEADS]), b("msg", [P, PAIR, D]), b("mt", [P, PAIR, D])
        nt, h1 = b("nt", [P, PAIR, D]), b("h1", [P, PAIR, 2 * D])
        stats, mv, rs = b("stats", [P, 2, 6]), b("mv", [P, 2, 2]), b("rs", [P, 2])
        names = ("w_in p_own d_own staged x_turned x_copied q_done neg_ready exp_ready q_ready num_done msg_ready "
                 "m_turned m_copied m_done var std n_ready n_turned n_copied h_done h_ready o_done round_done")
        (w_in, p_own, d_own, staged, x_turned, x_copied, q_done, neg_ready, exp_ready, q_ready, num_done, msg_ready,
         m_turned, m_copied, m_done, var, std, n_ready, n_turned, n_copied, h_done, h_ready, o_done, round_done) = (
            s(n) for n in names.split())
        block = ctx.enter_context(nc.Block())

        @block.sync
        def _(sp):
            for dst, src in ((wq[:, :, :], v["w_mix"][:, 0:D]), (wm[:, :, :], v["wm"]),
                             (w1[:, :, :], v["w1m"]), (w2[:, :, :], v["w2m"])):
                sp.dma_start(dst, src.rearrange("(k p) c -> p k c", p=P)).then_inc(w_in, 16)
            sp.dma_start(gb[:, :, :], v["gb_mix"]).then_inc(w_in, 16)
            sp.dma_start(heads[:, :], v["head_mask"]).then_inc(w_in, 16)
            sp.wait_ge(w_in, 96)

        @block.gpsimd
        def _(g):
            with g.Fori(0, PAIRS) as r:
                g.wait_ge(round_done, r + 1)
                for h in range(PAIR):
                    g.tensor_copy(stage[:, h, :], tile_of(xn_all, r * 2 + h)).then_inc(staged, 1)

        @block.vector
        def _(d):
            d.wait_ge(w_in, 96)
            first = Own(d, d_own)
            for k in range(KB):
                for c in range(HB):
                    first.link(d.tensor_scalar(sums[:, k, c * HD:(c + 1) * HD], kv_sum[:, k, c * HD:(c + 1) * HD],
                                               heads[:, c:c + 1], None, ALU.mult))
                first.link(d.tensor_scalar(sums[:, k, P:ZW], heads[:, :], kv_sum[:, k, P:P + 1], None, ALU.mult))
            d.sem_inc(round_done, 1)
            with d.Fori(0, PAIRS) as r:
                own = Own(d, d_own, KB * (HB + 1), 32, r)

                def norm(bank, g_, res):
                    for h in range(PAIR):
                        own.link(d.bn_stats(stats[:, h, :], banks[4 * h + bank][:, 0:D]))
                        own.rest(idle)
                        own.link(d.bn_aggr(mv[:, h, :], stats[:, h, :]))
                        d.tensor_scalar(rs[:, h:h + 1], mv[:, h, 1:2], LN_EPS, None, ALU.add).then_inc(var, 1)
                    for h in range(PAIR):
                        d.wait_ge(std, r * 4 + (res * 2 + h + 1))
                        own.link(d.reciprocal(rs[:, h:h + 1], rs[:, h:h + 1]))
                        own.link(d.tensor_scalar(msg[:, h, :], banks[4 * h + bank][:, 0:D], mv[:, h, 0:1], rs[:, h:h + 1],
                                                 ALU.subtract, ALU.mult))
                        own.link(d.tensor_tensor(msg[:, h, :], msg[:, h, :], gb[:, g_, :], ALU.mult))
                        last = d.tensor_tensor(msg[:, h, :], msg[:, h, :], gb[:, g_ + 1, :], ALU.add)
                        if res:
                            own.link(last)
                        else:
                            last.then_inc(n_ready, 1)

                for h in range(PAIR):
                    d.wait_ge(q_done, r * 2 + (h + 1))
                    d.tensor_scalar(neg[:, h, :], banks[4 * h + 1][:, 0:D], 0.0, None, ALU.min).then_inc(neg_ready, 1)
                for h in range(PAIR):
                    d.wait_ge(exp_ready, r * 2 + (h + 1))
                    d.scalar_tensor_tensor(out=qt[:, h, :], in0=banks[4 * h + 1][:, 0:D], scalar=0.0, in1=neg[:, h, :],
                                           op0=ALU.max, op1=ALU.add).then_inc(q_ready, 1)
                for h in range(PAIR):
                    d.wait_ge(num_done, r * 2 + (h + 1))
                    num = banks[4 * h + 2][:, 0:KB * ZW].rearrange("p (k c) -> p k c", k=KB)
                    own.link(d.tensor_scalar(z[:, h, :].rearrange("p (k c) -> p k c", k=KB), num[:, :, P:ZW],
                                             ATT_EPS, None, ALU.add))
                    own.link(d.reciprocal(z[:, h, :], z[:, h, :]))
                    own.link(d.tensor_scalar(z[:, h, :], z[:, h, :], float(NODES), None, ALU.mult))
                    for k in range(KB):
                        last = d.tensor_tensor(
                            msg[:, h, k * P:(k + 1) * P].rearrange("p (c e) -> p c e", e=HD),
                            num[:, k, 0:P].rearrange("p (c e) -> p c e", e=HD),
                            z[:, h, k * HB:(k + 1) * HB].unsqueeze(2).to_broadcast([P, HB, HD]), ALU.mult)
                        last.then_inc(msg_ready, 1)
                for h in range(PAIR):
                    d.wait_ge(m_done, r * 2 + (h + 1))
                norm(3, 0, 0)
                for h in range(PAIR):
                    d.wait_ge(o_done, r * 2 + (h + 1))
                norm(1, 2, 1)
                for h in range(PAIR):
                    res = tile_of(x_all, r * 2 + h)
                    own.link(d.scalar_tensor_tensor(out=stage[:, h, :], in0=stage[:, h, :], scalar=2.0, in1=res,
                                                    op0=ALU.mult, op1=ALU.add))
                    own.link(d.tensor_tensor(res, stage[:, h, :], msg[:, h, :], ALU.add))
                own.closed()
                d.sem_inc(round_done, 1)

        @block.scalar
        def _(a):
            with a.Fori(0, PAIRS) as r:
                for h in range(PAIR):
                    a.wait_ge(x_turned, r * 2 + (h + 1))
                    a.activation(xt[:, h, :], banks[4 * h][:, 0:D], ACT.Copy).then_inc(x_copied, 1)
                for h in range(PAIR):
                    a.wait_ge(neg_ready, r * 2 + (h + 1))
                    a.activation(neg[:, h, :], neg[:, h, :], ACT.Exp).then_inc(exp_ready, 1)
                for h in range(PAIR):
                    a.wait_ge(m_turned, r * 2 + (h + 1))
                    a.activation(mt[:, h, :], banks[4 * h][:, 0:D], ACT.Copy).then_inc(m_copied, 1)
                for h in range(PAIR):
                    a.wait_ge(var, r * 4 + (h + 1))
                    a.activation(rs[:, h:h + 1], rs[:, h:h + 1], ACT.Sqrt).then_inc(std, 1)
                for h in range(PAIR):
                    a.wait_ge(n_turned, r * 2 + (h + 1))
                    a.activation(nt[:, h, :], banks[4 * h][:, 0:D], ACT.Copy).then_inc(n_copied, 1)
                for h in range(PAIR):
                    a.wait_ge(h_done, r * 2 + (h + 1))
                    a.activation(h1[:, h, :], banks[4 * h + 2][:, :], ACT.Relu).then_inc(h_ready, 1)
                for h in range(PAIR):
                    a.wait_ge(var, r * 4 + (h + 3))
                    a.activation(rs[:, h:h + 1], rs[:, h:h + 1], ACT.Sqrt).then_inc(std, 1)

        @block.tensor
        def _(t):
            t.wait_ge(w_in, 96)
            with t.Fori(0, PAIRS) as r:
                def turn(rows, signal, ready, per):
                    for h in range(PAIR):
                        t.wait_ge(ready, r * 2 * per + per * (h + 1))
                        for k in range(KB):
                            last = nc.tensor.transpose(banks[4 * h][:, k * P:(k + 1) * P],
                                                       rows[:, h, k * P:(k + 1) * P], ident[:, :])
                        last.then_inc(signal, 1)

                turn(stage, x_turned, staged, 1)
                for h in range(PAIR):
                    t.wait_ge(x_copied, r * 2 + (h + 1))
                    for m in range(KB):
                        for k in range(KB):
                            last = nc.tensor.matmul(banks[4 * h + 1][:, m * P:(m + 1) * P], wq[:, k, m * P:(m + 1) * P],
                                                    xt[:, h, k * P:(k + 1) * P], start=(k == 0), stop=(k == KB - 1))
                    last.then_inc(q_done, 1)
                for h in range(PAIR):
                    t.wait_ge(q_ready, r * 2 + (h + 1))
                    for k in range(KB):
                        last = nc.tensor.matmul(banks[4 * h + 2][:, k * ZW:(k + 1) * ZW], qt[:, h, k * P:(k + 1) * P],
                                                sums[:, k, :], start=True, stop=True)
                    last.then_inc(num_done, 1)
                turn(msg, m_turned, msg_ready, KB)
                for h in range(PAIR):
                    t.wait_ge(m_copied, r * 2 + (h + 1))
                    for k in range(KB):
                        last = nc.tensor.matmul(banks[4 * h + 3][:, 0:D], mt[:, h, k * P:(k + 1) * P], wm[:, k, :],
                                                start=(k == 0), stop=(k == KB - 1))
                    last.then_inc(m_done, 1)
                turn(msg, n_turned, n_ready, 1)
                for h in range(PAIR):
                    t.wait_ge(n_copied, r * 2 + (h + 1))
                    for m in range(2 * KB):
                        for k in range(2 * KB):
                            rows = (xt if k < KB else nt)[:, h, (k % KB) * P:(k % KB + 1) * P]
                            last = nc.tensor.matmul(banks[4 * h + 2][:, m * P:(m + 1) * P], w1[:, k, m * P:(m + 1) * P],
                                                    rows, start=(k == 0), stop=(k == 2 * KB - 1))
                    last.then_inc(h_done, 1)
                for h in range(PAIR):
                    t.wait_ge(h_ready, r * 2 + (h + 1))
                    for k in range(2 * KB):
                        last = nc.tensor.matmul(banks[4 * h + 1][:, 0:D], h1[:, h, k * P:(k + 1) * P], w2[:, k, :],
                                                start=(k == 0), stop=(k == 2 * KB - 1))
                    last.then_inc(o_done, 1)


def build_edges(nc, sem, sb, banks, v):
    q_table, kv_table, acc, before = v["q_table"], v["kv_table"], v["acc"], v["before"]
    ALLC = (ROUNDS + 1) * CH
    ctx = ExitStack()
    with ctx:
        def s(name): return sem("e_" + name, ctx)

        def b(name, shape, dt=fp32): return sb("e_" + name, shape, dt, ctx)

        w = b("w", [KE, 2 * D])
        idx = b("idx", [P, 2, 2, HALF], i32)
        attr = b("attr", [KE, 2, HALF * P])
        row = b("row", [P, 2, HALF * P], i32)
        dst_i, dst_f, weight = b("dst_i", [P, ALLC], i32), b("dst_f", [P, ALLC]), b("weight", [P, ALLC])
        spare, cut, near = b("spare", [P, ALLC]), b("cut", [P, ALLC]), b("near", [P, ALLC])
        lane, half_pi = b("lane", [P, 1]), b("half_pi", [P, 1])
        kv, q, dkv = b("kv", [P, SLOTS, 2 * D]), b("q", [P, SLOTS, D]), b("dkv", [P, SLOTS, 2 * D])
        msg, total = b("msg", [P, SLOTS, D]), b("total", [P, SLOTS, D])
        same = b("same", [P, SLOTS, P])
        prod, earlier = b("prod", [P, 2, D]), b("earlier", [P, 2, P])
        score, gate, cnt = b("score", [P, 2, QUAD]), b("gate", [P, 2, QUAD]), b("cnt", [P, 2, QUAD])
        away, target = b("away", [P, 2, QUAD]), b("target", [P, 2, QUAD], i32)
        dq = b("dq", [P, 2, QUAD])

        once, half_in = s("once"), [s("half_in0"), s("half_in1")]
        rows_in = [s(f"rows_in{k}") for k in range(SLOTS)]
        scattered = [s(f"scattered{k}") for k in range(NACC)]
        proj_done, silu_done, msg_done, sum_done, total_ready, total_free = (
            s(n) for n in "proj_done silu_done msg_done sum_done total_ready total_free".split())
        score_ready, gate_ready, d_own, clamped, sine, tick, lane_made, zero_made, score_parts = (
            s(n) for n in "score_ready gate_ready d_own clamped sine tick lane_made zero_made score_parts".split())
        block = ctx.enter_context(nc.Block())

        MSG0, SILU0, TOT0, SUM0, FREE0 = SLOTS, 2, 2, SLOTS, SLOTS - NACC

        @block.sync
        def _(sp):
            def load(i, half):
                one = bass.ds(i, 1)
                at = half * HALF
                sp.dma_start(idx[:, half, 0, :], v["src"][one, :, at:at + HALF].rearrange("a p c -> (a p) c"))\
                  .then_inc(half_in[half], 16)
                sp.dma_start(attr[:, half, :], v["attr"][:, one, at * P:(at + HALF) * P].rearrange("k a c -> k (a c)"))\
                  .then_inc(half_in[half], 16)
                sp.dma_start(idx[:, half, 1, :], v["dst"][one, :, at:at + HALF].rearrange("a p c -> (a p) c"))\
                  .then_inc(half_in[half], 16)
                sp.dma_start(row[:, half, :],
                             v["dst_row"][one, at * P:(at + HALF) * P].to_broadcast([P, HALF * P]))\
                  .then_inc(half_in[half], 16)

            for half in range(2):
                load(0, half)
            sp.dma_start(w[:, :], v["w_edge"]).then_inc(once, 16)
            sp.dma_start(dst_i[:, :].rearrange("p (i c) -> p i c", c=CH), v["dst"].rearrange("i p c -> p i c")).then_inc(once, 16)
            sp.dma_start(weight[:, :].rearrange("p (i c) -> p i c", c=CH), v["weight"].rearrange("i p c -> p i c")).then_inc(once, 16)
            with sp.Fori(0, ROUNDS) as r:
                for half in range(2):
                    sp.wait_ge(msg_done, r * CH + ((half + 1) * HALF + MSG0))
                    load(r + 1, half)
            for half in range(2):
                sp.wait_ge(half_in[half], 64 * (ROUNDS + 1))

        @block.gpsimd
        def _(g):
            g.iota(lane[:, :], [[1, 1]], base=ROWS, channel_multiplier=1,
                   allow_small_or_imprecise_dtypes=True).then_inc(lane_made, 1)
            g.sem_inc(total_free, FREE0)

            def gather(quad, j):
                slot = (quad % 2) * QUAD + j
                half, at = (quad // 2) % 2, (quad % 2) * QUAD + j
                g.indirect_dma_start(kv[:, slot, :], None, kv_table,
                                     bass.IndirectOffsetOnAxis(ap=idx[:, half, 0, at:at + 1], axis=0))\
                 .then_inc(rows_in[slot], 16)
                g.indirect_dma_start(q[:, slot, :], None, q_table,
                                     bass.IndirectOffsetOnAxis(ap=idx[:, half, 1, at:at + 1], axis=0))\
                 .then_inc(rows_in[slot], 16)

            g.wait_ge(zero_made, 1)
            for k in range(NACC):
                g.dma_start(acc[k][0:P, :], total[:, k, :], accum_op=ALU.add).then_inc(scattered[k], 16)
            g.wait_ge(half_in[0], 64)
            for quad in range(2):
                for j in range(QUAD):
                    gather(quad, j)
            with g.Fori(0, ROUNDS) as r:
                for quad in range(QUADS):
                    if quad == 0:
                        g.wait_ge(half_in[1], r * 64 + 64)
                        g.sem_inc(tick, 1)
                    if quad == 2:
                        g.wait_ge(half_in[0], r * 64 + 128)
                        g.sem_inc(tick, 1)
                    for j in range(QUAD):
                        n = quad * QUAD + j
                        g.wait_ge(msg_done, r * CH + (n + 1 + MSG0))
                        g.sem_inc(tick, 1)
                        gather(quad + 2, j)
                        g.wait_ge(total_ready, r * CH + (n + 1 + TOT0))
                        g.wait_ge(scattered[j % NACC], r * (16 * CH // NACC) + 16 * (n // NACC + 1))
                        g.sem_inc(total_free, 1)
                        slot = (quad % 2) * QUAD + j
                        g.indirect_dma_start(acc[j % NACC], bass.IndirectOffsetOnAxis(
                            ap=target[:, quad % 2, j:j + 1], axis=0), total[:, slot, :], None, compute_op=ALU.add)\
                         .then_inc(scattered[j % NACC], 16)
            for k in range(NACC):
                g.wait_ge(scattered[k], 16 + 16 * ROUNDS * CH // NACC)
            for k in range(SLOTS):
                g.wait_ge(rows_in[k], 32 * (2 * ROUNDS + 1))

        @block.tensor
        def _(t):
            def project(r, n):
                half = (n // HALF) % 2
                if n % HALF == 0:
                    t.wait_ge(half_in[half], r * 64 + 64 * (1 + n // CH))
                t.wait_ge(silu_done, r * CH + (n + 1))
                nc.tensor.matmul(banks[n % 2][:, :], attr[:, half, (n % HALF) * P:(n % HALF + 1) * P], w[:, :],
                                 start=True, stop=True).then_inc(proj_done, 1)

            t.wait_ge(once, 48)
            for n in range(QUAD):
                project(0, n)
            with t.Fori(0, ROUNDS) as r:
                for quad in range(QUADS):
                    for j in range(QUAD):
                        project(r, (quad + 1) * QUAD + j)
                    for j in range(QUAD):
                        n = quad * QUAD + j
                        t.wait_ge(msg_done, r * CH + (n + 1 + MSG0))
                        t.wait_ge(total_ready, r * CH + (n + 1))
                        nc.tensor.matmul(banks[2 + n % 2][:, 0:D], same[:, n % SLOTS, :], msg[:, n % SLOTS, :],
                                         start=True, stop=True).then_inc(sum_done, 1)

        @block.scalar
        def _(a):
            def silus(r, quad):
                for j in range(QUAD):
                    n = quad * QUAD + j
                    a.wait_ge(proj_done, r * CH + (n + 1))
                    a.wait_ge(msg_done, r * CH + (n + 1))
                    a.activation(dkv[:, n % SLOTS, :], banks[n % 2][:, :], ACT.Silu).then_inc(silu_done, 1)

            a.sem_inc(silu_done, SILU0)
            a.sem_inc(total_ready, TOT0)
            a.wait_ge(clamped, 2)
            a.activation(cut[:, :], cut[:, :], ACT.Sin, bias=half_pi[:, 0:1], scale=-math.pi / CUTOFF).then_inc(sine, 1)
            silus(0, 0)
            with a.Fori(0, ROUNDS) as r:
                for quad in range(QUADS):
                    a.wait_ge(score_ready, r * QUADS + (quad + 1))
                    a.activation(gate[:, quad % 2, :], score[:, quad % 2, :], ACT.Silu).then_inc(gate_ready, 1)
                    silus(r, quad + 1)
                    for j in range(QUAD):
                        n = quad * QUAD + j
                        a.wait_ge(sum_done, r * CH + (n + 1 + SUM0))
                        a.wait_ge(total_free, r * CH + (n + 1))
                        a.activation(total[:, n % SLOTS, :], banks[2 + n % 2][:, 0:D], ACT.Copy).then_inc(total_ready, 1)

        @block.vector
        def _(d):
            d.memset(total[:, 0:NACC, :], 0.0).then_inc(zero_made, 1)
            d.sem_inc(msg_done, MSG0)
            d.sem_inc(sum_done, SUM0)
            first = Own(d, d_own)
            d.memset(half_pi[:, :], math.pi / 2).then_inc(clamped, 1)
            d.wait_ge(once, 48)
            d.wait_ge(lane_made, 1)
            d.tensor_scalar(cut[:, :], weight[:, :], CUTOFF, None, ALU.min).then_inc(clamped, 1)
            first.link(d.tensor_copy(dst_f[:, :], dst_i[:, :]))
            first.link(d.tensor_scalar(spare[:, :], dst_f[:, :], -1.0, lane[:, 0:1], ALU.mult, ALU.add))
            first.link(d.tensor_scalar(near[:, :], weight[:, :], CUTOFF, None, ALU.is_lt))
            d.wait_ge(sine, 1)
            first.link(d.tensor_scalar(cut[:, :], cut[:, :], 0.5, 0.5, ALU.mult, ALU.add))
            first.link(d.tensor_tensor(cut[:, :], cut[:, :], near[:, :], ALU.mult))

            def front(r, quad, own):
                par = quad % 2
                chunks = bass.ds(r * CH + quad * QUAD, QUAD)
                if quad % 2 == 0:
                    d.wait_ge(half_in[(quad // 2) % 2], r * 64 + 64 * (1 + quad // QUADS))
                d.wait_ge(total_free, r * CH + (quad + 1) * QUAD)
                own.link(d.tensor_copy(dq[:, par, :], dst_f[:, chunks]))
                for j in range(QUAD):
                    n = quad * QUAD + j
                    slot = n % SLOTS
                    d.wait_ge(rows_in[slot], r * 64 + 32 * (1 + n // SLOTS))
                    d.wait_ge(silu_done, r * CH + (n + 1 + SILU0))
                    own.link(d.tensor_tensor(prod[:, j % 2, :], q[:, slot, :], kv[:, slot, 0:D], ALU.mult))
                    d.tensor_tensor_reduce(out=prod[:, j % 2, :], in0=prod[:, j % 2, :], in1=dkv[:, slot, 0:D],
                                           scale=1.0, scalar=0.0, op0=ALU.mult, op1=ALU.add,
                                           accum_out=score[:, par, j:j + 1]).then_inc(score_parts, 1)
                    d.wait_ge(sum_done, r * CH + (n + 1))
                    own.link(d.tensor_scalar(same[:, slot, :], row[:, (n // HALF) % 2, (n % HALF) * P:(n % HALF + 1) * P],
                                             dq[:, par, j:j + 1], None, ALU.is_equal))
                    own.link(d.tensor_tensor_reduce(out=earlier[:, j % 2, :], in0=same[:, slot, :], in1=before[:, :],
                                                    scale=1.0, scalar=0.0, op0=ALU.mult, op1=ALU.add,
                                                    accum_out=cnt[:, par, j:j + 1]))
                own.link(d.tensor_scalar(cnt[:, par, :], cnt[:, par, :], 0.0, None, ALU.is_gt))
                own.link(d.tensor_tensor(away[:, par, :], cnt[:, par, :], spare[:, chunks], ALU.mult))
                d.tensor_tensor(target[:, par, :], away[:, par, :], dq[:, par, :], ALU.add).then_inc(score_ready, 1)

            FRONT = 1 + 3 * QUAD + 2
            opening = Own(d, d_own, 5)
            front(0, 0, opening)
            with d.Fori(0, ROUNDS) as r:
                own = Own(d, d_own, 5 + FRONT, QUADS * (FRONT + 1), r)
                for quad in range(QUADS):
                    par = quad % 2
                    d.wait_ge(gate_ready, r * QUADS + (quad + 1))
                    own.link(d.tensor_tensor(gate[:, par, :], gate[:, par, :],
                                             cut[:, bass.ds(r * CH + quad * QUAD, QUAD)], ALU.mult))
                    for j in range(QUAD):
                        slot = (quad * QUAD + j) % SLOTS
                        d.scalar_tensor_tensor(out=msg[:, slot, :], in0=kv[:, slot, D:2 * D], scalar=gate[:, par, j:j + 1],
                                               in1=dkv[:, slot, D:2 * D], op0=ALU.mult, op1=ALU.mult).then_inc(msg_done, 1)
                    front(r, quad + 1, own)
                own.closed()


def build_routing(nc, sem, sb, banks, v):
    x_all, xn_all, ident, acc, logits = v["x_all"], v["xn_all"], v["ident"], v["acc"], v["logits"]
    ctx = ExitStack()
    with ctx:
        def s(name): return sem("r_" + name, ctx)

        idle = s("idle")

        def b(name, shape, dt=fp32): return sb("r_" + name, shape, dt, ctx)

        wo, gw = b("wo", [P, KB, D]), b("gw", [P, KB, EXPERTS])
        bo, gbias = b("bo", [P, D]), b("gbias", [P, EXPERTS])
        part, agg, at_ = b("part", [P, PAIR, NACC, D]), b("agg", [P, PAIR, D]), b("at", [P, PAIR, D])
        hn, ht = b("hn", [P, PAIR, D]), b("ht", [P, PAIR, D])
        stats, mv, rs = b("stats", [P, 2, 6]), b("mv", [P, 2, 2]), b("rs", [P, 2])
        (w_in, part_in, d_own, a_own, agg_ready, a_turned, a_copied, o_done, var, std, h_ready, h_turned, h_copied,
         l_done, round_done) = (s(n) for n in ("w_in part_in d_own a_own agg_ready a_turned a_copied o_done var std "
                                               "h_ready h_turned h_copied l_done round_done").split())
        block = ctx.enter_context(nc.Block())

        @block.sync
        def _(sp):
            sp.dma_start(wo[:, :, :], v["wo"].rearrange("(k p) c -> p k c", p=P)).then_inc(w_in, 16)
            sp.dma_start(gw[:, :, :], v["gate_w"].rearrange("(k p) c -> p k c", p=P)).then_inc(w_in, 16)
            sp.dma_start(bo[:, :], v["bo"]).then_inc(w_in, 16)
            sp.dma_start(gbias[:, :], v["gate_b"]).then_inc(w_in, 16)
            with sp.Fori(0, PAIRS) as r:
                sp.wait_ge(round_done, r + 1)
                for h in range(PAIR):
                    for k in range(NACC):
                        sp.dma_start(part[:, h, k, :], rows_of(acc[k][0:ROWS, :], r * 2 + h)).then_inc(part_in, 16)

        @block.vector
        def _(d):
            d.sem_inc(round_done, 1)
            d.wait_ge(w_in, 64)
            with d.Fori(0, PAIRS) as r:
                own = Own(d, d_own, 0, 12, r)
                d.wait_ge(part_in, r * (32 * NACC) + 32 * NACC)
                for h in range(PAIR):
                    d.tensor_tensor(agg[:, h, :], part[:, h, 0, :], part[:, h, 1, :], ALU.add).then_inc(agg_ready, 1)
                for h in range(PAIR):
                    res = tile_of(x_all, r * 2 + h)
                    d.wait_ge(o_done, r * 2 + (h + 1))
                    own.link(d.tensor_tensor(hn[:, h, :], banks[4 * h + 1][:, 0:D], bo[:, :], ALU.add))
                    own.link(d.tensor_tensor(res, res, hn[:, h, :], ALU.add))
                    own.rest(idle)
                    own.link(d.bn_stats(stats[:, h, :], res))
                    own.rest(idle)
                    own.link(d.bn_aggr(mv[:, h, :], stats[:, h, :]))
                    d.tensor_scalar(rs[:, h:h + 1], mv[:, h, 1:2], LN_EPS, None, ALU.add).then_inc(var, 1)
                for h in range(PAIR):
                    d.wait_ge(std, r * 2 + (h + 1))
                    own.link(d.reciprocal(rs[:, h:h + 1], rs[:, h:h + 1]))
                    d.tensor_scalar(hn[:, h, :], tile_of(x_all, r * 2 + h), mv[:, h, 0:1], rs[:, h:h + 1],
                                    ALU.subtract, ALU.mult).then_inc(h_ready, 1)
                for h in range(PAIR):
                    d.wait_ge(l_done, r * 2 + (h + 1))
                    own.link(d.tensor_tensor(tile_of(logits, r * 2 + h), banks[4 * h + 2][:, 0:EXPERTS], gbias[:, :], ALU.add))
                own.closed()
                d.wait_ge(a_own, r * 2 + 2)
                d.sem_inc(round_done, 1)

        @block.scalar
        def _(a):
            with a.Fori(0, PAIRS) as r:
                for h in range(PAIR):
                    a.wait_ge(a_turned, r * 2 + (h + 1))
                    a.activation(at_[:, h, :], banks[4 * h][:, 0:D], ACT.Copy).then_inc(a_copied, 1)
                for h in range(PAIR):
                    a.wait_ge(var, r * 2 + (h + 1))
                    a.activation(rs[:, h:h + 1], rs[:, h:h + 1], ACT.Sqrt).then_inc(std, 1)
                for h in range(PAIR):
                    a.wait_ge(h_turned, r * 2 + (h + 1))
                    a.activation(ht[:, h, :], banks[4 * h][:, 0:D], ACT.Copy).then_inc(h_copied, 1)
                    a.activation(tile_of(xn_all, r * 2 + h), hn[:, h, :], ACT.Copy).then_inc(a_own, 1)

        @block.tensor
        def _(t):
            t.wait_ge(w_in, 64)
            with t.Fori(0, PAIRS) as r:
                def turn(rows, signal, ready):
                    for h in range(PAIR):
                        t.wait_ge(ready, r * 2 + (h + 1))
                        for k in range(KB):
                            last = nc.tensor.transpose(banks[4 * h][:, k * P:(k + 1) * P],
                                                       rows[:, h, k * P:(k + 1) * P], ident[:, :])
                        last.then_inc(signal, 1)

                def product(bank, cols, rows, w, ready, signal):
                    for h in range(PAIR):
                        t.wait_ge(ready, r * 2 + (h + 1))
                        for k in range(KB):
                            last = nc.tensor.matmul(banks[4 * h + bank][:, 0:cols], rows[:, h, k * P:(k + 1) * P],
                                                    w[:, k, :], start=(k == 0), stop=(k == KB - 1))
                        last.then_inc(signal, 1)

                turn(agg, a_turned, agg_ready)
                product(1, D, at_, wo, a_copied, o_done)
                turn(hn, h_turned, h_ready)
                product(2, EXPERTS, ht, gw, h_copied, l_done)


def build_experts(nc, sem, sb, banks, v):
    x_all, xn_all, ident, logits = v["x_all"], v["xn_all"], v["ident"], v["logits"]
    upto, ones, slots, answers = v["upto"], v["ones"], v["slots"], v["answers"]
    LIVE = REAL_TILES
    ctx = ExitStack()
    with ctx:
        def s(name): return sem("x_" + name, ctx)

        idle = s("idle")

        def b(name, shape, dt=fp32): return sb("x_" + name, shape, dt, ctx)

        TE = [P, TILES, EXPERTS]
        number, best, shown, hot = b("number", TE), b("best", [P, TILES]), b("shown", TE), b("hot", TE)
        probs, sums, pick, place = b("probs", TE), b("sums", [P, TILES]), b("pick", [P, TILES]), b("place", TE)
        carry, pos, kept, gate = b("carry", TE), b("pos", [P, TILES]), b("kept", [P, TILES]), b("gate", [P, TILES])
        base = b("base", [P, TILES])
        put, get = b("put", [P, TILES], i32), b("get", [P, TILES], i32)
        w1, w2 = b("w1", [P, 2, KB, FF]), b("w2", [P, 2, FC, D])
        b1s, b2 = b("b1s", [P, 2, FC]), b("b2", [P, 2, D])
        rows, cols = b("rows", [P, 2, CT, D]), b("cols", [P, KB, CPAD])
        mid, ans = b("mid", [P, FC, CPAD]), b("ans", [P, CT, D])
        y, work = b("y", [P, LIVE, D]), b("work", [P, D])
        over = b("over", [P, D], u32)
        zero_row, top_row, low_row = b("zero_row", [P, D]), b("top_row", [P, D]), b("low_row", [P, D])

        (d_own, numbered, shifted, exped, hot_ready, place_done, put_ready, moved, turned, c_copied, m_done,
         m_ready, y_done, ans_ready, fixed) = (
            s(n) for n in ("d_own numbered shifted exped hot_ready place_done put_ready moved turned c_copied "
                           "m_done m_ready y_done ans_ready fixed").split())
        load_in, ans_out, fetched, out_done = [s("load_in0"), s("load_in1")], s("ans_out"), s("fetched"), s("out_done")
        block = ctx.enter_context(nc.Block())

        @block.sync
        def _(sp):
            def weights(e, h):
                one = bass.ds(e, 1)
                sp.dma_start(w1[:, h, :, :], v["e_w1"][one, :, :].rearrange("a (k p) f -> p (a k) f", p=P)).then_inc(load_in[h], 16)
                sp.dma_start(w2[:, h, :, :], v["e_w2"][one, :, :].rearrange("a (k p) c -> p (a k) c", p=P)).then_inc(load_in[h], 16)
                sp.dma_start(b1s[:, h, :], v["e_b1"][one, :, :].rearrange("a p f -> (a p) f")).then_inc(load_in[h], 16)
                sp.dma_start(b2[:, h, :], v["e_b2"][one, :].to_broadcast([P, D])).then_inc(load_in[h], 16)

            def tokens(e, h):
                sp.dma_start(rows[:, h, :, :], slots.rearrange("(e t p) c -> e p t c", p=P, t=CT)[bass.ds(e, 1), :, :, :]
                             .rearrange("a p t c -> (a p) t c")).then_inc(load_in[h], 16)

            weights(0, 0)
            weights(1, 1)
            sp.wait_ge(moved, 16 * LIVE)
            tokens(0, 0)
            tokens(1, 1)
            with sp.Fori(0, EXPERTS // 2) as r:
                for h in range(2):
                    sp.wait_ge(ans_ready, r * (2 * CT) + (CT * (h + 1) + 2))
                    sp.dma_start(answers.rearrange("(e t p) c -> e p t c", p=P, t=CT)[bass.ds(r * 2 + h, 1), :, :, :]
                                 .rearrange("a p t c -> (a p) t c"), ans[:, :, :]).then_inc(ans_out, 16)
                    nxt = r * 2 + (2 + h)
                    weights(nxt, h)
                    tokens(nxt, h)
            for h in range(2):
                sp.wait_ge(load_in[h], 80 * (EXPERTS // 2 + 1))
            with sp.Fori(0, LIVE) as t:
                sp.wait_ge(fixed, t + 1)
                sp.dma_start(rows_of(v["out"], t), tile_of(x_all, t)).then_inc(out_done, 16)
            sp.wait_ge(out_done, 16 * LIVE)

        @block.gpsimd
        def _(g):
            g.iota(number[:, :, :], [[0, TILES], [1, EXPERTS]], base=0, channel_multiplier=0,
                   allow_small_or_imprecise_dtypes=True).then_inc(numbered, 1)
            g.wait_ge(put_ready, 2)
            for t in range(LIVE):
                g.indirect_dma_start(slots, bass.IndirectOffsetOnAxis(ap=put[:, t:t + 1], axis=0), xn_all[:, t, :], None,
                                     bounds_check=EXPERTS * CPAD - 1, oob_is_err=False).then_inc(moved, 16)
            g.wait_ge(ans_out, 16 * EXPERTS + 16)
            for t in range(LIVE):
                g.indirect_dma_start(y[:, t, :], None, answers,
                                     bass.IndirectOffsetOnAxis(ap=get[:, t:t + 1], axis=0)).then_inc(fetched, 16)
            g.wait_ge(fetched, 16 * LIVE)

        @block.vector
        def _(d):
            own = Own(d, d_own)
            wide = TE

            def over_experts(a): return a.unsqueeze(2).to_broadcast(wide)

            own.link(d.memset(zero_row[:, :], 0.0))
            own.link(d.memset(top_row[:, :], 10000.0))
            own.link(d.memset(low_row[:, :], -10000.0))
            own.link(d.tensor_reduce(best[:, :], logits[:, :, :], AX.X, ALU.max))
            d.tensor_tensor(shown[:, :, :], logits[:, :, :], over_experts(best[:, :]), ALU.subtract).then_inc(shifted, 1)
            d.wait_ge(exped, 1)
            own.link(d.tensor_reduce(sums[:, :], probs[:, :, :], AX.X, ALU.add))
            own.link(d.reciprocal(sums[:, :], sums[:, :]))
            own.link(d.tensor_tensor(probs[:, :, :], probs[:, :, :], over_experts(sums[:, :]), ALU.mult))
            own.link(d.tensor_reduce(best[:, :], probs[:, :, :], AX.X, ALU.max))
            own.link(d.tensor_tensor(shown[:, :, :], probs[:, :, :], over_experts(best[:, :]), ALU.is_lt))
            d.wait_ge(numbered, 1)
            own.link(d.scalar_tensor_tensor(out=shown[:, :, :], in0=shown[:, :, :], scalar=float(EXPERTS),
                                            in1=number[:, :, :], op0=ALU.mult, op1=ALU.add))
            own.link(d.tensor_reduce(pick[:, :], shown[:, :, :], AX.X, ALU.min))
            own.link(d.tensor_tensor(hot[:, :, :], number[:, :, :], over_experts(pick[:, :]), ALU.is_equal))
            own.link(d.memset(carry[:, 0, :], 0.0))
            for t in range(1, TILES):
                own.link(d.tensor_tensor(carry[:, t, :], carry[:, t - 1, :], hot[:, t - 1, :], ALU.add))
            d.sem_inc(hot_ready, 1)
            d.wait_ge(place_done, 1)
            own.link(d.tensor_tensor(place[:, :, :], hot[:, :, :],
                                     banks[0][:, 0:TILES * EXPERTS].rearrange("p (t e) -> p t e", e=EXPERTS), ALU.mult))
            own.link(d.tensor_reduce(pos[:, :], place[:, :, :], AX.X, ALU.add))
            own.link(d.tensor_scalar(pos[:, :], pos[:, :], -1.0, None, ALU.add))
            own.link(d.tensor_scalar(kept[:, :], pos[:, :], float(CAP), None, ALU.is_lt))
            own.link(d.tensor_tensor(gate[:, :], best[:, :], kept[:, :], ALU.mult))
            own.link(d.tensor_scalar(base[:, :], pick[:, :], float(CPAD), None, ALU.mult))
            own.link(d.tensor_scalar(kept[:, :], kept[:, :], float(-FAR), float(FAR), ALU.mult, ALU.add))
            own.link(d.tensor_tensor(kept[:, :], kept[:, :], pos[:, :], ALU.add))
            d.tensor_tensor(put[:, :], kept[:, :], base[:, :], ALU.add).then_inc(put_ready, 1)
            own.link(d.tensor_scalar(pos[:, :], pos[:, :], float(CAP - 1), None, ALU.min))
            d.tensor_tensor(get[:, :], pos[:, :], base[:, :], ALU.add).then_inc(put_ready, 1)
            d.sem_inc(ans_out, 16)
            d.sem_inc(ans_ready, 2)
            with d.Fori(0, EXPERTS // 2) as r:
                for h in range(2):
                    d.wait_ge(ans_out, r * 32 + 16 * (h + 1))
                    for c in range(CT):
                        d.wait_ge(y_done, r * (2 * CT) + (CT * h + c + 1))
                        d.tensor_tensor(ans[:, c, :], banks[4 + c % 2][:, 0:D], b2[:, h, :], ALU.add).then_inc(ans_ready, 1)
            d.wait_ge(fetched, 16 * LIVE)
            fix0 = own.n
            with d.Fori(0, LIVE) as t:
                mine = Own(d, d_own, fix0, 8, t)
                one = work[:, :]
                mine.link(d.tensor_scalar(one, tile_of(y, t), gate[:, bass.ds(t, 1)], None, ALU.mult))
                mine.link(d.tensor_tensor(over[:, :], one, one, ALU.not_equal))
                mine.rest(idle)
                mine.link(d.copy_predicated(one, over[:, :], zero_row[:, :]))
                for row, limit, op in ((top_row, BIG, ALU.is_gt), (low_row, -BIG, ALU.is_lt)):
                    mine.link(d.tensor_scalar(over[:, :], one, limit, None, op))
                    mine.rest(idle)
                    mine.link(d.copy_predicated(one, over[:, :], row[:, :]))
                mine.link(d.tensor_tensor(tile_of(x_all, t), tile_of(x_all, t), one, ALU.add))
                d.sem_inc(fixed, 1)
                mine.closed()

        @block.scalar
        def _(a):
            a.wait_ge(shifted, 1)
            a.activation(probs[:, :, :].rearrange("p t e -> p (t e)"), shown[:, :, :].rearrange("p t e -> p (t e)"),
                         ACT.Exp).then_inc(exped, 1)
            with a.Fori(0, EXPERTS // 2) as r:
                for h in range(2):
                    for k in range(KB):
                        a.wait_ge(turned, r * (2 * KB) + (KB * h + k + 1))
                        a.activation(cols[:, k, :], banks[k][:, :], ACT.Copy).then_inc(c_copied, 1)
                    for f in range(FC):
                        a.wait_ge(m_done, r * (2 * FC) + (FC * h + f + 1))
                        a.activation(mid[:, f, :], banks[2 + f % 2][:, :], ACT.Relu, bias=b1s[:, h, f:f + 1])\
                         .then_inc(m_ready, 1)

        @block.tensor
        def _(t_):
            t_.wait_ge(hot_ready, 1)
            n = TILES * EXPERTS
            nc.tensor.matmul(banks[0][:, 0:n], upto[:, :], hot[:, :, :].rearrange("p t e -> p (t e)"), start=True, stop=False)
            nc.tensor.matmul(banks[0][:, 0:n], ones[:, :], carry[:, :, :].rearrange("p t e -> p (t e)"), start=False, stop=True)\
              .then_inc(place_done, 1)
            t_.wait_ge(put_ready, 1)
            with t_.Fori(0, EXPERTS // 2) as r:
                for h in range(2):
                    t_.wait_ge(load_in[h], r * 80 + 80)
                    for k in range(KB):
                        for c in range(CT):
                            last = nc.tensor.transpose(banks[k][:, c * P:(c + 1) * P], rows[:, h, c, k * P:(k + 1) * P], ident[:, :])
                        last.then_inc(turned, 1)
                    t_.wait_ge(c_copied, r * (2 * KB) + KB * (h + 1))
                    for f in range(FC):
                        if f >= 2:
                            t_.wait_ge(m_ready, r * (2 * FC) + (FC * h + f - 1))
                        for k in range(KB):
                            last = nc.tensor.matmul(banks[2 + f % 2][:, :], w1[:, h, k, f * P:(f + 1) * P], cols[:, k, :],
                                                    start=(k == 0), stop=(k == KB - 1))
                        last.then_inc(m_done, 1)
                    t_.wait_ge(m_ready, r * (2 * FC) + FC * (h + 1))
                    for c in range(CT):
                        t_.wait_ge(ans_ready, r * (2 * CT) + (CT * h + c + 1))
                        for f in range(FC):
                            last = nc.tensor.matmul(banks[4 + c % 2][:, 0:D], mid[:, f, c * P:(c + 1) * P], w2[:, h, f, :],
                                                    start=(f == 0), stop=(f == FC - 1))
                        last.then_inc(y_done, 1)


def build(nc, *arrays):
    v = dict(zip(ARRAYS, arrays))
    top = ExitStack()
    with top:
        def sem(name, ctx=top): return ctx.enter_context(nc.semaphore(name))

        def sb(name, shape, dt=fp32, ctx=top): return ctx.enter_context(nc.sbuf_tensor(name, shape, dt))

        def dram(name, rows, cols):
            return nc.dram_tensor(name, [rows, cols], fp32, kind="Internal").ap()

        v["kv_table"], v["q_table"] = dram("kv_table", ROWS, 2 * D), dram("q_table", ROWS, D)
        v["acc"] = [dram(f"acc{k}", ROWS + P, D) for k in range(NACC)]
        v["slots"], v["answers"] = dram("slots", (EXPERTS + 2) * CPAD, D), dram("answers", EXPERTS * CPAD, D)
        banks = [top.enter_context(nc.psum_tensor(f"bank{k}", [P, 512], fp32)) for k in range(8)]
        v["x_all"] = sb("x_all", [P, TILES, D])
        v["xn_all"] = sb("xn_all", [P, TILES, D])
        v["ident"], v["ones"] = sb("ident", [P, P]), sb("ones", [P, P])
        v["before"], v["upto"] = sb("before", [P, P]), sb("upto", [P, P])
        v["kv_sum"] = sb("kv_sum", [P, KB, P + 1])
        v["logits"] = sb("logits", [P, TILES, EXPERTS])
        v["consts_made"] = sem("consts_made")
        build_nodes(nc, sem, sb, banks, v)
        build_mixer(nc, sem, sb, banks, v)
        build_edges(nc, sem, sb, banks, v)
        build_routing(nc, sem, sb, banks, v)
        build_experts(nc, sem, sb, banks, v)


ARRAYS = ("x", "row_mask", "head_mask", "src", "dst", "dst_row", "weight", "attr", "ln_gb", "w_gnn", "b_gnn", "wo", "bo",
          "w_edge", "w_mix", "wm", "w1m", "w2m", "gb_mix", "gate_w", "gate_b", "e_w1", "e_b1", "e_w2", "e_b2", "out")


def kernel(**inputs):
    import numpy as np
    import concourse.bacc as bacc
    from concourse.bass_utils import run_bass_kernel_spmd

    a = {k: np.asarray(x) for k, x in inputs.items()}
    g = {k[7:]: x for k, x in a.items() if k.startswith("L0_gnn_")}
    m = {k[7:]: x for k, x in a.items() if k.startswith("L0_mix_")}
    f = {k[7:]: x for k, x in a.items() if k.startswith("L0_ffn_")}
    slots_all = (ROUNDS + 1) * CH * P
    more = slots_all - EDGES

    def to_chunks(e, fill):
        return np.pad(e, (0, more), constant_values=fill).reshape(ROUNDS + 1, CH, P)

    def spread(row):
        return np.broadcast_to(row, (P,) + row.shape)

    attr = np.concatenate([np.pad(a["edge_attr_64"], ((0, more), (0, 0))).T, np.ones((1, slots_all), np.float32)])
    arrays = {
        "x": np.pad(a["x"], ((0, ROWS - NODES), (0, 0))),
        "row_mask": (np.arange(ROWS) < NODES).astype(np.float32).reshape(TILES, P).T,
        "head_mask": (np.arange(P)[:, None] // HD == np.arange(HB)).astype(np.float32),
        "src": to_chunks(a["src"], 0).transpose(0, 2, 1),
        "dst": to_chunks(a["dst"], NODES).transpose(0, 2, 1),
        "dst_row": to_chunks(a["dst"], NODES).reshape(ROUNDS + 1, CH * P),
        "weight": to_chunks(a["edge_weight"], 0).transpose(0, 2, 1),
        "attr": attr.reshape(KE, ROUNDS + 1, CH * P),
        "ln_gb": spread(np.stack([g["ln_g"], g["ln_b"]])),
        "w_gnn": np.concatenate([g["Wq"].T, g["Wk"].T, g["Wv"].T], 1),
        "b_gnn": spread(np.concatenate([g["bq"], g["bk"], g["bv"]])),
        "wo": g["Wo"].T, "bo": spread(g["bo"]),
        "w_edge": np.concatenate([np.concatenate([g["Wdk"].T, g["Wdv"].T], 1), np.concatenate([g["bdk"], g["bdv"]])[None]]),
        "w_mix": np.concatenate([m["Wq"], m["Wk"], m["Wv"]], 1),
        "wm": m["Wm"], "w1m": m["W1"], "w2m": m["W2"],
        "gb_mix": spread(np.stack([m["g1"], m["b1"], m["g2"], m["b2"]])),
        "gate_w": f["gate_w"], "gate_b": spread(f["gate_b"]),
        "e_w1": np.concatenate([f["w1"], f["w1"][:2]]), "e_b1": np.concatenate([f["b1"], f["b1"][:2]]).reshape(EXPERTS + 2, FC, P).transpose(0, 2, 1),
        "e_w2": np.concatenate([f["w2"], f["w2"][:2]]), "e_b2": np.concatenate([f["b2"], f["b2"][:2]]),
    }
    arrays = {f"in_{k}": np.ascontiguousarray(arrays[k]) for k in ARRAYS[:-1]}
    nc = bacc.Bacc("TRN2", target_bir_lowering=False, num_devices=1)
    args = [nc.dram_tensor(k, x.shape, mybir.dt.from_np(x.dtype), kind="ExternalInput").ap() for k, x in arrays.items()]
    args.append(nc.dram_tensor("out_rows", [REAL_TILES * P, D], fp32, kind="ExternalOutput").ap())
    build(nc, *args)
    r = run_bass_kernel_spmd(nc, [arrays], core_ids=[0])
    return r.results[0]["out_rows"][:NODES]
```

```python
import math

import concourse.bass as bass
from concourse import mybir
from contextlib import ExitStack

P = 128
NODES, EDGES, D, R = 3125, 53125, 256, 64
TILES = 26
ROWS = TILES * P
REAL_TILES = -(-NODES // P)
PAIR = 2
PAIRS = TILES // PAIR
QUAD, QUADS = 4, 4
CH = QUAD * QUADS
ROUNDS = 26
GROUPS = (ROUNDS + 1) * QUADS
HALF = CH // 2
SLOTS = 8
NACC = 2
HEADS, HD = 8, D // 8
EXPERTS, FF = 8, 1024
FC = FF // P
CAP = max(1, math.ceil(1.25 * NODES / EXPERTS))
CT = 4
CPAD = CT * P
LN_EPS, ATT_EPS, CUTOFF = 1e-5, 1e-6, 5.0
KB = D // P
HB = HEADS // KB
ZW = P + HB
FAR = 1 << 20
BIG = 3.4028234e38

fp32, bf16, i32, u32 = mybir.dt.float32, mybir.dt.bfloat16, mybir.dt.int32, mybir.dt.uint32
ALU = mybir.AluOpType
ACT = mybir.ActivationFunctionType
AX = mybir.AxisListType


class Own:

    def __init__(self, eng, sem, before=0, per=0, r=0):
        self.eng, self.sem, self.per, self.r = eng, sem, per, r
        self.start = self.n = before

    def link(self, ins):
        ins.then_inc(self.sem, 1)
        self.n += 1
        self.eng.wait_ge(self.sem, self.r * self.per + self.n)

    def rest(self, idle):
        self.eng.sem_inc(idle, 1)

    def closed(self):
        assert self.n - self.start == self.per, (self.n - self.start, self.per)


def tile_of(all_, t):
    return all_[:, bass.ds(t, 1), :].rearrange("p a c -> p (a c)")


def rows_of(table, t):
    return table.rearrange("(t p) c -> t p c", p=P)[bass.ds(t, 1), :, :].rearrange("a p c -> (a p) c")


def build_nodes(nc, sem, sb, banks, v):
    x_all, xn_all, ident, before, upto, ones = v["x_all"], v["xn_all"], v["ident"], v["before"], v["upto"], v["ones"]
    kv_sum, consts_made = v["kv_sum"], v["consts_made"]
    q_table, kv_table, acc, slots = v["q_table"], v["kv_table"], v["acc"], v["slots"]
    ctx = ExitStack()
    with ctx:
        def s(name): return sem("n_" + name, ctx)

        idle = s("idle")

        def b(name, shape, dt=fp32): return sb("n_" + name, shape, dt, ctx)

        ln_gb, bias = b("ln_gb", [P, 2, D]), b("bias", [P, 3 * D])
        w_gnn, w_kv = b("w_gnn", [P, KB, 3 * D]), b("w_kv", [P, KB, 2 * D])
        mask, zeros = b("mask", [P, TILES]), b("zeros", [P, 2048])
        stats, mv, rs = b("stats", [P, 2, 6]), b("mv", [P, 2, 2]), b("rs", [P, 2])
        stats2, mv2, rs2 = b("stats2", [P, 2, 6]), b("mv2", [P, 2, 2]), b("rs2", [P, 2])
        xn, xg = b("xn", [P, PAIR, D]), b("xg", [P, PAIR, D])
        xt, gt = b("xt", [P, PAIR, D]), b("gt", [P, PAIR, D])
        q, kv = b("q", [P, PAIR, D]), b("kv", [P, PAIR, 2 * D])
        neg, kpos, vext = b("neg", [P, PAIR, D]), b("kpos", [P, PAIR, D]), b("vext", [P, PAIR, KB, P + 1])

        x_in, w_in, zeros_made, zero_out = s("x_in"), s("w_in"), s("zeros_made"), s("zero_out")
        p_own, d_own, a_own = s("p_own"), s("d_own"), s("a_own")
        var, std, var2, std2, normed, turned, copied = (s(n) for n in "var std var2 std2 normed turned copied".split())
        q_done, kv_done, mix_done, q_ready, kv_ready, neg_ready, exp_ready = (
            s(n) for n in "q_done kv_done mix_done q_ready kv_ready neg_ready exp_ready".split())
        k_ready, v_ready, sums_done, round_done = (s(n) for n in "k_ready v_ready sums_done round_done".split())
        rows_out, parts_ready = s("rows_out"), s("parts_ready")
        parts, rest = b("parts", [P, PAIR, 3, D], bf16), b("rest", [P, D])
        block = ctx.enter_context(nc.Block())

        @block.sync
        def _(sp):
            xr = v["x"].rearrange("(t p) c -> p t c", p=P)
            sp.dma_start(x_all[:, :, :], xr).then_inc(x_in, 16)
            sp.dma_start(ln_gb[:, :, :], v["ln_gb"]).then_inc(w_in, 16)
            sp.dma_start(bias[:, :], v["b_gnn"]).then_inc(w_in, 16)
            sp.dma_start(w_gnn[:, :, :], v["w_gnn"].rearrange("(k p) c -> p k c", p=P)).then_inc(w_in, 16)
            sp.dma_start(w_kv[:, :, :], v["w_mix"][:, D:3 * D].rearrange("(k p) c -> p k c", p=P)).then_inc(w_in, 16)
            sp.dma_start(mask[:, :], v["row_mask"]).then_inc(w_in, 16)
            sp.wait_ge(zeros_made, 1)
            sent, span = 0, 2048 // D
            for table, tiles in [(a, TILES + 1) for a in acc] + [(slots, (EXPERTS + 2) * CT)]:
                for t in range(0, tiles, span):
                    m = min(span, tiles - t)
                    sp.dma_start(table[t * P:(t + m) * P, :].rearrange("(t p) c -> p t c", p=P),
                                 zeros[:, 0:m * D].rearrange("p (t c) -> p t c", c=D)).then_inc(zero_out, 16)
                    sent += 1
            with sp.Fori(0, PAIRS) as r:
                for h in range(PAIR):
                    sp.wait_ge(q_ready, r * 2 + (h + 1))
                    sp.dma_start(rows_of(q_table, r * 2 + h), q[:, h, :]).then_inc(rows_out, 16)
                    sp.wait_ge(kv_ready, r * 2 + (h + 1))
                    sp.dma_start(rows_of(kv_table, r * 2 + h), kv[:, h, :]).then_inc(rows_out, 16)
                for h in range(PAIR):
                    sp.wait_ge(parts_ready, r * 2 + (h + 1))
                    sp.dma_start(rows_of(v["parts_table"], r * 2 + h), parts[:, h, :, :].rearrange("p a c -> p (a c)"))\
                      .then_inc(rows_out, 16)
                sp.wait_ge(rows_out, r * 96 + 96)
                sp.sem_inc(round_done, 1)
            sp.wait_ge(zero_out, 16 * sent)

        @block.gpsimd
        def _(g):
            own = Own(g, p_own)
            own.link(g.memset(ident[:, :], 0.0))
            own.link(g.memset(ones[:, :], 1.0))
            g.affine_select(out=ident[:, :], in_=ident[:, :], compare_op=ALU.not_equal, fill=1.0, base=0,
                            pattern=[[-1, P]], channel_multiplier=1).then_inc(consts_made, 1)
            g.affine_select(out=before[:, :], in_=ones[:, :], compare_op=ALU.is_gt, fill=0.0, base=0,
                            pattern=[[-1, P]], channel_multiplier=1).then_inc(consts_made, 1)
            g.affine_select(out=upto[:, :], in_=ones[:, :], compare_op=ALU.is_ge, fill=0.0, base=0,
                            pattern=[[1, P]], channel_multiplier=-1).then_inc(consts_made, 1)
            g.wait_ge(consts_made, 3)
            with g.Fori(0, PAIRS) as r:
                for h in range(PAIR):
                    own = Own(g, p_own, 2 + 4 * h, 4 * PAIR, r)
                    g.wait_ge(q_ready, r * 2 + (h + 1))
                    own.rest(idle)
                    own.link(g.tensor_copy(parts[:, h, 0, :], q[:, h, :]))
                    own.link(g.tensor_tensor(rest[:, :], q[:, h, :], parts[:, h, 0, :], ALU.subtract))
                    own.rest(idle)
                    own.link(g.tensor_copy(parts[:, h, 1, :], rest[:, :]))
                    own.link(g.tensor_tensor(parts[:, h, 2, :], rest[:, :], parts[:, h, 1, :], ALU.subtract))
                    g.sem_inc(parts_ready, 1)

        @block.vector
        def _(d):
            d.memset(zeros[:, :], 0.0).then_inc(zeros_made, 1)
            first = Own(d, d_own)
            first.link(d.memset(kv_sum[:, :, :], 0.0))
            d.sem_inc(round_done, 2)
            d.wait_ge(x_in, 16)
            d.wait_ge(w_in, 80)
            with d.Fori(0, PAIRS) as r:
                d.wait_ge(round_done, r * 2 + 2)
                own = Own(d, d_own, 1, 20, r)
                for h in range(PAIR):
                    own.rest(idle)
                    own.link(d.bn_stats(stats[:, h, :], tile_of(x_all, r * 2 + h)))
                    own.rest(idle)
                    own.link(d.bn_aggr(mv[:, h, :], stats[:, h, :]))
                    d.tensor_scalar(rs[:, h:h + 1], mv[:, h, 1:2], LN_EPS, None, ALU.add).then_inc(var, 1)
                for h in range(PAIR):
                    d.wait_ge(std, r * 2 + (h + 1))
                    own.link(d.reciprocal(rs[:, h:h + 1], rs[:, h:h + 1]))
                    own.link(d.tensor_scalar(xn[:, h, :], tile_of(x_all, r * 2 + h), mv[:, h, 0:1], rs[:, h:h + 1],
                                             ALU.subtract, ALU.mult))
                    own.link(d.bn_stats(stats2[:, h, :], xn[:, h, :]))
                    own.rest(idle)
                    own.link(d.bn_aggr(mv2[:, h, :], stats2[:, h, :]))
                    d.tensor_scalar(rs2[:, h:h + 1], mv2[:, h, 1:2], LN_EPS, None, ALU.add).then_inc(var2, 1)
                for h in range(PAIR):
                    d.wait_ge(std2, r * 2 + (h + 1))
                    own.link(d.reciprocal(rs2[:, h:h + 1], rs2[:, h:h + 1]))
                    own.link(d.tensor_scalar(xg[:, h, :], xn[:, h, :], mv2[:, h, 0:1], rs2[:, h:h + 1],
                                             ALU.subtract, ALU.mult))
                    own.link(d.tensor_tensor(xg[:, h, :], xg[:, h, :], ln_gb[:, 0, :], ALU.mult))
                    d.tensor_tensor(xg[:, h, :], xg[:, h, :], ln_gb[:, 1, :], ALU.add).then_inc(normed, 1)
                for h in range(PAIR):
                    d.wait_ge(q_done, r * 2 + (h + 1))
                    d.tensor_tensor(q[:, h, :], banks[4 * h + 1][:, 0:D], bias[:, 0:D], ALU.add).then_inc(q_ready, 1)
                    d.wait_ge(kv_done, r * 2 + (h + 1))
                    d.tensor_tensor(kv[:, h, :], banks[4 * h + 2][:, :], bias[:, D:3 * D], ALU.add).then_inc(kv_ready, 1)
                    d.wait_ge(mix_done, r * 2 + (h + 1))
                    d.tensor_scalar(neg[:, h, :], banks[4 * h + 3][:, 0:D], 0.0, None, ALU.min).then_inc(neg_ready, 1)
                for h in range(PAIR):
                    d.wait_ge(exp_ready, r * 2 + (h + 1))
                    d.scalar_tensor_tensor(out=kpos[:, h, :], in0=banks[4 * h + 3][:, 0:D], scalar=0.0, in1=neg[:, h, :],
                                           op0=ALU.max, op1=ALU.add).then_inc(k_ready, 1)
                for h in range(PAIR):
                    d.wait_ge(sums_done, r * 2 + (h + 1))
                    own.link(d.tensor_tensor(kv_sum[:, :, :], kv_sum[:, :, :],
                                             banks[4 * h][:, 0:KB * (P + 1)].rearrange("p (k c) -> p k c", k=KB), ALU.add))
                own.closed()
                d.sem_inc(round_done, 1)

        @block.scalar
        def _(a):
            a.wait_ge(w_in, 80)
            with a.Fori(0, PAIRS) as r:
                for h in range(PAIR):
                    a.wait_ge(var, r * 2 + (h + 1))
                    a.activation(rs[:, h:h + 1], rs[:, h:h + 1], ACT.Sqrt).then_inc(std, 1)
                for h in range(PAIR):
                    a.wait_ge(var2, r * 2 + (h + 1))
                    a.activation(rs2[:, h:h + 1], rs2[:, h:h + 1], ACT.Sqrt).then_inc(std2, 1)
                    a.activation(tile_of(xn_all, r * 2 + h), xn[:, h, :], ACT.Copy).then_inc(a_own, 1)
                for h in range(PAIR):
                    a.wait_ge(turned, r * 2 + (h + 1))
                    a.activation(xt[:, h, :], banks[4 * h][:, 0:D], ACT.Copy).then_inc(copied, 1)
                    a.activation(gt[:, h, :], banks[4 * h][:, D:2 * D], ACT.Copy).then_inc(copied, 1)
                for h in range(PAIR):
                    a.wait_ge(neg_ready, r * 2 + (h + 1))
                    a.activation(neg[:, h, :], neg[:, h, :], ACT.Exp).then_inc(exp_ready, 1)
                for h in range(PAIR):
                    a.wait_ge(k_ready, r * 2 + (h + 1))
                    for k in range(KB):
                        a.activation(vext[:, h, k, 0:P], banks[4 * h + 3][:, D + k * P:D + (k + 1) * P], ACT.Copy,
                                     scale=1.0 / NODES).then_inc(v_ready, 1)
                        a.activation(vext[:, h, k, P:P + 1], mask[:, bass.ds(r * 2 + h, 1)], ACT.Copy).then_inc(v_ready, 1)

        @block.tensor
        def _(t):
            t.wait_ge(consts_made, 3)
            t.wait_ge(w_in, 80)
            with t.Fori(0, PAIRS) as r:
                for h in range(PAIR):
                    t.wait_ge(normed, r * 2 + (h + 1))
                    for k in range(2 * KB):
                        half = (xn if k < KB else xg)[:, h, (k % KB) * P:(k % KB + 1) * P]
                        last = nc.tensor.transpose(banks[4 * h][:, k * P:(k + 1) * P], half, ident[:, :])
                    last.then_inc(turned, 1)
                for h in range(PAIR):
                    t.wait_ge(copied, r * 4 + (2 * h + 2))
                    for out_, lhs, w, signal in (
                            (banks[4 * h + 1][:, 0:D], gt, w_gnn[:, :, 0:D], q_done),
                            (banks[4 * h + 2][:, :], gt, w_gnn[:, :, D:3 * D], kv_done),
                            (banks[4 * h + 3][:, :], xt, w_kv, mix_done)):
                        for k in range(KB):
                            last = nc.tensor.matmul(out_, lhs[:, h, k * P:(k + 1) * P], w[:, k, :],
                                                    start=(k == 0), stop=(k == KB - 1))
                        last.then_inc(signal, 1)
                for h in range(PAIR):
                    t.wait_ge(k_ready, r * 2 + (h + 1))
                    t.wait_ge(v_ready, r * 8 + (4 * h + 4))
                    for k in range(KB):
                        last = nc.tensor.matmul(banks[4 * h][:, k * (P + 1):(k + 1) * (P + 1)],
                                                kpos[:, h, k * P:(k + 1) * P], vext[:, h, k, :], start=True, stop=True)
                    last.then_inc(sums_done, 1)


def build_mixer(nc, sem, sb, banks, v):
    x_all, xn_all, ident, kv_sum = v["x_all"], v["xn_all"], v["ident"], v["kv_sum"]
    ctx = ExitStack()
    with ctx:
        def s(name): return sem("m_" + name, ctx)

        idle = s("idle")

        def b(name, shape, dt=fp32): return sb("m_" + name, shape, dt, ctx)

        wq, wm = b("wq", [P, KB, D]), b("wm", [P, KB, D])
        w1, w2 = b("w1", [P, 2 * KB, 2 * D]), b("w2", [P, 2 * KB, D])
        gb = b("gb", [P, 4, D])
        heads = b("heads", [P, HB])
        sums = b("sums", [P, KB, ZW])
        xt = b("xt", [P, PAIR, D])
        stage = b("stage", [P, PAIR, D])
        neg, qt = b("neg", [P, PAIR, D]), b("qt", [P, PAIR, D])
        z, msg, mt = b("z", [P, PAIR, HEADS]), b("msg", [P, PAIR, D]), b("mt", [P, PAIR, D])
        nt, h1 = b("nt", [P, PAIR, D]), b("h1", [P, PAIR, 2 * D])
        stats, mv, rs = b("stats", [P, 2, 6]), b("mv", [P, 2, 2]), b("rs", [P, 2])
        names = ("w_in p_own d_own staged x_turned x_copied q_done neg_ready exp_ready q_ready num_done msg_ready "
                 "m_turned m_copied m_done var std n_ready n_turned n_copied h_done h_ready o_done round_done")
        (w_in, p_own, d_own, staged, x_turned, x_copied, q_done, neg_ready, exp_ready, q_ready, num_done, msg_ready,
         m_turned, m_copied, m_done, var, std, n_ready, n_turned, n_copied, h_done, h_ready, o_done, round_done) = (
            s(n) for n in names.split())
        block = ctx.enter_context(nc.Block())

        @block.sync
        def _(sp):
            for dst, src in ((wq[:, :, :], v["w_mix"][:, 0:D]), (wm[:, :, :], v["wm"]),
                             (w1[:, :, :], v["w1m"]), (w2[:, :, :], v["w2m"])):
                sp.dma_start(dst, src.rearrange("(k p) c -> p k c", p=P)).then_inc(w_in, 16)
            sp.dma_start(gb[:, :, :], v["gb_mix"]).then_inc(w_in, 16)
            sp.dma_start(heads[:, :], v["head_mask"]).then_inc(w_in, 16)
            sp.wait_ge(w_in, 96)

        @block.gpsimd
        def _(g):
            with g.Fori(0, PAIRS) as r:
                g.wait_ge(round_done, r + 1)
                for h in range(PAIR):
                    g.tensor_copy(stage[:, h, :], tile_of(xn_all, r * 2 + h)).then_inc(staged, 1)

        @block.vector
        def _(d):
            d.wait_ge(w_in, 96)
            first = Own(d, d_own)
            for k in range(KB):
                for c in range(HB):
                    first.link(d.tensor_scalar(sums[:, k, c * HD:(c + 1) * HD], kv_sum[:, k, c * HD:(c + 1) * HD],
                                               heads[:, c:c + 1], None, ALU.mult))
                first.link(d.tensor_scalar(sums[:, k, P:ZW], heads[:, :], kv_sum[:, k, P:P + 1], None, ALU.mult))
            d.sem_inc(round_done, 1)
            with d.Fori(0, PAIRS) as r:
                own = Own(d, d_own, KB * (HB + 1), 32, r)

                def norm(bank, g_, res):
                    for h in range(PAIR):
                        own.link(d.bn_stats(stats[:, h, :], banks[4 * h + bank][:, 0:D]))
                        own.rest(idle)
                        own.link(d.bn_aggr(mv[:, h, :], stats[:, h, :]))
                        d.tensor_scalar(rs[:, h:h + 1], mv[:, h, 1:2], LN_EPS, None, ALU.add).then_inc(var, 1)
                    for h in range(PAIR):
                        d.wait_ge(std, r * 4 + (res * 2 + h + 1))
                        own.link(d.reciprocal(rs[:, h:h + 1], rs[:, h:h + 1]))
                        own.link(d.tensor_scalar(msg[:, h, :], banks[4 * h + bank][:, 0:D], mv[:, h, 0:1], rs[:, h:h + 1],
                                                 ALU.subtract, ALU.mult))
                        own.link(d.tensor_tensor(msg[:, h, :], msg[:, h, :], gb[:, g_, :], ALU.mult))
                        last = d.tensor_tensor(msg[:, h, :], msg[:, h, :], gb[:, g_ + 1, :], ALU.add)
                        if res:
                            own.link(last)
                        else:
                            last.then_inc(n_ready, 1)

                for h in range(PAIR):
                    d.wait_ge(q_done, r * 2 + (h + 1))
                    d.tensor_scalar(neg[:, h, :], banks[4 * h + 1][:, 0:D], 0.0, None, ALU.min).then_inc(neg_ready, 1)
                for h in range(PAIR):
                    d.wait_ge(exp_ready, r * 2 + (h + 1))
                    d.scalar_tensor_tensor(out=qt[:, h, :], in0=banks[4 * h + 1][:, 0:D], scalar=0.0, in1=neg[:, h, :],
                                           op0=ALU.max, op1=ALU.add).then_inc(q_ready, 1)
                for h in range(PAIR):
                    d.wait_ge(num_done, r * 2 + (h + 1))
                    num = banks[4 * h + 2][:, 0:KB * ZW].rearrange("p (k c) -> p k c", k=KB)
                    own.link(d.tensor_scalar(z[:, h, :].rearrange("p (k c) -> p k c", k=KB), num[:, :, P:ZW],
                                             ATT_EPS, None, ALU.add))
                    own.link(d.reciprocal(z[:, h, :], z[:, h, :]))
                    own.link(d.tensor_scalar(z[:, h, :], z[:, h, :], float(NODES), None, ALU.mult))
                    for k in range(KB):
                        last = d.tensor_tensor(
                            msg[:, h, k * P:(k + 1) * P].rearrange("p (c e) -> p c e", e=HD),
                            num[:, k, 0:P].rearrange("p (c e) -> p c e", e=HD),
                            z[:, h, k * HB:(k + 1) * HB].unsqueeze(2).to_broadcast([P, HB, HD]), ALU.mult)
                        last.then_inc(msg_ready, 1)
                for h in range(PAIR):
                    d.wait_ge(m_done, r * 2 + (h + 1))
                norm(3, 0, 0)
                for h in range(PAIR):
                    d.wait_ge(o_done, r * 2 + (h + 1))
                norm(1, 2, 1)
                for h in range(PAIR):
                    res = tile_of(x_all, r * 2 + h)
                    own.link(d.scalar_tensor_tensor(out=stage[:, h, :], in0=stage[:, h, :], scalar=2.0, in1=res,
                                                    op0=ALU.mult, op1=ALU.add))
                    own.link(d.tensor_tensor(res, stage[:, h, :], msg[:, h, :], ALU.add))
                own.closed()
                d.sem_inc(round_done, 1)

        @block.scalar
        def _(a):
            with a.Fori(0, PAIRS) as r:
                for h in range(PAIR):
                    a.wait_ge(x_turned, r * 2 + (h + 1))
                    a.activation(xt[:, h, :], banks[4 * h][:, 0:D], ACT.Copy).then_inc(x_copied, 1)
                for h in range(PAIR):
                    a.wait_ge(neg_ready, r * 2 + (h + 1))
                    a.activation(neg[:, h, :], neg[:, h, :], ACT.Exp).then_inc(exp_ready, 1)
                for h in range(PAIR):
                    a.wait_ge(m_turned, r * 2 + (h + 1))
                    a.activation(mt[:, h, :], banks[4 * h][:, 0:D], ACT.Copy).then_inc(m_copied, 1)
                for h in range(PAIR):
                    a.wait_ge(var, r * 4 + (h + 1))
                    a.activation(rs[:, h:h + 1], rs[:, h:h + 1], ACT.Sqrt).then_inc(std, 1)
                for h in range(PAIR):
                    a.wait_ge(n_turned, r * 2 + (h + 1))
                    a.activation(nt[:, h, :], banks[4 * h][:, 0:D], ACT.Copy).then_inc(n_copied, 1)
                for h in range(PAIR):
                    a.wait_ge(h_done, r * 2 + (h + 1))
                    a.activation(h1[:, h, :], banks[4 * h + 2][:, :], ACT.Relu).then_inc(h_ready, 1)
                for h in range(PAIR):
                    a.wait_ge(var, r * 4 + (h + 3))
                    a.activation(rs[:, h:h + 1], rs[:, h:h + 1], ACT.Sqrt).then_inc(std, 1)

        @block.tensor
        def _(t):
            t.wait_ge(w_in, 96)
            with t.Fori(0, PAIRS) as r:
                def turn(rows, signal, ready, per):
                    for h in range(PAIR):
                        t.wait_ge(ready, r * 2 * per + per * (h + 1))
                        for k in range(KB):
                            last = nc.tensor.transpose(banks[4 * h][:, k * P:(k + 1) * P],
                                                       rows[:, h, k * P:(k + 1) * P], ident[:, :])
                        last.then_inc(signal, 1)

                turn(stage, x_turned, staged, 1)
                for h in range(PAIR):
                    t.wait_ge(x_copied, r * 2 + (h + 1))
                    for m in range(KB):
                        for k in range(KB):
                            last = nc.tensor.matmul(banks[4 * h + 1][:, m * P:(m + 1) * P], wq[:, k, m * P:(m + 1) * P],
                                                    xt[:, h, k * P:(k + 1) * P], start=(k == 0), stop=(k == KB - 1))
                    last.then_inc(q_done, 1)
                for h in range(PAIR):
                    t.wait_ge(q_ready, r * 2 + (h + 1))
                    for k in range(KB):
                        last = nc.tensor.matmul(banks[4 * h + 2][:, k * ZW:(k + 1) * ZW], qt[:, h, k * P:(k + 1) * P],
                                                sums[:, k, :], start=True, stop=True)
                    last.then_inc(num_done, 1)
                turn(msg, m_turned, msg_ready, KB)
                for h in range(PAIR):
                    t.wait_ge(m_copied, r * 2 + (h + 1))
                    for k in range(KB):
                        last = nc.tensor.matmul(banks[4 * h + 3][:, 0:D], mt[:, h, k * P:(k + 1) * P], wm[:, k, :],
                                                start=(k == 0), stop=(k == KB - 1))
                    last.then_inc(m_done, 1)
                turn(msg, n_turned, n_ready, 1)
                for h in range(PAIR):
                    t.wait_ge(n_copied, r * 2 + (h + 1))
                    for m in range(2 * KB):
                        for k in range(2 * KB):
                            rows = (xt if k < KB else nt)[:, h, (k % KB) * P:(k % KB + 1) * P]
                            last = nc.tensor.matmul(banks[4 * h + 2][:, m * P:(m + 1) * P], w1[:, k, m * P:(m + 1) * P],
                                                    rows, start=(k == 0), stop=(k == 2 * KB - 1))
                    last.then_inc(h_done, 1)
                for h in range(PAIR):
                    t.wait_ge(h_ready, r * 2 + (h + 1))
                    for k in range(2 * KB):
                        last = nc.tensor.matmul(banks[4 * h + 1][:, 0:D], h1[:, h, k * P:(k + 1) * P], w2[:, k, :],
                                                start=(k == 0), stop=(k == 2 * KB - 1))
                    last.then_inc(o_done, 1)


def build_windows(nc, sem, sb, banks, v):
    base_i, base_all, near_flag, far_flag, ones, ident, bias_rows = (
        v[k] for k in ("base_i", "base_all", "near_flag", "far_flag", "ones", "ident", "bias_rows"))
    ctx = ExitStack()
    with ctx:
        def s(name): return sem("w_" + name, ctx)

        def b(name, shape, dt=fp32): return sb("w_" + name, shape, dt, ctx)

        rows = b("rows", [P, QUAD * P], i32)
        bias, part, kept = b("bias", [P, 2 * D]), b("part", [P, 3, 2 * D], bf16), b("kept", [P, 3])
        low, span = b("low", [P, 1]), b("span", [P, 1])
        diag, widest = b("diag", [P, 2, GROUPS]), b("widest", [P, 1])
        rows_in, d_own, diag_ready, spread_done = (s(n) for n in "rows_in d_own diag_ready spread_done".split())
        block = ctx.enter_context(nc.Block())

        @block.sync
        def _(sp):
            sp.dma_start(rows[0:GROUPS, :], v["dst_row"].rearrange("i (q e) -> (i q) e", q=QUADS)).then_inc(rows_in, 16)
            sp.dma_start(bias[:, :], v["b_edge"]).then_inc(rows_in, 16)
            sp.dma_start(kept[:, :], v["part_mask"]).then_inc(rows_in, 16)

        @block.vector
        def _(d):
            own = Own(d, d_own)
            own.link(d.memset(low[:, :], 0.0))
            own.link(d.memset(span[:, :], 0.0))
            d.wait_ge(rows_in, 48)
            own.link(d.tensor_reduce(low[0:GROUPS, :], rows[0:GROUPS, :], AX.X, ALU.min))
            own.link(d.tensor_reduce(span[0:GROUPS, :], rows[0:GROUPS, :], AX.X, ALU.max))
            own.link(d.tensor_tensor(span[:, :], span[:, :], low[:, :], ALU.subtract))
            own.link(d.tensor_scalar(diag[:, 0, :], ident[:, 0:GROUPS], low[:, 0:1], None, ALU.mult))
            d.tensor_scalar(diag[:, 1, :], ident[:, 0:GROUPS], span[:, 0:1], None, ALU.mult).then_inc(diag_ready, 1)
            for k in range(3):
                own.link(d.tensor_copy(part[:, k, :], bias[:, :]))
                own.link(d.tensor_tensor(bias[:, :], bias[:, :], part[:, k, :], ALU.subtract))
            own.link(d.tensor_scalar(bias_rows[:, :], part[:, 0, :], kept[:, 0:1], None, ALU.mult))
            for k in (1, 2):
                own.link(d.scalar_tensor_tensor(out=bias_rows[:, :], in0=part[:, k, :], scalar=kept[:, k:k + 1],
                                                in1=bias_rows[:, :], op0=ALU.mult, op1=ALU.add))
            d.wait_ge(spread_done, 1)
            own.link(d.tensor_copy(base_all[:, :], banks[0][:, 0:GROUPS]))
            own.link(d.tensor_copy(base_i[:, :], banks[0][:, 0:GROUPS]))
            own.link(d.tensor_reduce(widest[:, :], banks[0][:, GROUPS:2 * GROUPS], AX.X, ALU.max))
            own.link(d.tensor_scalar(near_flag[:, :], widest[:, :], float(P), None, ALU.is_lt))
            own.link(d.tensor_scalar(far_flag[:, :], widest[:, :], float(P), None, ALU.is_ge))

        @block.tensor
        def _(t):
            t.wait_ge(diag_ready, 1)
            nc.tensor.matmul(banks[0][:, 0:2 * GROUPS], ones[:, :], diag[:, :, :].rearrange("p a g -> p (a g)"),
                             start=True, stop=True).then_inc(spread_done, 1)


def build_near_edges(nc, sem, sb, banks, v):
    kv_table, parts_table, acc, base_i, base_all = (v[k] for k in ("kv_table", "parts_table", "acc", "base_i", "base_all"))
    ALLC = (ROUNDS + 1) * CH
    PARTS = 3
    ctx = ExitStack()
    with ctx:
        def s(name): return sem("f_" + name, ctx)

        def b(name, shape, dt=fp32): return sb("f_" + name, shape, dt, ctx)

        w = b("w", [P, 2 * D])
        bias, one = v["bias_rows"], b("one", [P, P], bf16)
        idx = b("idx", [P, 2, HALF], i32)
        attr = b("attr", [P, 2, HALF // 2 * P])
        row = b("row", [P, 2, HALF * P], i32)
        window = b("window", [P, 2, PARTS, D], bf16)
        weight = b("weight", [P, ALLC])
        cut, near, rel = b("cut", [P, ALLC]), b("near", [P, ALLC]), b("rel", [P, ALLC])
        dst_i = b("dst_i", [P, ALLC], i32)
        lane, half_pi, lane_at = b("lane", [P, 1]), b("half_pi", [P, 1]), b("lane_at", [P, GROUPS])
        count = b("count", [P, P])
        kv, dkv, msg = b("kv", [P, SLOTS, 2 * D]), b("dkv", [P, SLOTS, 2 * D]), b("msg", [P, SLOTS, D])
        pick = b("pick", [P, 2, QUAD * P], bf16)
        give = b("give", [P, SLOTS, P])
        prod, total = b("prod", [P, QUAD, D]), b("total", [P, 2, D])
        score, gate = b("score", [P, 2, QUAD]), b("gate", [P, 2, QUAD])

        once, half_in, window_in = s("once"), [s("half_in0"), s("half_in1")], [s("window_in0"), s("window_in1")]
        rows_in = [s(f"rows_in{k}") for k in range(SLOTS)]
        added = [s(f"added{k}") for k in range(NACC)]
        (proj_done, silu_done, msg_done, q_done, prod_done, sum_done, total_ready, pick_ready, score_ready,
         gate_ready, d_own, clamped, sine, tick, made, zero_made) = (
            s(n) for n in ("proj_done silu_done msg_done q_done prod_done sum_done total_ready pick_ready score_ready "
                           "gate_ready d_own clamped sine tick made zero_made").split())
        block = ctx.enter_context(nc.Block())

        SILU0, MSG0, Q0, PROD0, SUM0, TOT0 = 2, SLOTS, 2 * QUAD, QUAD, 2, 2

        @block.sync
        def _(sp):
            def load(i, half):
                at, one_ = half * HALF, bass.ds(i, 1)
                sp.dma_start(idx[:, half, :], v["src"][one_, :, at:at + HALF].rearrange("a p c -> (a p) c"))\
                  .then_inc(half_in[half], 16)
                sp.dma_start(attr[:, half, :], v["attr"][:, one_, half * (HALF // 2) * P:(half + 1) * (HALF // 2) * P]
                             .rearrange("k a c -> k (a c)")).then_inc(half_in[half], 16)
                sp.dma_start(row[:, half, :], v["dst_row"][one_, at * P:(at + HALF) * P].to_broadcast([P, HALF * P]))\
                  .then_inc(half_in[half], 16)

            def load_window(group, par):
                first = sp.value_load(base_i[0:1, bass.ds(group, 1)], min_val=0, max_val=ROWS - P)
                sp.dma_start(window[:, par, :, :], parts_table[bass.ds(first, P), :].rearrange("p (a c) -> p a c", a=PARTS))\
                  .then_inc(window_in[par], 16)

            with sp.If(sp.value_load(v["near_flag"][0:1, 0:1], min_val=0, max_val=1)):
                for half in range(2):
                    load(0, half)
                sp.dma_start(w[:, :], v["w_edge"]).then_inc(once, 16)
                for dst_, src_ in ((dst_i, v["dst"]), (weight, v["weight"])):
                    sp.dma_start(dst_[:, :].rearrange("p (i c) -> p i c", c=CH), src_.rearrange("i p c -> p i c")).then_inc(once, 16)
                load_window(0, 0)
                load_window(1, 1)
                with sp.Fori(0, ROUNDS) as r:
                    for quad in range(QUADS):
                        sp.wait_ge(q_done, r * CH + ((quad + 1) * QUAD + Q0))
                        load_window(r * QUADS + (quad + 2), quad % 2)
                        if quad % 2:
                            sp.wait_ge(msg_done, r * CH + ((quad + 1) * QUAD + MSG0))
                            load(r + 1, quad // 2)
                for half in range(2):
                    sp.wait_ge(half_in[half], 48 * (ROUNDS + 1))
                    sp.wait_ge(window_in[half], 32 * ROUNDS + 16)

        @block.gpsimd
        def _(g):
            def gather(quad, j):
                slot = (quad % 2) * QUAD + j
                g.indirect_dma_start(kv[:, slot, :], None, kv_table,
                                     bass.IndirectOffsetOnAxis(ap=idx[:, (quad // 2) % 2, slot:slot + 1], axis=0))\
                 .then_inc(rows_in[slot], 16)

            with g.If(g.value_load(v["near_flag"][0:1, 0:1], min_val=0, max_val=1)):
                g.iota(lane[:, :], [[1, 1]], base=0, channel_multiplier=1,
                       allow_small_or_imprecise_dtypes=True).then_inc(made, 1)
                g.iota(count[:, :], [[1, P]], base=0, channel_multiplier=0,
                       allow_small_or_imprecise_dtypes=True).then_inc(made, 1)
                g.wait_ge(zero_made, 1)
                for k in range(NACC):
                    g.dma_start(acc[k][0:P, :], total[:, k, :], accum_op=ALU.add).then_inc(added[k], 16)
                g.wait_ge(half_in[0], 48)
                for quad in range(2):
                    for j in range(QUAD):
                        gather(quad, j)
                with g.Fori(0, ROUNDS) as r:
                    for quad in range(QUADS):
                        if quad % 2 == 0:
                            g.wait_ge(half_in[1 - quad // 2], r * 48 + 48 * (1 + quad // 2))
                            g.sem_inc(tick, 1)
                        for j in range(QUAD):
                            g.wait_ge(msg_done, r * CH + (quad * QUAD + j + 1 + MSG0))
                            g.sem_inc(tick, 1)
                            gather(quad + 2, j)
                        g.wait_ge(total_ready, r * QUADS + (quad + 1 + TOT0))
                        first = g.value_load(base_i[0:1, bass.ds(r * QUADS + quad, 1)], min_val=0, max_val=ROWS - P)
                        g.sem_inc(tick, 1)
                        g.dma_start(acc[quad % 2][bass.ds(first, P), :], total[:, quad % 2, :], accum_op=ALU.add)\
                         .then_inc(added[quad % 2], 16)
                for k in range(NACC):
                    g.wait_ge(added[k], 16 + 16 * ROUNDS * QUADS // NACC)
                for k in range(SLOTS):
                    g.wait_ge(rows_in[k], 16 * (2 * ROUNDS + 1))

        @block.tensor
        def _(t):
            def project(r, quad):
                if quad % 2 == 0:
                    t.wait_ge(half_in[(quad // 2) % 2], r * 48 + 48 * (1 + quad // QUADS))
                for j in range(QUAD):
                    n = quad * QUAD + j
                    at, up = (n % HALF) // 2 * P, R * (n % 2)
                    t.wait_ge(silu_done, r * CH + (n + 1))
                    nc.tensor.matmul(banks[n % 2][:, :], attr[up:up + R, (n // HALF) % 2, at:at + P], w[up:up + R, :],
                                     start=True, stop=False)
                    nc.tensor.matmul(banks[n % 2][:, :], one[up:up + R, :], bias[up:up + R, :],
                                     start=False, stop=True).then_inc(proj_done, 1)

            def queries(r, quad):
                t.wait_ge(pick_ready, r * QUADS + (quad + 1))
                t.wait_ge(window_in[quad % 2], r * 32 + 16 * (1 + quad // 2))
                for j in range(QUAD):
                    n = quad * QUAD + j
                    t.wait_ge(prod_done, r * CH + (n + 1))
                    for part in range(PARTS):
                        last = nc.tensor.matmul(banks[2 + j][:, 0:D], pick[:, quad % 2, j * P:(j + 1) * P],
                                                window[:, quad % 2, part, :], start=(part == 0), stop=(part == PARTS - 1))
                    last.then_inc(q_done, 1)

            with t.If(t.value_load(v["near_flag"][0:1, 0:1], min_val=0, max_val=1)):
                t.wait_ge(once, 48)
                t.wait_ge(made, 3)
                project(0, 0)
                queries(0, 0)
                with t.Fori(0, ROUNDS) as r:
                    for quad in range(QUADS):
                        project(r, quad + 1)
                        queries(r, quad + 1)
                        t.wait_ge(total_ready, r * QUADS + (quad + 1))
                        for j in range(QUAD):
                            n = quad * QUAD + j
                            t.wait_ge(msg_done, r * CH + (n + 1 + MSG0))
                            last = nc.tensor.matmul(banks[6 + quad % 2][:, 0:D], give[:, n % SLOTS, :], msg[:, n % SLOTS, :],
                                                    start=(j == 0), stop=(j == QUAD - 1))
                        last.then_inc(sum_done, 1)

        @block.scalar
        def _(a):
            def silus(r, quad):
                for j in range(QUAD):
                    n = quad * QUAD + j
                    a.wait_ge(proj_done, r * CH + (n + 1))
                    a.wait_ge(msg_done, r * CH + (n + 1))
                    a.activation(dkv[:, n % SLOTS, :], banks[n % 2][:, :], ACT.Silu).then_inc(silu_done, 1)

            with a.If(a.value_load(v["near_flag"][0:1, 0:1], min_val=0, max_val=1)):
                a.sem_inc(silu_done, SILU0)
                a.sem_inc(total_ready, TOT0)
                a.wait_ge(clamped, 2)
                a.activation(cut[:, :], cut[:, :], ACT.Sin, bias=half_pi[:, 0:1], scale=-math.pi / CUTOFF).then_inc(sine, 1)
                silus(0, 0)
                with a.Fori(0, ROUNDS) as r:
                    for quad in range(QUADS):
                        a.wait_ge(score_ready, r * QUADS + (quad + 1))
                        a.activation(gate[:, quad % 2, :], score[:, quad % 2, :], ACT.Silu).then_inc(gate_ready, 1)
                        silus(r, quad + 1)
                        a.wait_ge(sum_done, r * QUADS + (quad + 1 + SUM0))
                        a.wait_ge(added[quad % 2], r * 32 + 16 * (quad // 2 + 1))
                        a.activation(total[:, quad % 2, :], banks[6 + quad % 2][:, 0:D], ACT.Copy).then_inc(total_ready, 1)

        @block.vector
        def _(d):
            def picks(r, quad):
                if quad % 2 == 0:
                    d.wait_ge(half_in[(quad // 2) % 2], r * 48 + 48 * (1 + quad // QUADS))
                d.wait_ge(q_done, r * CH + (quad + 1) * QUAD)
                at = (quad % 2) * QUAD * P
                d.tensor_scalar(pick[:, quad % 2, :], row[:, (quad // 2) % 2, at:at + QUAD * P],
                                lane_at[:, bass.ds(r * QUADS + quad, 1)], None, ALU.is_equal).then_inc(pick_ready, 1)

            def scores(r, quad):
                for j in range(QUAD + 1):
                    n = quad * QUAD + j
                    if j < QUAD:
                        slot = n % SLOTS
                        d.wait_ge(rows_in[slot], r * 32 + 16 * (1 + n // SLOTS))
                        d.wait_ge(q_done, r * CH + (n + 1 + Q0))
                        d.tensor_tensor(prod[:, j, :], banks[2 + j][:, 0:D], kv[:, slot, 0:D], ALU.mult).then_inc(prod_done, 1)
                    if j:
                        d.wait_ge(prod_done, r * CH + (n + PROD0))
                        d.wait_ge(silu_done, r * CH + (n + SILU0))
                        last = d.tensor_tensor_reduce(out=prod[:, j - 1, :], in0=prod[:, j - 1, :],
                                                      in1=dkv[:, (n - 1) % SLOTS, 0:D], scale=1.0, scalar=0.0,
                                                      op0=ALU.mult, op1=ALU.add, accum_out=score[:, quad % 2, j - 1:j])
                last.then_inc(score_ready, 1)

            with d.If(d.value_load(v["near_flag"][0:1, 0:1], min_val=0, max_val=1)):
                d.memset(total[:, :, :], 0.0).then_inc(zero_made, 1)
                d.memset(one[:, :], 1.0).then_inc(made, 1)
                d.sem_inc(msg_done, MSG0)
                d.sem_inc(q_done, Q0)
                d.sem_inc(prod_done, PROD0)
                d.sem_inc(sum_done, SUM0)
                first = Own(d, d_own)
                d.memset(half_pi[:, :], math.pi / 2).then_inc(clamped, 1)
                d.wait_ge(once, 48)
                d.wait_ge(made, 3)
                d.tensor_scalar(cut[:, :], weight[:, :], CUTOFF, None, ALU.min).then_inc(clamped, 1)
                first.link(d.tensor_tensor(rel[:, :].rearrange("p (g c) -> p g c", c=QUAD),
                                           dst_i[:, :].rearrange("p (g c) -> p g c", c=QUAD),
                                           base_all[:, :].unsqueeze(2).to_broadcast([P, GROUPS, QUAD]), ALU.subtract))
                first.link(d.tensor_scalar(lane_at[:, :], base_all[:, :], lane[:, 0:1], None, ALU.add))
                first.link(d.tensor_scalar(near[:, :], weight[:, :], CUTOFF, None, ALU.is_lt))
                d.wait_ge(sine, 1)
                first.link(d.tensor_scalar(cut[:, :], cut[:, :], 0.5, 0.5, ALU.mult, ALU.add))
                first.link(d.tensor_tensor(cut[:, :], cut[:, :], near[:, :], ALU.mult))
                picks(0, 0)
                scores(0, 0)
                with d.Fori(0, ROUNDS) as r:
                    own = Own(d, d_own, 5, QUADS, r)
                    for quad in range(QUADS):
                        par = quad % 2
                        picks(r, quad + 1)
                        d.wait_ge(gate_ready, r * QUADS + (quad + 1))
                        own.link(d.tensor_tensor(gate[:, par, :], gate[:, par, :],
                                                 cut[:, bass.ds(r * CH + quad * QUAD, QUAD)], ALU.mult))
                        d.wait_ge(sum_done, r * QUADS + (quad + 1))
                        for j in range(QUAD):
                            slot = (quad * QUAD + j) % SLOTS
                            d.tensor_scalar(give[:, slot, :], count[:, :], rel[:, bass.ds(r * CH + (quad * QUAD + j), 1)],
                                            gate[:, par, j:j + 1], ALU.is_equal, ALU.mult)
                            d.tensor_tensor(msg[:, slot, :], kv[:, slot, D:2 * D], dkv[:, slot, D:2 * D], ALU.mult)\
                             .then_inc(msg_done, 1)
                        scores(r, quad + 1)
                    own.closed()


def build_edges(nc, sem, sb, banks, v):
    q_table, kv_table, acc, before = v["q_table"], v["kv_table"], v["acc"], v["before"]
    ALLC = (ROUNDS + 1) * CH
    ctx = ExitStack()
    with ctx:
        def s(name): return sem("e_" + name, ctx)

        def b(name, shape, dt=fp32): return sb("e_" + name, shape, dt, ctx)

        w, bias, one = b("w", [P, 2 * D]), v["bias_rows"], b("one", [P, P], bf16)
        idx = b("idx", [P, 2, 2, HALF], i32)
        attr = b("attr", [P, 2, HALF // 2 * P])
        row = b("row", [P, 2, HALF * P], i32)
        dst_i, dst_f, weight = b("dst_i", [P, ALLC], i32), b("dst_f", [P, ALLC]), b("weight", [P, ALLC])
        spare, cut, near = b("spare", [P, ALLC]), b("cut", [P, ALLC]), b("near", [P, ALLC])
        lane, half_pi = b("lane", [P, 1]), b("half_pi", [P, 1])
        kv, q, dkv = b("kv", [P, SLOTS, 2 * D]), b("q", [P, SLOTS, D]), b("dkv", [P, SLOTS, 2 * D])
        msg, total = b("msg", [P, SLOTS, D]), b("total", [P, SLOTS, D])
        same = b("same", [P, SLOTS, P])
        prod, earlier = b("prod", [P, 2, D]), b("earlier", [P, 2, P])
        score, gate, cnt = b("score", [P, 2, QUAD]), b("gate", [P, 2, QUAD]), b("cnt", [P, 2, QUAD])
        away, target = b("away", [P, 2, QUAD]), b("target", [P, 2, QUAD], i32)
        dq = b("dq", [P, 2, QUAD])

        once, half_in = s("once"), [s("half_in0"), s("half_in1")]
        rows_in = [s(f"rows_in{k}") for k in range(SLOTS)]
        scattered = [s(f"scattered{k}") for k in range(NACC)]
        proj_done, silu_done, msg_done, sum_done, total_ready, total_free = (
            s(n) for n in "proj_done silu_done msg_done sum_done total_ready total_free".split())
        score_ready, gate_ready, d_own, clamped, sine, tick, lane_made, zero_made, one_made, score_parts = (
            s(n) for n in "score_ready gate_ready d_own clamped sine tick lane_made zero_made one_made score_parts".split())
        block = ctx.enter_context(nc.Block())

        MSG0, SILU0, TOT0, SUM0, FREE0 = SLOTS, 2, 2, SLOTS, SLOTS - NACC

        @block.sync
        def _(sp):
            with sp.If(sp.value_load(v["far_flag"][0:1, 0:1], min_val=0, max_val=1)):
                def load(i, half):
                    one_ = bass.ds(i, 1)
                    at = half * HALF
                    sp.dma_start(idx[:, half, 0, :], v["src"][one_, :, at:at + HALF].rearrange("a p c -> (a p) c"))\
                      .then_inc(half_in[half], 16)
                    sp.dma_start(attr[:, half, :], v["attr"][:, one_, half * (HALF // 2) * P:(half + 1) * (HALF // 2) * P]
                                 .rearrange("k a c -> k (a c)"))\
                      .then_inc(half_in[half], 16)
                    sp.dma_start(idx[:, half, 1, :], v["dst"][one_, :, at:at + HALF].rearrange("a p c -> (a p) c"))\
                      .then_inc(half_in[half], 16)
                    sp.dma_start(row[:, half, :],
                                 v["dst_row"][one_, at * P:(at + HALF) * P].to_broadcast([P, HALF * P]))\
                      .then_inc(half_in[half], 16)

                for half in range(2):
                    load(0, half)
                sp.dma_start(w[:, :], v["w_edge"]).then_inc(once, 16)
                sp.dma_start(dst_i[:, :].rearrange("p (i c) -> p i c", c=CH), v["dst"].rearrange("i p c -> p i c")).then_inc(once, 16)
                sp.dma_start(weight[:, :].rearrange("p (i c) -> p i c", c=CH), v["weight"].rearrange("i p c -> p i c")).then_inc(once, 16)
                with sp.Fori(0, ROUNDS) as r:
                    for half in range(2):
                        sp.wait_ge(msg_done, r * CH + ((half + 1) * HALF + MSG0))
                        load(r + 1, half)
                for half in range(2):
                    sp.wait_ge(half_in[half], 64 * (ROUNDS + 1))

        @block.gpsimd
        def _(g):
            with g.If(g.value_load(v["far_flag"][0:1, 0:1], min_val=0, max_val=1)):
                g.iota(lane[:, :], [[1, 1]], base=ROWS, channel_multiplier=1,
                       allow_small_or_imprecise_dtypes=True).then_inc(lane_made, 1)
                g.sem_inc(total_free, FREE0)

                def gather(quad, j):
                    slot = (quad % 2) * QUAD + j
                    half, at = (quad // 2) % 2, (quad % 2) * QUAD + j
                    g.indirect_dma_start(kv[:, slot, :], None, kv_table,
                                         bass.IndirectOffsetOnAxis(ap=idx[:, half, 0, at:at + 1], axis=0))\
                     .then_inc(rows_in[slot], 16)
                    g.indirect_dma_start(q[:, slot, :], None, q_table,
                                         bass.IndirectOffsetOnAxis(ap=idx[:, half, 1, at:at + 1], axis=0))\
                     .then_inc(rows_in[slot], 16)

                g.wait_ge(zero_made, 1)
                for k in range(NACC):
                    g.dma_start(acc[k][0:P, :], total[:, k, :], accum_op=ALU.add).then_inc(scattered[k], 16)
                g.wait_ge(half_in[0], 64)
                for quad in range(2):
                    for j in range(QUAD):
                        gather(quad, j)
                with g.Fori(0, ROUNDS) as r:
                    for quad in range(QUADS):
                        if quad == 0:
                            g.wait_ge(half_in[1], r * 64 + 64)
                            g.sem_inc(tick, 1)
                        if quad == 2:
                            g.wait_ge(half_in[0], r * 64 + 128)
                            g.sem_inc(tick, 1)
                        for j in range(QUAD):
                            n = quad * QUAD + j
                            g.wait_ge(msg_done, r * CH + (n + 1 + MSG0))
                            g.sem_inc(tick, 1)
                            gather(quad + 2, j)
                            g.wait_ge(total_ready, r * CH + (n + 1 + TOT0))
                            g.wait_ge(scattered[j % NACC], r * (16 * CH // NACC) + 16 * (n // NACC + 1))
                            g.sem_inc(total_free, 1)
                            slot = (quad % 2) * QUAD + j
                            g.indirect_dma_start(acc[j % NACC], bass.IndirectOffsetOnAxis(
                                ap=target[:, quad % 2, j:j + 1], axis=0), total[:, slot, :], None, compute_op=ALU.add)\
                             .then_inc(scattered[j % NACC], 16)
                for k in range(NACC):
                    g.wait_ge(scattered[k], 16 + 16 * ROUNDS * CH // NACC)
                for k in range(SLOTS):
                    g.wait_ge(rows_in[k], 32 * (2 * ROUNDS + 1))

        @block.tensor
        def _(t):
            with t.If(t.value_load(v["far_flag"][0:1, 0:1], min_val=0, max_val=1)):
                def project(r, n):
                    half = (n // HALF) % 2
                    if n % HALF == 0:
                        t.wait_ge(half_in[half], r * 64 + 64 * (1 + n // CH))
                    t.wait_ge(silu_done, r * CH + (n + 1))
                    at, up = (n % HALF) // 2 * P, R * (n % 2)
                    nc.tensor.matmul(banks[n % 2][:, :], attr[up:up + R, half, at:at + P], w[up:up + R, :],
                                     start=True, stop=False)
                    nc.tensor.matmul(banks[n % 2][:, :], one[up:up + R, :], bias[up:up + R, :],
                                     start=False, stop=True).then_inc(proj_done, 1)

                t.wait_ge(once, 48)
                t.wait_ge(one_made, 1)
                for n in range(QUAD):
                    project(0, n)
                with t.Fori(0, ROUNDS) as r:
                    for quad in range(QUADS):
                        for j in range(QUAD):
                            project(r, (quad + 1) * QUAD + j)
                        for j in range(QUAD):
                            n = quad * QUAD + j
                            t.wait_ge(msg_done, r * CH + (n + 1 + MSG0))
                            t.wait_ge(total_ready, r * CH + (n + 1))
                            nc.tensor.matmul(banks[2 + n % 2][:, 0:D], same[:, n % SLOTS, :], msg[:, n % SLOTS, :],
                                             start=True, stop=True).then_inc(sum_done, 1)

        @block.scalar
        def _(a):
            with a.If(a.value_load(v["far_flag"][0:1, 0:1], min_val=0, max_val=1)):
                def silus(r, quad):
                    for j in range(QUAD):
                        n = quad * QUAD + j
                        a.wait_ge(proj_done, r * CH + (n + 1))
                        a.wait_ge(msg_done, r * CH + (n + 1))
                        a.activation(dkv[:, n % SLOTS, :], banks[n % 2][:, :], ACT.Silu).then_inc(silu_done, 1)

                a.sem_inc(silu_done, SILU0)
                a.sem_inc(total_ready, TOT0)
                a.wait_ge(clamped, 2)
                a.activation(cut[:, :], cut[:, :], ACT.Sin, bias=half_pi[:, 0:1], scale=-math.pi / CUTOFF).then_inc(sine, 1)
                silus(0, 0)
                with a.Fori(0, ROUNDS) as r:
                    for quad in range(QUADS):
                        a.wait_ge(score_ready, r * QUADS + (quad + 1))
                        a.activation(gate[:, quad % 2, :], score[:, quad % 2, :], ACT.Silu).then_inc(gate_ready, 1)
                        silus(r, quad + 1)
                        for j in range(QUAD):
                            n = quad * QUAD + j
                            a.wait_ge(sum_done, r * CH + (n + 1 + SUM0))
                            a.wait_ge(total_free, r * CH + (n + 1))
                            a.activation(total[:, n % SLOTS, :], banks[2 + n % 2][:, 0:D], ACT.Copy).then_inc(total_ready, 1)

        @block.vector
        def _(d):
            with d.If(d.value_load(v["far_flag"][0:1, 0:1], min_val=0, max_val=1)):
                d.memset(total[:, 0:NACC, :], 0.0).then_inc(zero_made, 1)
                d.memset(one[:, :], 1.0).then_inc(one_made, 1)
                d.sem_inc(msg_done, MSG0)
                d.sem_inc(sum_done, SUM0)
                first = Own(d, d_own)
                d.memset(half_pi[:, :], math.pi / 2).then_inc(clamped, 1)
                d.wait_ge(once, 48)
                d.wait_ge(lane_made, 1)
                d.tensor_scalar(cut[:, :], weight[:, :], CUTOFF, None, ALU.min).then_inc(clamped, 1)
                first.link(d.tensor_copy(dst_f[:, :], dst_i[:, :]))
                first.link(d.tensor_scalar(spare[:, :], dst_f[:, :], -1.0, lane[:, 0:1], ALU.mult, ALU.add))
                first.link(d.tensor_scalar(near[:, :], weight[:, :], CUTOFF, None, ALU.is_lt))
                d.wait_ge(sine, 1)
                first.link(d.tensor_scalar(cut[:, :], cut[:, :], 0.5, 0.5, ALU.mult, ALU.add))
                first.link(d.tensor_tensor(cut[:, :], cut[:, :], near[:, :], ALU.mult))

                def front(r, quad, own):
                    par = quad % 2
                    chunks = bass.ds(r * CH + quad * QUAD, QUAD)
                    if quad % 2 == 0:
                        d.wait_ge(half_in[(quad // 2) % 2], r * 64 + 64 * (1 + quad // QUADS))
                    d.wait_ge(total_free, r * CH + (quad + 1) * QUAD)
                    own.link(d.tensor_copy(dq[:, par, :], dst_f[:, chunks]))
                    for j in range(QUAD):
                        n = quad * QUAD + j
                        slot = n % SLOTS
                        d.wait_ge(rows_in[slot], r * 64 + 32 * (1 + n // SLOTS))
                        d.wait_ge(silu_done, r * CH + (n + 1 + SILU0))
                        own.link(d.tensor_tensor(prod[:, j % 2, :], q[:, slot, :], kv[:, slot, 0:D], ALU.mult))
                        d.tensor_tensor_reduce(out=prod[:, j % 2, :], in0=prod[:, j % 2, :], in1=dkv[:, slot, 0:D],
                                               scale=1.0, scalar=0.0, op0=ALU.mult, op1=ALU.add,
                                               accum_out=score[:, par, j:j + 1]).then_inc(score_parts, 1)
                        d.wait_ge(sum_done, r * CH + (n + 1))
                        own.link(d.tensor_scalar(same[:, slot, :], row[:, (n // HALF) % 2, (n % HALF) * P:(n % HALF + 1) * P],
                                                 dq[:, par, j:j + 1], None, ALU.is_equal))
                        own.link(d.tensor_tensor_reduce(out=earlier[:, j % 2, :], in0=same[:, slot, :], in1=before[:, :],
                                                        scale=1.0, scalar=0.0, op0=ALU.mult, op1=ALU.add,
                                                        accum_out=cnt[:, par, j:j + 1]))
                    own.link(d.tensor_scalar(cnt[:, par, :], cnt[:, par, :], 0.0, None, ALU.is_gt))
                    own.link(d.tensor_tensor(away[:, par, :], cnt[:, par, :], spare[:, chunks], ALU.mult))
                    d.tensor_tensor(target[:, par, :], away[:, par, :], dq[:, par, :], ALU.add).then_inc(score_ready, 1)

                FRONT = 1 + 3 * QUAD + 2
                opening = Own(d, d_own, 5)
                front(0, 0, opening)
                with d.Fori(0, ROUNDS) as r:
                    own = Own(d, d_own, 5 + FRONT, QUADS * (FRONT + 1), r)
                    for quad in range(QUADS):
                        par = quad % 2
                        d.wait_ge(gate_ready, r * QUADS + (quad + 1))
                        own.link(d.tensor_tensor(gate[:, par, :], gate[:, par, :],
                                                 cut[:, bass.ds(r * CH + quad * QUAD, QUAD)], ALU.mult))
                        for j in range(QUAD):
                            slot = (quad * QUAD + j) % SLOTS
                            d.scalar_tensor_tensor(out=msg[:, slot, :], in0=kv[:, slot, D:2 * D], scalar=gate[:, par, j:j + 1],
                                                   in1=dkv[:, slot, D:2 * D], op0=ALU.mult, op1=ALU.mult).then_inc(msg_done, 1)
                        front(r, quad + 1, own)
                    own.closed()


def build_routing(nc, sem, sb, banks, v):
    x_all, xn_all, ident, acc, logits = v["x_all"], v["xn_all"], v["ident"], v["acc"], v["logits"]
    ctx = ExitStack()
    with ctx:
        def s(name): return sem("r_" + name, ctx)

        idle = s("idle")

        def b(name, shape, dt=fp32): return sb("r_" + name, shape, dt, ctx)

        wo, gw = b("wo", [P, KB, D]), b("gw", [P, KB, EXPERTS])
        bo, gbias = b("bo", [P, D]), b("gbias", [P, EXPERTS])
        part, agg, at_ = b("part", [P, PAIR, NACC, D]), b("agg", [P, PAIR, D]), b("at", [P, PAIR, D])
        hn, ht = b("hn", [P, PAIR, D]), b("ht", [P, PAIR, D])
        stats, mv, rs = b("stats", [P, 2, 6]), b("mv", [P, 2, 2]), b("rs", [P, 2])
        (w_in, part_in, d_own, a_own, agg_ready, a_turned, a_copied, o_done, var, std, h_ready, h_turned, h_copied,
         l_done, round_done) = (s(n) for n in ("w_in part_in d_own a_own agg_ready a_turned a_copied o_done var std "
                                               "h_ready h_turned h_copied l_done round_done").split())
        block = ctx.enter_context(nc.Block())

        @block.sync
        def _(sp):
            sp.dma_start(wo[:, :, :], v["wo"].rearrange("(k p) c -> p k c", p=P)).then_inc(w_in, 16)
            sp.dma_start(gw[:, :, :], v["gate_w"].rearrange("(k p) c -> p k c", p=P)).then_inc(w_in, 16)
            sp.dma_start(bo[:, :], v["bo"]).then_inc(w_in, 16)
            sp.dma_start(gbias[:, :], v["gate_b"]).then_inc(w_in, 16)
            with sp.Fori(0, PAIRS) as r:
                sp.wait_ge(round_done, r + 1)
                for h in range(PAIR):
                    for k in range(NACC):
                        sp.dma_start(part[:, h, k, :], rows_of(acc[k][0:ROWS, :], r * 2 + h)).then_inc(part_in, 16)

        @block.vector
        def _(d):
            d.sem_inc(round_done, 1)
            d.wait_ge(w_in, 64)
            with d.Fori(0, PAIRS) as r:
                own = Own(d, d_own, 0, 12, r)
                d.wait_ge(part_in, r * (32 * NACC) + 32 * NACC)
                for h in range(PAIR):
                    d.tensor_tensor(agg[:, h, :], part[:, h, 0, :], part[:, h, 1, :], ALU.add).then_inc(agg_ready, 1)
                for h in range(PAIR):
                    res = tile_of(x_all, r * 2 + h)
                    d.wait_ge(o_done, r * 2 + (h + 1))
                    own.link(d.tensor_tensor(hn[:, h, :], banks[4 * h + 1][:, 0:D], bo[:, :], ALU.add))
                    own.link(d.tensor_tensor(res, res, hn[:, h, :], ALU.add))
                    own.rest(idle)
                    own.link(d.bn_stats(stats[:, h, :], res))
                    own.rest(idle)
                    own.link(d.bn_aggr(mv[:, h, :], stats[:, h, :]))
                    d.tensor_scalar(rs[:, h:h + 1], mv[:, h, 1:2], LN_EPS, None, ALU.add).then_inc(var, 1)
                for h in range(PAIR):
                    d.wait_ge(std, r * 2 + (h + 1))
                    own.link(d.reciprocal(rs[:, h:h + 1], rs[:, h:h + 1]))
                    d.tensor_scalar(hn[:, h, :], tile_of(x_all, r * 2 + h), mv[:, h, 0:1], rs[:, h:h + 1],
                                    ALU.subtract, ALU.mult).then_inc(h_ready, 1)
                for h in range(PAIR):
                    d.wait_ge(l_done, r * 2 + (h + 1))
                    own.link(d.tensor_tensor(tile_of(logits, r * 2 + h), banks[4 * h + 2][:, 0:EXPERTS], gbias[:, :], ALU.add))
                own.closed()
                d.wait_ge(a_own, r * 2 + 2)
                d.sem_inc(round_done, 1)

        @block.scalar
        def _(a):
            with a.Fori(0, PAIRS) as r:
                for h in range(PAIR):
                    a.wait_ge(a_turned, r * 2 + (h + 1))
                    a.activation(at_[:, h, :], banks[4 * h][:, 0:D], ACT.Copy).then_inc(a_copied, 1)
                for h in range(PAIR):
                    a.wait_ge(var, r * 2 + (h + 1))
                    a.activation(rs[:, h:h + 1], rs[:, h:h + 1], ACT.Sqrt).then_inc(std, 1)
                for h in range(PAIR):
                    a.wait_ge(h_turned, r * 2 + (h + 1))
                    a.activation(ht[:, h, :], banks[4 * h][:, 0:D], ACT.Copy).then_inc(h_copied, 1)
                    a.activation(tile_of(xn_all, r * 2 + h), hn[:, h, :], ACT.Copy).then_inc(a_own, 1)

        @block.tensor
        def _(t):
            t.wait_ge(w_in, 64)
            with t.Fori(0, PAIRS) as r:
                def turn(rows, signal, ready):
                    for h in range(PAIR):
                        t.wait_ge(ready, r * 2 + (h + 1))
                        for k in range(KB):
                            last = nc.tensor.transpose(banks[4 * h][:, k * P:(k + 1) * P],
                                                       rows[:, h, k * P:(k + 1) * P], ident[:, :])
                        last.then_inc(signal, 1)

                def product(bank, cols, rows, w, ready, signal):
                    for h in range(PAIR):
                        t.wait_ge(ready, r * 2 + (h + 1))
                        for k in range(KB):
                            last = nc.tensor.matmul(banks[4 * h + bank][:, 0:cols], rows[:, h, k * P:(k + 1) * P],
                                                    w[:, k, :], start=(k == 0), stop=(k == KB - 1))
                        last.then_inc(signal, 1)

                turn(agg, a_turned, agg_ready)
                product(1, D, at_, wo, a_copied, o_done)
                turn(hn, h_turned, h_ready)
                product(2, EXPERTS, ht, gw, h_copied, l_done)


def build_experts(nc, sem, sb, banks, v):
    x_all, xn_all, ident, logits = v["x_all"], v["xn_all"], v["ident"], v["logits"]
    upto, ones, slots, answers = v["upto"], v["ones"], v["slots"], v["answers"]
    LIVE = REAL_TILES
    ctx = ExitStack()
    with ctx:
        def s(name): return sem("x_" + name, ctx)

        idle = s("idle")

        def b(name, shape, dt=fp32): return sb("x_" + name, shape, dt, ctx)

        TE = [P, TILES, EXPERTS]
        number, best, shown, hot = b("number", TE), b("best", [P, TILES]), b("shown", TE), b("hot", TE)
        probs, sums, pick, place = b("probs", TE), b("sums", [P, TILES]), b("pick", [P, TILES]), b("place", TE)
        carry, pos, kept, gate = b("carry", TE), b("pos", [P, TILES]), b("kept", [P, TILES]), b("gate", [P, TILES])
        base = b("base", [P, TILES])
        put, get = b("put", [P, TILES], i32), b("get", [P, TILES], i32)
        w1, w2 = b("w1", [P, 2, KB, FF]), b("w2", [P, 2, FC, D])
        b1s, b2 = b("b1s", [P, 2, FC]), b("b2", [P, 2, D])
        rows, cols = b("rows", [P, 2, CT, D]), b("cols", [P, KB, CPAD])
        mid, ans = b("mid", [P, FC, CPAD]), b("ans", [P, CT, D])
        y, work = b("y", [P, LIVE, D]), b("work", [P, D])
        over = b("over", [P, D], u32)
        zero_row, top_row, low_row = b("zero_row", [P, D]), b("top_row", [P, D]), b("low_row", [P, D])

        (d_own, numbered, shifted, exped, hot_ready, place_done, put_ready, moved, turned, c_copied, m_done,
         m_ready, y_done, ans_ready, fixed) = (
            s(n) for n in ("d_own numbered shifted exped hot_ready place_done put_ready moved turned c_copied "
                           "m_done m_ready y_done ans_ready fixed").split())
        load_in, ans_out, fetched, out_done = [s("load_in0"), s("load_in1")], s("ans_out"), s("fetched"), s("out_done")
        block = ctx.enter_context(nc.Block())

        @block.sync
        def _(sp):
            def weights(e, h):
                one = bass.ds(e, 1)
                sp.dma_start(w1[:, h, :, :], v["e_w1"][one, :, :].rearrange("a (k p) f -> p (a k) f", p=P)).then_inc(load_in[h], 16)
                sp.dma_start(w2[:, h, :, :], v["e_w2"][one, :, :].rearrange("a (k p) c -> p (a k) c", p=P)).then_inc(load_in[h], 16)
                sp.dma_start(b1s[:, h, :], v["e_b1"][one, :, :].rearrange("a p f -> (a p) f")).then_inc(load_in[h], 16)
                sp.dma_start(b2[:, h, :], v["e_b2"][one, :].to_broadcast([P, D])).then_inc(load_in[h], 16)

            def tokens(e, h):
                sp.dma_start(rows[:, h, :, :], slots.rearrange("(e t p) c -> e p t c", p=P, t=CT)[bass.ds(e, 1), :, :, :]
                             .rearrange("a p t c -> (a p) t c")).then_inc(load_in[h], 16)

            weights(0, 0)
            weights(1, 1)
            sp.wait_ge(moved, 16 * LIVE)
            tokens(0, 0)
            tokens(1, 1)
            with sp.Fori(0, EXPERTS // 2) as r:
                for h in range(2):
                    sp.wait_ge(ans_ready, r * (2 * CT) + (CT * (h + 1) + 2))
                    sp.dma_start(answers.rearrange("(e t p) c -> e p t c", p=P, t=CT)[bass.ds(r * 2 + h, 1), :, :, :]
                                 .rearrange("a p t c -> (a p) t c"), ans[:, :, :]).then_inc(ans_out, 16)
                    nxt = r * 2 + (2 + h)
                    weights(nxt, h)
                    tokens(nxt, h)
            for h in range(2):
                sp.wait_ge(load_in[h], 80 * (EXPERTS // 2 + 1))
            with sp.Fori(0, LIVE) as t:
                sp.wait_ge(fixed, t + 1)
                sp.dma_start(rows_of(v["out"], t), tile_of(x_all, t)).then_inc(out_done, 16)
            sp.wait_ge(out_done, 16 * LIVE)

        @block.gpsimd
        def _(g):
            g.iota(number[:, :, :], [[0, TILES], [1, EXPERTS]], base=0, channel_multiplier=0,
                   allow_small_or_imprecise_dtypes=True).then_inc(numbered, 1)
            g.wait_ge(put_ready, 2)
            for t in range(LIVE):
                g.indirect_dma_start(slots, bass.IndirectOffsetOnAxis(ap=put[:, t:t + 1], axis=0), xn_all[:, t, :], None,
                                     bounds_check=EXPERTS * CPAD - 1, oob_is_err=False).then_inc(moved, 16)
            g.wait_ge(ans_out, 16 * EXPERTS + 16)
            for t in range(LIVE):
                g.indirect_dma_start(y[:, t, :], None, answers,
                                     bass.IndirectOffsetOnAxis(ap=get[:, t:t + 1], axis=0)).then_inc(fetched, 16)
            g.wait_ge(fetched, 16 * LIVE)

        @block.vector
        def _(d):
            own = Own(d, d_own)
            wide = TE

            def over_experts(a): return a.unsqueeze(2).to_broadcast(wide)

            own.link(d.memset(zero_row[:, :], 0.0))
            own.link(d.memset(top_row[:, :], 10000.0))
            own.link(d.memset(low_row[:, :], -10000.0))
            own.link(d.tensor_reduce(best[:, :], logits[:, :, :], AX.X, ALU.max))
            d.tensor_tensor(shown[:, :, :], logits[:, :, :], over_experts(best[:, :]), ALU.subtract).then_inc(shifted, 1)
            d.wait_ge(exped, 1)
            own.link(d.tensor_reduce(sums[:, :], probs[:, :, :], AX.X, ALU.add))
            own.link(d.reciprocal(sums[:, :], sums[:, :]))
            own.link(d.tensor_tensor(probs[:, :, :], probs[:, :, :], over_experts(sums[:, :]), ALU.mult))
            own.link(d.tensor_reduce(best[:, :], probs[:, :, :], AX.X, ALU.max))
            own.link(d.tensor_tensor(shown[:, :, :], probs[:, :, :], over_experts(best[:, :]), ALU.is_lt))
            d.wait_ge(numbered, 1)
            own.link(d.scalar_tensor_tensor(out=shown[:, :, :], in0=shown[:, :, :], scalar=float(EXPERTS),
                                            in1=number[:, :, :], op0=ALU.mult, op1=ALU.add))
            own.link(d.tensor_reduce(pick[:, :], shown[:, :, :], AX.X, ALU.min))
            own.link(d.tensor_tensor(hot[:, :, :], number[:, :, :], over_experts(pick[:, :]), ALU.is_equal))
            own.link(d.memset(carry[:, 0, :], 0.0))
            for t in range(1, TILES):
                own.link(d.tensor_tensor(carry[:, t, :], carry[:, t - 1, :], hot[:, t - 1, :], ALU.add))
            d.sem_inc(hot_ready, 1)
            d.wait_ge(place_done, 1)
            own.link(d.tensor_tensor(place[:, :, :], hot[:, :, :],
                                     banks[0][:, 0:TILES * EXPERTS].rearrange("p (t e) -> p t e", e=EXPERTS), ALU.mult))
            own.link(d.tensor_reduce(pos[:, :], place[:, :, :], AX.X, ALU.add))
            own.link(d.tensor_scalar(pos[:, :], pos[:, :], -1.0, None, ALU.add))
            own.link(d.tensor_scalar(kept[:, :], pos[:, :], float(CAP), None, ALU.is_lt))
            own.link(d.tensor_tensor(gate[:, :], best[:, :], kept[:, :], ALU.mult))
            own.link(d.tensor_scalar(base[:, :], pick[:, :], float(CPAD), None, ALU.mult))
            own.link(d.tensor_scalar(kept[:, :], kept[:, :], float(-FAR), float(FAR), ALU.mult, ALU.add))
            own.link(d.tensor_tensor(kept[:, :], kept[:, :], pos[:, :], ALU.add))
            d.tensor_tensor(put[:, :], kept[:, :], base[:, :], ALU.add).then_inc(put_ready, 1)
            own.link(d.tensor_scalar(pos[:, :], pos[:, :], float(CAP - 1), None, ALU.min))
            d.tensor_tensor(get[:, :], pos[:, :], base[:, :], ALU.add).then_inc(put_ready, 1)
            d.sem_inc(ans_out, 16)
            d.sem_inc(ans_ready, 2)
            with d.Fori(0, EXPERTS // 2) as r:
                for h in range(2):
                    d.wait_ge(ans_out, r * 32 + 16 * (h + 1))
                    for c in range(CT):
                        d.wait_ge(y_done, r * (2 * CT) + (CT * h + c + 1))
                        d.tensor_tensor(ans[:, c, :], banks[4 + c % 2][:, 0:D], b2[:, h, :], ALU.add).then_inc(ans_ready, 1)
            d.wait_ge(fetched, 16 * LIVE)
            fix0 = own.n
            with d.Fori(0, LIVE) as t:
                mine = Own(d, d_own, fix0, 8, t)
                one = work[:, :]
                mine.link(d.tensor_scalar(one, tile_of(y, t), gate[:, bass.ds(t, 1)], None, ALU.mult))
                mine.link(d.tensor_tensor(over[:, :], one, one, ALU.not_equal))
                mine.rest(idle)
                mine.link(d.copy_predicated(one, over[:, :], zero_row[:, :]))
                for row, limit, op in ((top_row, BIG, ALU.is_gt), (low_row, -BIG, ALU.is_lt)):
                    mine.link(d.tensor_scalar(over[:, :], one, limit, None, op))
                    mine.rest(idle)
                    mine.link(d.copy_predicated(one, over[:, :], row[:, :]))
                mine.link(d.tensor_tensor(tile_of(x_all, t), tile_of(x_all, t), one, ALU.add))
                d.sem_inc(fixed, 1)
                mine.closed()

        @block.scalar
        def _(a):
            a.wait_ge(shifted, 1)
            a.activation(probs[:, :, :].rearrange("p t e -> p (t e)"), shown[:, :, :].rearrange("p t e -> p (t e)"),
                         ACT.Exp).then_inc(exped, 1)
            with a.Fori(0, EXPERTS // 2) as r:
                for h in range(2):
                    for k in range(KB):
                        a.wait_ge(turned, r * (2 * KB) + (KB * h + k + 1))
                        a.activation(cols[:, k, :], banks[k][:, :], ACT.Copy).then_inc(c_copied, 1)
                    for f in range(FC):
                        a.wait_ge(m_done, r * (2 * FC) + (FC * h + f + 1))
                        a.activation(mid[:, f, :], banks[2 + f % 2][:, :], ACT.Relu, bias=b1s[:, h, f:f + 1])\
                         .then_inc(m_ready, 1)

        @block.tensor
        def _(t_):
            t_.wait_ge(hot_ready, 1)
            n = TILES * EXPERTS
            nc.tensor.matmul(banks[0][:, 0:n], upto[:, :], hot[:, :, :].rearrange("p t e -> p (t e)"), start=True, stop=False)
            nc.tensor.matmul(banks[0][:, 0:n], ones[:, :], carry[:, :, :].rearrange("p t e -> p (t e)"), start=False, stop=True)\
              .then_inc(place_done, 1)
            t_.wait_ge(put_ready, 1)
            with t_.Fori(0, EXPERTS // 2) as r:
                for h in range(2):
                    t_.wait_ge(load_in[h], r * 80 + 80)
                    for k in range(KB):
                        for c in range(CT):
                            last = nc.tensor.transpose(banks[k][:, c * P:(c + 1) * P], rows[:, h, c, k * P:(k + 1) * P], ident[:, :])
                        last.then_inc(turned, 1)
                    t_.wait_ge(c_copied, r * (2 * KB) + KB * (h + 1))
                    for f in range(FC):
                        if f >= 2:
                            t_.wait_ge(m_ready, r * (2 * FC) + (FC * h + f - 1))
                        for k in range(KB):
                            last = nc.tensor.matmul(banks[2 + f % 2][:, :], w1[:, h, k, f * P:(f + 1) * P], cols[:, k, :],
                                                    start=(k == 0), stop=(k == KB - 1))
                        last.then_inc(m_done, 1)
                    t_.wait_ge(m_ready, r * (2 * FC) + FC * (h + 1))
                    for c in range(CT):
                        t_.wait_ge(ans_ready, r * (2 * CT) + (CT * h + c + 1))
                        for f in range(FC):
                            last = nc.tensor.matmul(banks[4 + c % 2][:, 0:D], mid[:, f, c * P:(c + 1) * P], w2[:, h, f, :],
                                                    start=(f == 0), stop=(f == FC - 1))
                        last.then_inc(y_done, 1)


def build(nc, *arrays):
    v = dict(zip(ARRAYS, arrays))
    top = ExitStack()
    with top:
        def sem(name, ctx=top): return ctx.enter_context(nc.semaphore(name))

        def sb(name, shape, dt=fp32, ctx=top): return ctx.enter_context(nc.sbuf_tensor(name, shape, dt))

        def dram(name, rows, cols):
            return nc.dram_tensor(name, [rows, cols], fp32, kind="Internal").ap()

        v["kv_table"], v["q_table"] = dram("kv_table", ROWS, 2 * D), dram("q_table", ROWS, D)
        v["parts_table"] = nc.dram_tensor("parts_table", [ROWS, 3 * D], bf16, kind="Internal").ap()
        v["acc"] = [dram(f"acc{k}", ROWS + P, D) for k in range(NACC)]
        v["slots"], v["answers"] = dram("slots", (EXPERTS + 2) * CPAD, D), dram("answers", EXPERTS * CPAD, D)
        banks = [top.enter_context(nc.psum_tensor(f"bank{k}", [P, 512], fp32)) for k in range(8)]
        v["x_all"] = sb("x_all", [P, TILES, D])
        v["xn_all"] = sb("xn_all", [P, TILES, D])
        v["ident"], v["ones"] = sb("ident", [P, P]), sb("ones", [P, P])
        v["before"], v["upto"] = sb("before", [P, P]), sb("upto", [P, P])
        v["kv_sum"] = sb("kv_sum", [P, KB, P + 1])
        v["base_i"], v["base_all"] = sb("base_i", [P, GROUPS], i32), sb("base_all", [P, GROUPS])
        v["near_flag"], v["far_flag"] = sb("near_flag", [P, 1], i32), sb("far_flag", [P, 1], i32)
        v["bias_rows"] = sb("bias_rows", [P, 2 * D], bf16)
        v["logits"] = sb("logits", [P, TILES, EXPERTS])
        v["consts_made"] = sem("consts_made")
        build_nodes(nc, sem, sb, banks, v)
        build_windows(nc, sem, sb, banks, v)
        build_mixer(nc, sem, sb, banks, v)
        build_near_edges(nc, sem, sb, banks, v)
        build_edges(nc, sem, sb, banks, v)
        build_routing(nc, sem, sb, banks, v)
        build_experts(nc, sem, sb, banks, v)


ARRAYS = ("x", "row_mask", "head_mask", "src", "dst", "dst_row", "weight", "attr", "ln_gb", "w_gnn", "b_gnn", "wo", "bo",
          "w_edge", "b_edge", "part_mask", "w_mix", "wm", "w1m", "w2m", "gb_mix", "gate_w", "gate_b", "e_w1", "e_b1", "e_w2", "e_b2", "out")


def kernel(**inputs):
    import numpy as np
    import concourse.bacc as bacc
    from concourse.bass_utils import run_bass_kernel_spmd

    a = {k: np.asarray(x) for k, x in inputs.items()}
    g = {k[7:]: x for k, x in a.items() if k.startswith("L0_gnn_")}
    m = {k[7:]: x for k, x in a.items() if k.startswith("L0_mix_")}
    f = {k[7:]: x for k, x in a.items() if k.startswith("L0_ffn_")}
    slots_all = (ROUNDS + 1) * CH * P
    more = slots_all - EDGES

    def to_chunks(e, fill):
        return np.pad(e, (0, more), constant_values=fill).reshape(ROUNDS + 1, CH, P)

    def spread(row):
        return np.broadcast_to(row, (P,) + row.shape)

    attr = np.pad(a["edge_attr_64"], ((0, more), (0, 0))).reshape(ROUNDS + 1, CH // 2, 2, P, R)
    arrays = {
        "x": np.pad(a["x"], ((0, ROWS - NODES), (0, 0))),
        "row_mask": (np.arange(ROWS) < NODES).astype(np.float32).reshape(TILES, P).T,
        "head_mask": (np.arange(P)[:, None] // HD == np.arange(HB)).astype(np.float32),
        "src": to_chunks(a["src"], 0).transpose(0, 2, 1),
        "dst": to_chunks(a["dst"], NODES).transpose(0, 2, 1),
        "dst_row": to_chunks(a["dst"], NODES).reshape(ROUNDS + 1, CH * P),
        "weight": to_chunks(a["edge_weight"], 0).transpose(0, 2, 1),
        "attr": attr.transpose(2, 4, 0, 1, 3).reshape(2 * R, ROUNDS + 1, CH // 2 * P),
        "ln_gb": spread(np.stack([g["ln_g"], g["ln_b"]])),
        "w_gnn": np.concatenate([g["Wq"].T, g["Wk"].T, g["Wv"].T], 1),
        "b_gnn": spread(np.concatenate([g["bq"], g["bk"], g["bv"]])),
        "wo": g["Wo"].T, "bo": spread(g["bo"]),
        "w_edge": np.tile(np.concatenate([g["Wdk"].T, g["Wdv"].T], 1), (2, 1)),
        "b_edge": spread(np.concatenate([g["bdk"], g["bdv"]])),
        "part_mask": (np.arange(P)[:, None] % R == np.arange(3)).astype(np.float32),
        "w_mix": np.concatenate([m["Wq"], m["Wk"], m["Wv"]], 1),
        "wm": m["Wm"], "w1m": m["W1"], "w2m": m["W2"],
        "gb_mix": spread(np.stack([m["g1"], m["b1"], m["g2"], m["b2"]])),
        "gate_w": f["gate_w"], "gate_b": spread(f["gate_b"]),
        "e_w1": np.concatenate([f["w1"], f["w1"][:2]]), "e_b1": np.concatenate([f["b1"], f["b1"][:2]]).reshape(EXPERTS + 2, FC, P).transpose(0, 2, 1),
        "e_w2": np.concatenate([f["w2"], f["w2"][:2]]), "e_b2": np.concatenate([f["b2"], f["b2"][:2]]),
    }
    arrays = {f"in_{k}": np.ascontiguousarray(arrays[k]) for k in ARRAYS[:-1]}
    nc = bacc.Bacc("TRN2", target_bir_lowering=False, num_devices=1)
    args = [nc.dram_tensor(k, x.shape, mybir.dt.from_np(x.dtype), kind="ExternalInput").ap() for k, x in arrays.items()]
    args.append(nc.dram_tensor("out_rows", [REAL_TILES * P, D], fp32, kind="ExternalOutput").ap())
    build(nc, *args)
    r = run_bass_kernel_spmd(nc, [arrays], core_ids=[0])
    return r.results[0]["out_rows"][:NODES]
```

```python
import math

import concourse.bass as bass
from concourse import mybir
from contextlib import ExitStack

P = 128
NODES, EDGES, D, R = 3125, 53125, 256, 64
TILES = 26
ROWS = TILES * P
REAL_TILES = -(-NODES // P)
PAIR = 2
PAIRS = TILES // PAIR
QUAD, QUADS = 4, 4
CH = QUAD * QUADS
ROUNDS = 26
GROUPS = (ROUNDS + 1) * QUADS
KE = R + 1
HALF = CH // 2
SLOTS = 8
NACC = 2
HEADS, HD = 8, D // 8
EXPERTS, FF = 8, 1024
FC = FF // P
CAP = max(1, math.ceil(1.25 * NODES / EXPERTS))
CT = 4
CPAD = CT * P
LN_EPS, ATT_EPS, CUTOFF = 1e-5, 1e-6, 5.0
KB = D // P
HB = HEADS // KB
ZW = P + HB
DS = D + 2
FAR = 1 << 20
BIG = 3.4028234e38

fp32, bf16, i32, u32 = mybir.dt.float32, mybir.dt.bfloat16, mybir.dt.int32, mybir.dt.uint32
ALU = mybir.AluOpType
ACT = mybir.ActivationFunctionType
AX = mybir.AxisListType


class Own:

    def __init__(self, eng, sem, before=0, per=0, r=0):
        self.eng, self.sem, self.per, self.r = eng, sem, per, r
        self.start = self.n = before

    def link(self, ins):
        ins.then_inc(self.sem, 1)
        self.n += 1
        self.eng.wait_ge(self.sem, self.r * self.per + self.n)

    def rest(self, idle):
        self.eng.sem_inc(idle, 1)

    def closed(self):
        assert self.n - self.start == self.per, (self.n - self.start, self.per)


def tile_of(all_, t):
    return all_[:, bass.ds(t, 1), :].rearrange("p a c -> p (a c)")


def rows_of(table, t):
    return table.rearrange("(t p) c -> t p c", p=P)[bass.ds(t, 1), :, :].rearrange("a p c -> (a p) c")


class Windows:

    def __init__(self, nc, s, b, v, bank):
        self.nc, self.v, self.bank = nc, v, bank
        self.rows, self.low, self.span = b("rows", [P, QUAD * P], i32), b("low", [P, 1]), b("span", [P, 1])
        self.diag, self.widest = b("diag", [P, 2, GROUPS]), b("widest", [P, 1])
        self.rows_in, self.own, self.diag_ready, self.spread_done = (
            s(n) for n in "win_rows_in win_own win_diag_ready win_spread_done".split())

    def load(self, sp):
        sp.dma_start(self.rows[0:GROUPS, :], self.v["dst_row"].rearrange("i (q e) -> (i q) e", q=QUADS)).then_inc(self.rows_in, 16)

    def vector(self, d):
        v, rows, low, span, diag, widest = self.v, self.rows, self.low, self.span, self.diag, self.widest
        ident = v["ident"]
        own = Own(d, self.own)
        own.link(d.memset(low[:, :], 0.0))
        own.link(d.memset(span[:, :], 0.0))
        d.wait_ge(self.rows_in, 16)
        own.link(d.tensor_reduce(low[0:GROUPS, :], rows[0:GROUPS, :], AX.X, ALU.min))
        own.link(d.tensor_reduce(span[0:GROUPS, :], rows[0:GROUPS, :], AX.X, ALU.max))
        own.link(d.tensor_tensor(span[:, :], span[:, :], low[:, :], ALU.subtract))
        d.wait_ge(v["consts_made"], 3)
        own.link(d.tensor_scalar(diag[:, 0, :], ident[:, 0:GROUPS], low[:, 0:1], None, ALU.mult))
        d.tensor_scalar(diag[:, 1, :], ident[:, 0:GROUPS], span[:, 0:1], None, ALU.mult).then_inc(self.diag_ready, 1)
        d.wait_ge(self.spread_done, 1)
        own.link(d.tensor_copy(v["base_all"][:, :], self.bank[:, 0:GROUPS]))
        own.link(d.tensor_copy(v["base_i"][:, :], self.bank[:, 0:GROUPS]))
        own.link(d.tensor_reduce(widest[:, :], self.bank[:, GROUPS:2 * GROUPS], AX.X, ALU.max))
        own.link(d.tensor_scalar(v["near_flag"][:, :], widest[:, :], float(P), None, ALU.is_lt))
        own.link(d.tensor_scalar(v["far_flag"][:, :], widest[:, :], float(P), None, ALU.is_ge))

    def tensor(self, t):
        t.wait_ge(self.diag_ready, 1)
        self.nc.tensor.matmul(self.bank[:, 0:2 * GROUPS], self.v["ones"][:, :], self.diag[:, :, :].rearrange("p a g -> p (a g)"),
                              start=True, stop=True).then_inc(self.spread_done, 1)


def build_nodes(nc, sem, sb, banks, v):
    x_all, rows_all, ident, before, upto, ones = v["x_all"], v["rows_all"], v["ident"], v["before"], v["upto"], v["ones"]
    kv_sum, consts_made = v["kv_sum"], v["consts_made"]
    q_table, kv_table, acc, slots = v["q_table"], v["kv_table"], v["acc"], v["slots"]
    turn_bank, q_banks, kv_banks, mix_banks, sums_bank = banks[0], banks[1:3], banks[3:5], banks[5:7], banks[7]
    ctx = ExitStack()
    with ctx:
        def s(name): return sem("n_" + name, ctx)

        def b(name, shape, dt=fp32): return sb("n_" + name, shape, dt, ctx)

        ln_gb, bias = b("ln_gb", [P, 2, D]), b("bias", [P, 3 * D])
        bo = b("bo", [P, D])
        w_gnn, w_mix = b("w_gnn", [P, KB, 3 * D]), b("w_mix", [P, KB, 3 * D])
        mask, zeros = b("mask", [P, TILES]), b("zeros", [P, 2048])
        stats, work = b("stats", [P, TILES, 6]), b("work", [P, TILES // 2, D])
        mv, rs, mv2, rs2 = b("mv", [P, TILES, 2]), b("rs", [P, TILES]), b("mv2", [P, TILES, 2]), b("rs2", [P, TILES])
        xn, xg = b("xn", [P, 2, D]), b("xg", [P, 2, D])
        xt, gt = b("xt", [P, 2, D]), b("gt", [P, 2, D])
        q, kv = b("q", [P, 2, D]), b("kv", [P, 2, 2 * D])
        qneg, kneg = b("qneg", [P, 2, D]), b("kneg", [P, 2, D])
        kpos, vext = b("kpos", [P, 2, D]), b("vext", [P, 2, KB, P + 1])
        parts, rest = b("parts", [P, 2, 3, D], bf16), b("rest", [P, D])

        x_in, w_in, zeros_made, zero_out = [s("x_in0"), s("x_in1")], s("w_in"), s("zeros_made"), s("zero_out")
        p_own, d_own, n_own, a_own, idle = s("p_own"), s("d_own"), s("n_own"), s("a_own"), s("idle")
        stat, var, std, normed, turned, copied = (s(n) for n in "stat var std normed turned copied".split())
        q_done, kv_done, mix_done, q_ready, kv_ready, exp_ready = (
            s(n) for n in "q_done kv_done mix_done q_ready kv_ready exp_ready".split())
        k_ready, v_ready, sums_done, sum_added, parts_ready = (s(n) for n in "k_ready v_ready sums_done sum_added parts_ready".split())
        rows_out = [s("rows_out0"), s("rows_out1")]
        windows = Windows(nc, s, b, v, turn_bank)
        block = ctx.enter_context(nc.Block())
        SPAN = TILES // 2

        def rounds(eng, body):
            body(0)
            with eng.Fori(1, PAIRS - 1) as r:
                body(r)
            body(PAIRS - 1, last=True)

        @block.sync
        def _(sp):
            windows.load(sp)
            xr = v["x"].rearrange("(t p) c -> p t c", p=P)
            for part in range(2):
                tiles = slice(part * SPAN, (part + 1) * SPAN)
                sp.dma_start(x_all[:, tiles, :], xr[:, tiles, :]).then_inc(x_in[part], 16)
            sp.dma_start(ln_gb[:, :, :], v["ln_gb"]).then_inc(w_in, 16)
            sp.dma_start(bias[:, :], v["b_gnn"]).then_inc(w_in, 16)
            sp.dma_start(w_gnn[:, :, :], v["w_gnn"].rearrange("(k p) c -> p k c", p=P)).then_inc(w_in, 16)
            sp.dma_start(w_mix[:, :, :], v["w_mix"].rearrange("(k p) c -> p k c", p=P)).then_inc(w_in, 16)
            sp.dma_start(bo[:, :], v["bo"]).then_inc(w_in, 16)
            sp.dma_start(mask[:, :], v["row_mask"]).then_inc(w_in, 16)
            sp.wait_ge(zeros_made, 1)
            sent = 0
            for table, tiles, width in [(a, TILES + 1, D) for a in acc] + [(slots, EXPERTS * CT, DS)]:
                span = 2048 // width
                for t in range(0, tiles, span):
                    m = min(span, tiles - t)
                    sp.dma_start(table[t * P:(t + m) * P, :].rearrange("(t p) c -> p t c", p=P),
                                 zeros[:, 0:m * width].rearrange("p (t c) -> p t c", c=width)).then_inc(zero_out, 16)
                    sent += 1
            with sp.Fori(0, PAIRS) as r:
                for h in range(2):
                    sp.wait_ge(q_ready, r * 2 + (h + 1))
                    sp.dma_start(rows_of(q_table, r * 2 + h), q[:, h, :]).then_inc(rows_out[h], 16)
                    sp.wait_ge(kv_ready, r * 2 + (h + 1))
                    sp.dma_start(rows_of(kv_table, r * 2 + h), kv[:, h, :]).then_inc(rows_out[h], 16)
                    sp.wait_ge(parts_ready, r * 2 + (h + 1))
                    sp.dma_start(rows_of(v["parts_table"], r * 2 + h), parts[:, h, :, :].rearrange("p a c -> p (a c)"))\
                      .then_inc(rows_out[h], 16)
            for h in range(2):
                sp.wait_ge(rows_out[h], 48 * PAIRS)
            sp.wait_ge(zero_out, 16 * sent)

        @block.gpsimd
        def _(g):
            own = Own(g, p_own)
            own.link(g.memset(ident[:, :], 0.0))
            own.link(g.memset(ones[:, :], 1.0))
            g.affine_select(out=ident[:, :], in_=ident[:, :], compare_op=ALU.not_equal, fill=1.0, base=0,
                            pattern=[[-1, P]], channel_multiplier=1).then_inc(consts_made, 1)
            g.affine_select(out=before[:, :], in_=ones[:, :], compare_op=ALU.is_gt, fill=0.0, base=0,
                            pattern=[[-1, P]], channel_multiplier=1).then_inc(consts_made, 1)
            g.affine_select(out=upto[:, :], in_=ones[:, :], compare_op=ALU.is_ge, fill=0.0, base=0,
                            pattern=[[1, P]], channel_multiplier=-1).then_inc(consts_made, 1)
            g.wait_ge(consts_made, 3)
            with g.Fori(0, PAIRS) as r:
                for h in range(2):
                    own = Own(g, p_own, 2 + 4 * h, 8, r)
                    g.wait_ge(q_ready, r * 2 + (h + 1))
                    own.rest(idle)
                    own.link(g.tensor_copy(parts[:, h, 0, :], q[:, h, :]))
                    own.link(g.tensor_tensor(rest[:, :], q[:, h, :], parts[:, h, 0, :], ALU.subtract))
                    own.rest(idle)
                    own.link(g.tensor_copy(parts[:, h, 1, :], rest[:, :]))
                    own.link(g.tensor_tensor(parts[:, h, 2, :], rest[:, :], parts[:, h, 1, :], ALU.subtract))
                    g.sem_inc(parts_ready, 1)

        @block.vector
        def _(d):
            d.memset(zeros[:, :], 0.0).then_inc(zeros_made, 1)
            first = Own(d, d_own)
            first.link(d.memset(v["mix_q"][:, TILES, :], 0.0))
            windows.vector(d)
            for part in range(2):
                d.wait_ge(x_in[part], 16)
                for t in range(part * SPAN, (part + 1) * SPAN):
                    d.bn_stats(stats[:, t, :], x_all[:, t, :]).then_inc(stat, 1)
            for t in range(TILES):
                d.wait_ge(stat, t + 1)
                d.bn_aggr(mv[:, t, :], stats[:, t, :]).then_inc(stat, 1)
            d.wait_ge(stat, 2 * TILES)
            d.tensor_scalar(rs[:, :], mv[:, :, 1], LN_EPS, None, ALU.add).then_inc(var, 1)
            d.wait_ge(std, 1)
            first.link(d.reciprocal(rs[:, :], rs[:, :]))
            for part in range(2):
                for t in range(part * SPAN, (part + 1) * SPAN):
                    d.tensor_scalar(work[:, t - part * SPAN, :], x_all[:, t, :], mv[:, t:t + 1, 0], rs[:, t:t + 1],
                                    ALU.subtract, ALU.mult).then_inc(stat, 1)
                d.wait_ge(stat, 2 * TILES + (2 * part + 1) * SPAN)
                for t in range(part * SPAN, (part + 1) * SPAN):
                    d.bn_stats(stats[:, t, :], work[:, t - part * SPAN, :]).then_inc(stat, 1)
                d.wait_ge(stat, 2 * TILES + 2 * (part + 1) * SPAN)
            for t in range(TILES):
                d.bn_aggr(mv2[:, t, :], stats[:, t, :]).then_inc(stat, 1)
            d.wait_ge(stat, 5 * TILES)
            d.tensor_scalar(rs2[:, :], mv2[:, :, 1], LN_EPS, None, ALU.add).then_inc(var, 1)
            d.wait_ge(std, 2)
            first.link(d.reciprocal(rs2[:, :], rs2[:, :]))
            d.wait_ge(w_in, 96)

            def norm(r, c):
                t, h = r * 2 + c, c % 2
                own = Own(d, n_own, 3 * c, 6, r)
                x = tile_of(x_all, t)
                own.link(d.tensor_scalar(xn[:, h, :], x, mv[:, bass.ds(t, 1), 0], rs[:, bass.ds(t, 1)], ALU.subtract, ALU.mult))
                d.scalar_tensor_tensor(out=x, in0=xn[:, h, :], scalar=2.0, in1=x, op0=ALU.mult, op1=ALU.add).then_inc(idle, 1)
                own.link(d.tensor_scalar(xg[:, h, :], xn[:, h, :], mv2[:, bass.ds(t, 1), 0], rs2[:, bass.ds(t, 1)],
                                         ALU.subtract, ALU.mult))
                d.tensor_tensor(x, x, bo[:, :], ALU.add).then_inc(idle, 1)
                own.link(d.tensor_tensor(xg[:, h, :], xg[:, h, :], ln_gb[:, 0, :], ALU.mult))
                d.tensor_tensor(xg[:, h, :], xg[:, h, :], ln_gb[:, 1, :], ALU.add).then_inc(normed, 1)

            def positive(r, c):
                h = c % 2
                d.wait_ge(exp_ready, r * 2 + (c + 1))
                d.scalar_tensor_tensor(out=tile_of(v["mix_q"], r * 2 + c), in0=q_banks[h][:, D:2 * D], scalar=0.0,
                                       in1=qneg[:, h, :], op0=ALU.max, op1=ALU.add).then_inc(idle, 1)
                d.scalar_tensor_tensor(out=kpos[:, h, :], in0=mix_banks[h][:, 0:D], scalar=0.0, in1=kneg[:, h, :],
                                       op0=ALU.max, op1=ALU.add).then_inc(k_ready, 1)

            def body(r, last=False):
                for h in range(2):
                    if not last:
                        d.wait_ge(turned, r * 2 + (h + 1))
                        norm(r, h + 2)
                    if not (isinstance(r, int) and r == 0 and h == 0):
                        positive(r, h - 1)
                    d.wait_ge(q_done, r * 2 + (h + 1))
                    if not (isinstance(r, int) and r == 0):
                        d.wait_ge(rows_out[h], r * 48)
                    d.tensor_tensor(q[:, h, :], q_banks[h][:, 0:D], bias[:, 0:D], ALU.add).then_inc(q_ready, 1)
                    d.wait_ge(kv_done, r * 2 + (h + 1))
                    d.tensor_tensor(kv[:, h, :], kv_banks[h][:, :], bias[:, D:3 * D], ALU.add).then_inc(kv_ready, 1)
                    if not (isinstance(r, int) and r == 0):
                        add_sums(r, h - 2)

            def add_sums(r, c):
                d.wait_ge(sums_done, r * 2 + (c + 1))
                d.wait_ge(sum_added, r * 2 + (c + 1))
                d.tensor_tensor(kv_sum[:, :, :], kv_sum[:, :, :],
                                sums_bank[:, 0:KB * (P + 1)].rearrange("p (k c) -> p k c", k=KB), ALU.add).then_inc(sum_added, 1)

            d.memset(kv_sum[:, :, :], 0.0).then_inc(sum_added, 1)
            norm(0, 0)
            norm(0, 1)
            rounds(d, body)
            positive(PAIRS - 1, 1)
            add_sums(PAIRS - 1, 0)
            add_sums(PAIRS - 1, 1)

        @block.scalar
        def _(a):
            def turned_rows(r, c):
                h = c % 2
                a.wait_ge(turned, r * 2 + (c + 1))
                a.activation(xt[:, h, :], turn_bank[:, 0:D], ACT.Copy).then_inc(idle, 1)
                a.activation(gt[:, h, :], turn_bank[:, D:2 * D], ACT.Copy).then_inc(idle, 1)
                a.activation(tile_of(rows_all, r * 2 + c), turn_bank[:, 0:D], ACT.Copy).then_inc(copied, 1)

            def body(r, last=False):
                for h in range(2):
                    if not (last and h):
                        turned_rows(r, h + 1)
                    a.wait_ge(q_ready, r * 2 + (h + 1))
                    a.activation(qneg[:, h, :], q_banks[h][:, D:2 * D], ACT.Relu, scale=-1.0).then_inc(a_own, 1)
                    a.wait_ge(mix_done, r * 2 + (h + 1))
                    a.activation(kneg[:, h, :], mix_banks[h][:, 0:D], ACT.Relu, scale=-1.0).then_inc(a_own, 1)
                    for k in range(KB):
                        a.activation(vext[:, h, k, 0:P], mix_banks[h][:, D + k * P:D + (k + 1) * P], ACT.Copy,
                                     scale=1.0 / NODES).then_inc(idle, 1)
                        a.activation(vext[:, h, k, P:P + 1], mask[:, bass.ds(r * 2 + h, 1)], ACT.Copy).then_inc(v_ready, 1)
                    a.wait_ge(a_own, r * 4 + (2 * h + 2))
                    a.activation(qneg[:, h, :], qneg[:, h, :], ACT.Exp, scale=-1.0).then_inc(idle, 1)
                    a.activation(kneg[:, h, :], kneg[:, h, :], ACT.Exp, scale=-1.0).then_inc(exp_ready, 1)

            for part, root in enumerate((rs, rs2)):
                a.wait_ge(var, part + 1)
                a.activation(root[:, :], root[:, :], ACT.Sqrt).then_inc(std, 1)
            a.wait_ge(w_in, 96)
            turned_rows(0, 0)
            rounds(a, body)

        @block.tensor
        def _(t):
            def turn(r, c):
                h = c % 2
                t.wait_ge(normed, r * 2 + (c + 1))
                if not (isinstance(r, int) and r * 2 + c == 0):
                    t.wait_ge(copied, r * 2 + c)
                for k in range(2 * KB):
                    half = (xn if k < KB else xg)[:, h, (k % KB) * P:(k % KB + 1) * P]
                    last = nc.tensor.transpose(turn_bank[:, k * P:(k + 1) * P], half, ident[:, :])
                last.then_inc(turned, 1)

            def sums(r, c):
                t.wait_ge(sum_added, r * 2 + (c + 1))
                h = c % 2
                t.wait_ge(k_ready, r * 2 + (c + 1))
                t.wait_ge(v_ready, r * 4 + (2 * c + 2))
                for k in range(KB):
                    last = nc.tensor.matmul(sums_bank[:, k * (P + 1):(k + 1) * (P + 1)],
                                            kpos[:, h, k * P:(k + 1) * P], vext[:, h, k, :],
                                            start=True, stop=True)
                last.then_inc(sums_done, 1)

            def products(r, h):
                t.wait_ge(copied, r * 2 + (h + 1))
                for m in range(KB):
                    for k in range(KB):
                        nc.tensor.matmul(q_banks[h][:, D + m * P:D + (m + 1) * P], w_mix[:, k, m * P:(m + 1) * P],
                                         xt[:, h, k * P:(k + 1) * P], start=(k == 0), stop=(k == KB - 1))
                for out_, lhs, w, signal in (
                        (q_banks[h][:, 0:D], gt, w_gnn[:, :, 0:D], q_done),
                        (kv_banks[h][:, :], gt, w_gnn[:, :, D:3 * D], kv_done),
                        (mix_banks[h][:, :], xt, w_mix[:, :, D:3 * D], mix_done)):
                    for k in range(KB):
                        last = nc.tensor.matmul(out_, lhs[:, h, k * P:(k + 1) * P], w[:, k, :],
                                                start=(k == 0), stop=(k == KB - 1))
                    last.then_inc(signal, 1)

            def body(r, last=False):
                for h in range(2):
                    if not (last and h):
                        turn(r, h + 1)
                    if not (isinstance(r, int) and r == 0):
                        sums(r, h - 2)
                    products(r, h)

            t.wait_ge(consts_made, 3)
            windows.tensor(t)
            t.wait_ge(w_in, 96)
            turn(0, 0)
            rounds(t, body)
            sums(PAIRS - 1, 0)
            sums(PAIRS - 1, 1)


class Mixer:

    SIGNALS = ("weights_in q_ready num_done rows_ready turned copied m_done var std "
               "h_done h_ready o_done tile_done idle first_own").split()
    STEPS = 8
    OWN = 14

    def __init__(self, nc, b, v, bank):
        self.nc, self.v = nc, v
        self.bank = bank
        self.wm, self.q = b("wm", [P, KB, D]), b("q", [P, D])
        self.w1, self.w2 = b("w1", [P, 2 * KB, 2 * D]), b("w2", [P, 2 * KB, D])
        self.gb = b("gb", [P, 4, D])
        self.heads = b("heads", [P, HB])
        self.sums = b("sums", [P, KB, ZW])
        self.z, self.rows, self.cols = b("z", [P, HEADS]), b("mix_rows", [P, D]), b("mix_cols", [P, D])
        self.h1 = b("h1", [P, 2 * D])
        self.stats, self.mv, self.rs = b("mix_stats", [P, 6]), b("mix_mv", [P, 2]), b("mix_rs", [P, 1])
        (self.weights_in, self.q_ready, self.num_done, self.rows_ready,
         self.turned, self.copied, self.m_done, self.var, self.std, self.h_done, self.h_ready, self.o_done,
         self.tile_done, self.idle, self.first_own) = v["mixer_signals"]

    def load(self, sp):
        v = self.v
        for dst, src in ((self.wm, v["wm"]), (self.w1, v["w1m"]), (self.w2, v["w2m"])):
            sp.dma_start(dst[:, :, :], src.rearrange("(k p) c -> p k c", p=P)).then_inc(self.weights_in, 16)
        sp.dma_start(self.gb[:, :, :], v["gb_mix"]).then_inc(self.weights_in, 16)
        sp.dma_start(self.heads[:, :], v["head_mask"]).then_inc(self.weights_in, 16)

    def prepare(self, d):
        kv_sum, heads, sums = self.v["kv_sum"], self.heads, self.sums
        d.wait_ge(self.weights_in, 80)
        own = Own(d, self.first_own)
        for k in range(KB):
            for c in range(HB):
                own.link(d.tensor_scalar(sums[:, k, c * HD:(c + 1) * HD], kv_sum[:, k, c * HD:(c + 1) * HD],
                                         heads[:, c:c + 1], None, ALU.mult))
            own.link(d.tensor_scalar(sums[:, k, P:ZW], heads[:, :], kv_sum[:, k, P:P + 1], None, ALU.mult))
        d.sem_inc(self.tile_done, 1)

    def block_of(self, r, k):
        return self.v["rows_all"][:, bass.ds(r, 1), k * P:(k + 1) * P].rearrange("p a c -> p (a c)")

    def tensor(self, t, r, step):
        nc, cols = self.nc, self.cols
        if step == 0:
            t.wait_ge(self.tile_done, r + 1)
            t.wait_ge(self.q_ready, r + 1)
            for k in range(KB):
                last = nc.tensor.matmul(self.bank[:, k * ZW:(k + 1) * ZW], self.q[:, k * P:(k + 1) * P],
                                        self.sums[:, k, :], start=True, stop=True)
            last.then_inc(self.num_done, 1)
        if step in (1, 4):
            t.wait_ge(self.rows_ready, r * 2 + (2 if step == 4 else 1))
            for k in range(KB):
                last = nc.tensor.transpose(self.bank[:, k * P:(k + 1) * P], self.rows[:, k * P:(k + 1) * P],
                                           self.v["ident"][:, :])
            last.then_inc(self.turned, 1)
        if step == 2:
            t.wait_ge(self.copied, r * 2 + 1)
            for k in range(KB):
                last = nc.tensor.matmul(self.bank[:, 0:D], cols[:, k * P:(k + 1) * P], self.wm[:, k, :],
                                        start=(k == 0), stop=(k == KB - 1))
            last.then_inc(self.m_done, 1)
        if step == 5:
            t.wait_ge(self.copied, r * 2 + 2)
            for m in range(2 * KB):
                for k in range(2 * KB):
                    rhs = self.block_of(r, k) if k < KB else cols[:, (k - KB) * P:(k - KB + 1) * P]
                    last = nc.tensor.matmul(self.bank[:, m * P:(m + 1) * P], self.w1[:, k, m * P:(m + 1) * P],
                                            rhs, start=(k == 0), stop=(k == 2 * KB - 1))
            last.then_inc(self.h_done, 1)
        if step == 6:
            t.wait_ge(self.h_ready, r + 1)
            for k in range(2 * KB):
                last = nc.tensor.matmul(self.bank[:, 0:D], self.h1[:, k * P:(k + 1) * P], self.w2[:, k, :],
                                        start=(k == 0), stop=(k == 2 * KB - 1))
            last.then_inc(self.o_done, 1)

    def fetch(self, a, tile):
        a.activation(self.q[:, :], tile_of(self.v["mix_q"], tile), ACT.Copy).then_inc(self.q_ready, 1)

    def scalar(self, a, r, step):
        if step == 5:
            a.wait_ge(self.num_done, r + 1)
            self.fetch(a, r + 1)
        if step in (1, 4):
            a.wait_ge(self.turned, r * 2 + (2 if step == 4 else 1))
            a.activation(self.cols[:, :], self.bank[:, 0:D], ACT.Copy).then_inc(self.copied, 1)
        if step in (2, 6):
            a.wait_ge(self.var, r * 2 + (2 if step == 6 else 1))
            a.activation(self.rs[:, :], self.rs[:, :], ACT.Sqrt).then_inc(self.std, 1)
        if step == 5:
            a.wait_ge(self.h_done, r + 1)
            a.activation(self.h1[:, :], self.bank[:, :], ACT.Relu).then_inc(self.h_ready, 1)

    def vector(self, d, r, step, own):
        bank, rows, rs, mv = self.bank, self.rows, self.rs, self.mv
        if step == 0:
            d.wait_ge(self.num_done, r + 1)
            num = self.bank[:, 0:KB * ZW].rearrange("p (k c) -> p k c", k=KB)
            own.link(d.tensor_scalar(self.z[:, :].rearrange("p (k c) -> p k c", k=KB), num[:, :, P:ZW],
                                     ATT_EPS, None, ALU.add))
            own.link(d.reciprocal(self.z[:, :], self.z[:, :]))
            own.link(d.tensor_scalar(self.z[:, :], self.z[:, :], float(NODES), None, ALU.mult))
            for k in range(KB):
                last = d.tensor_tensor(rows[:, k * P:(k + 1) * P].rearrange("p (c e) -> p c e", e=HD),
                                       num[:, k, 0:P].rearrange("p (c e) -> p c e", e=HD),
                                       self.z[:, k * HB:(k + 1) * HB].unsqueeze(2).to_broadcast([P, HB, HD]), ALU.mult)
            last.then_inc(self.rows_ready, 1)
        if step in (2, 6):
            if step == 2:
                d.wait_ge(self.m_done, r + 1)
            else:
                d.wait_ge(self.o_done, r + 1)
            own.link(d.bn_stats(self.stats[:, :], bank[:, 0:D]))
            own.rest(self.idle)
            own.link(d.bn_aggr(mv[:, :], self.stats[:, :]))
            d.tensor_scalar(rs[:, :], mv[:, 1:2], LN_EPS, None, ALU.add).then_inc(self.var, 1)
        if step in (3, 7):
            g = 0 if step == 3 else 2
            d.wait_ge(self.std, r * 2 + (2 if step == 7 else 1))
            own.link(d.reciprocal(rs[:, :], rs[:, :]))
            own.link(d.tensor_scalar(rows[:, :], bank[:, 0:D], mv[:, 0:1], rs[:, :], ALU.subtract, ALU.mult))
            own.link(d.tensor_tensor(rows[:, :], rows[:, :], self.gb[:, g, :], ALU.mult))
            if step == 3:
                d.tensor_tensor(rows[:, :], rows[:, :], self.gb[:, g + 1, :], ALU.add).then_inc(self.rows_ready, 1)
            else:
                own.link(d.tensor_tensor(rows[:, :], rows[:, :], self.gb[:, g + 1, :], ALU.add))
                res = tile_of(self.v["x_all"], r)
                d.tensor_tensor(res, res, rows[:, :], ALU.add).then_inc(self.tile_done, 1)


def build_mixer(nc, sem, sb, banks, v):
    ctx = ExitStack()
    with ctx:
        mixer = Mixer(nc, lambda n, shape: sb("m_" + n, shape, fp32, ctx), v,
                      banks[0])
        d_own = sem("m_own", ctx)
        block = ctx.enter_context(nc.Block())

        @block.sync
        def _(sp):
            with sp.If(sp.value_load(v["far_flag"][0:1, 0:1], min_val=0, max_val=1)):
                mixer.load(sp)

        @block.tensor
        def _(t):
            with t.If(t.value_load(v["far_flag"][0:1, 0:1], min_val=0, max_val=1)):
                t.wait_ge(mixer.weights_in, 80)
                with t.Fori(0, TILES) as r:
                    for step in range(Mixer.STEPS):
                        mixer.tensor(t, r, step)

        @block.scalar
        def _(a):
            with a.If(a.value_load(v["far_flag"][0:1, 0:1], min_val=0, max_val=1)):
                mixer.fetch(a, 0)
                with a.Fori(0, TILES) as r:
                    for step in range(Mixer.STEPS):
                        mixer.scalar(a, r, step)

        @block.vector
        def _(d):
            with d.If(d.value_load(v["far_flag"][0:1, 0:1], min_val=0, max_val=1)):
                mixer.prepare(d)
                with d.Fori(0, TILES) as r:
                    own = Own(d, d_own, 0, Mixer.OWN, r)
                    for step in range(Mixer.STEPS):
                        mixer.vector(d, r, step, own)
                    own.closed()


def build_near_edges(nc, sem, sb, banks, v):
    kv_table, parts_table, acc, base_i, base_all = (v[k] for k in ("kv_table", "parts_table", "acc", "base_i", "base_all"))
    ALLC = (ROUNDS + 1) * CH
    PROJ_BANKS = (0, 1, 6, 7)
    PARTS = 3
    ctx = ExitStack()
    with ctx:
        def s(name): return sem("f_" + name, ctx)

        def b(name, shape, dt=fp32): return sb("f_" + name, shape, dt, ctx)

        w = b("w", [KE, 2 * D])
        idx = b("idx", [P, 2, HALF], i32)
        attr = b("attr", [KE, 2, HALF * P])
        row = b("row", [P, 2, HALF * P], i32)
        window = b("window", [P, 2, PARTS, D], bf16)
        weight = b("weight", [P, ALLC])
        cut, near, rel = b("cut", [P, ALLC]), b("near", [P, ALLC]), b("rel", [P, ALLC])
        dst_i = b("dst_i", [P, ALLC], i32)
        lane, half_pi, lane_at = b("lane", [P, 1]), b("half_pi", [P, 1]), b("lane_at", [P, GROUPS])
        count = b("count", [P, P])
        kv, dkv, msg = b("kv", [P, SLOTS, 2 * D]), b("dkv", [P, SLOTS, 2 * D]), b("msg", [P, SLOTS, D])
        pick = b("pick", [P, 2, QUAD * P], bf16)
        give = b("give", [P, SLOTS, P])
        prod, total = b("prod", [P, QUAD, D]), b("total", [P, 2, D])
        score, gate = b("score", [P, 2, QUAD]), b("gate", [P, 2, QUAD])

        once, half_in, window_in = s("once"), [s("half_in0"), s("half_in1")], [s("window_in0"), s("window_in1")]
        rows_in = [s(f"rows_in{k}") for k in range(SLOTS)]
        added = [s(f"added{k}") for k in range(NACC)]
        (proj_done, silu_done, msg_done, q_done, prod_done, sum_done, total_ready, pick_ready, score_ready,
         gate_ready, d_own, clamped, sine, tick, made, zero_made) = (
            s(n) for n in ("proj_done silu_done msg_done q_done prod_done sum_done total_ready pick_ready score_ready "
                           "gate_ready d_own clamped sine tick made zero_made").split())
        mixer = Mixer(nc, b, v, banks[5])
        block = ctx.enter_context(nc.Block())

        SILU0, MSG0, Q0, PROD0, SUM0, TOT0 = 4, SLOTS, 2 * QUAD, QUAD // 2, 2, 2

        @block.sync
        def _(sp):
            def load(i, half):
                at, one_ = half * HALF, bass.ds(i, 1)
                sp.dma_start(idx[:, half, :], v["src"][one_, :, at:at + HALF].rearrange("a p c -> (a p) c"))\
                  .then_inc(half_in[half], 16)
                sp.dma_start(attr[:, half, :], v["attr"][:, one_, at * P:(at + HALF) * P]
                             .rearrange("k a c -> k (a c)")).then_inc(half_in[half], 16)
                sp.dma_start(row[:, half, :], v["dst_row"][one_, at * P:(at + HALF) * P].to_broadcast([P, HALF * P]))\
                  .then_inc(half_in[half], 16)

            def load_window(group, par):
                first = sp.value_load(base_i[0:1, bass.ds(group, 1)], min_val=0, max_val=ROWS - P)
                sp.dma_start(window[:, par, :, :], parts_table[bass.ds(first, P), :].rearrange("p (a c) -> p a c", a=PARTS))\
                  .then_inc(window_in[par], 16)

            with sp.If(sp.value_load(v["near_flag"][0:1, 0:1], min_val=0, max_val=1)):
                load(0, 0)
                sp.dma_start(w[:, :], v["w_edge"]).then_inc(once, 16)
                for dst_, src_ in ((dst_i, v["dst"]), (weight, v["weight"])):
                    sp.dma_start(dst_[:, :].rearrange("p (i c) -> p i c", c=CH), src_.rearrange("i p c -> p i c")).then_inc(once, 16)
                load_window(0, 0)
                load_window(1, 1)
                load(0, 1)
                mixer.load(sp)
                with sp.Fori(0, ROUNDS) as r:
                    for quad in range(QUADS):
                        sp.wait_ge(q_done, r * CH + ((quad + 1) * QUAD + Q0))
                        load_window(r * QUADS + (quad + 2), quad % 2)
                        if quad % 2:
                            sp.wait_ge(msg_done, r * CH + ((quad + 1) * QUAD + MSG0))
                            load(r + 1, quad // 2)
                for half in range(2):
                    sp.wait_ge(half_in[half], 48 * (ROUNDS + 1))
                    sp.wait_ge(window_in[half], 32 * ROUNDS + 16)

        @block.gpsimd
        def _(g):
            def gather(quad, j):
                slot = (quad % 2) * QUAD + j
                g.indirect_dma_start(kv[:, slot, :], None, kv_table,
                                     bass.IndirectOffsetOnAxis(ap=idx[:, (quad // 2) % 2, slot:slot + 1], axis=0))\
                 .then_inc(rows_in[slot], 16)

            with g.If(g.value_load(v["near_flag"][0:1, 0:1], min_val=0, max_val=1)):
                g.iota(lane[:, :], [[1, 1]], base=0, channel_multiplier=1,
                       allow_small_or_imprecise_dtypes=True).then_inc(made, 1)
                g.iota(count[:, :], [[1, P]], base=0, channel_multiplier=0,
                       allow_small_or_imprecise_dtypes=True).then_inc(made, 1)
                g.wait_ge(zero_made, 1)
                for k in range(NACC):
                    g.dma_start(acc[k][0:P, :], total[:, k, :], accum_op=ALU.add).then_inc(added[k], 16)
                g.wait_ge(half_in[0], 48)
                for quad in range(2):
                    for j in range(QUAD):
                        gather(quad, j)
                with g.Fori(0, ROUNDS) as r:
                    for quad in range(QUADS):
                        if quad % 2 == 0:
                            g.wait_ge(half_in[1 - quad // 2], r * 48 + 48 * (1 + quad // 2))
                            g.sem_inc(tick, 1)
                        for j in range(QUAD):
                            g.wait_ge(msg_done, r * CH + (quad * QUAD + j + 1 + MSG0))
                            g.sem_inc(tick, 1)
                            gather(quad + 2, j)
                        g.wait_ge(total_ready, r * QUADS + (quad + 1 + TOT0))
                        first = g.value_load(base_i[0:1, bass.ds(r * QUADS + quad, 1)], min_val=0, max_val=ROWS - P)
                        g.sem_inc(tick, 1)
                        g.dma_start(acc[quad % 2][bass.ds(first, P), :], total[:, quad % 2, :], accum_op=ALU.add)\
                         .then_inc(added[quad % 2], 16)
                for k in range(NACC):
                    g.wait_ge(added[k], 16 + 16 * ROUNDS * QUADS // NACC)
                for k in range(SLOTS):
                    g.wait_ge(rows_in[k], 16 * (2 * ROUNDS + 1))

        @block.tensor
        def _(t):
            def project(r, quad):
                if quad % 2 == 0:
                    t.wait_ge(half_in[(quad // 2) % 2], r * 48 + 48 * (1 + quad // QUADS))
                for j in range(QUAD):
                    n = quad * QUAD + j
                    at = (n % HALF) * P
                    t.wait_ge(silu_done, r * CH + (n + 1))
                    nc.tensor.matmul(banks[PROJ_BANKS[n % 4]][:, :], attr[:, (n // HALF) % 2, at:at + P], w[:, :],
                                     start=True, stop=True).then_inc(proj_done, 1)

            def queries(r, quad):
                t.wait_ge(pick_ready, r * QUADS + (quad + 1))
                t.wait_ge(window_in[quad % 2], r * 32 + 16 * (1 + quad // 2))
                for j in range(QUAD):
                    if j % 2 == 0:
                        t.wait_ge(prod_done, r * (CH // 2) + (quad * QUAD + j) // 2 + 1)
                    for part in range(PARTS):
                        last = nc.tensor.matmul(banks[2 + j // 2][:, (j % 2) * D:(j % 2 + 1) * D], pick[:, quad % 2, j * P:(j + 1) * P],
                                                window[:, quad % 2, part, :], start=(part == 0), stop=(part == PARTS - 1))
                    last.then_inc(q_done, 1)

            with t.If(t.value_load(v["near_flag"][0:1, 0:1], min_val=0, max_val=1)):
                t.wait_ge(once, 48)
                project(0, 0)
                queries(0, 0)
                t.wait_ge(mixer.weights_in, 80)
                with t.Fori(0, ROUNDS) as r:
                    for quad in range(QUADS):
                        project(r, quad + 1)
                        queries(r, quad + 1)
                        mixer.tensor(t, r, 2 * quad)
                        t.wait_ge(total_ready, r * QUADS + (quad + 1 + TOT0 - 1))
                        for j in range(QUAD):
                            n = quad * QUAD + j
                            t.wait_ge(msg_done, r * CH + (n + 1 + MSG0))
                            last = nc.tensor.matmul(banks[4][:, 0:D], give[:, n % SLOTS, :], msg[:, n % SLOTS, :],
                                                    start=(j == 0), stop=(j == QUAD - 1))
                        last.then_inc(sum_done, 1)
                        mixer.tensor(t, r, 2 * quad + 1)

        @block.scalar
        def _(a):
            def silus(r, quad):
                for j in range(QUAD):
                    n = quad * QUAD + j
                    a.wait_ge(proj_done, r * CH + (n + 1))
                    a.wait_ge(msg_done, r * CH + (n + 1))
                    a.activation(dkv[:, n % SLOTS, :], banks[PROJ_BANKS[n % 4]][:, :], ACT.Silu).then_inc(silu_done, 1)

            with a.If(a.value_load(v["near_flag"][0:1, 0:1], min_val=0, max_val=1)):
                a.sem_inc(silu_done, SILU0)
                a.sem_inc(total_ready, TOT0)
                a.wait_ge(clamped, 2)
                a.activation(cut[:, :], cut[:, :], ACT.Sin, bias=half_pi[:, 0:1], scale=-math.pi / CUTOFF).then_inc(sine, 1)
                mixer.fetch(a, 0)
                silus(0, 0)
                with a.Fori(0, ROUNDS) as r:
                    for quad in range(QUADS):
                        a.wait_ge(score_ready, r * QUADS + (quad + 1))
                        a.activation(gate[:, quad % 2, :], score[:, quad % 2, :], ACT.Silu).then_inc(gate_ready, 1)
                        silus(r, quad + 1)
                        mixer.scalar(a, r, 2 * quad)
                        a.wait_ge(sum_done, r * QUADS + (quad + 1 + SUM0))
                        a.wait_ge(added[quad % 2], r * 32 + 16 * (quad // 2 + 1))
                        a.activation(total[:, quad % 2, :], banks[4][:, 0:D], ACT.Copy).then_inc(total_ready, 1)
                        mixer.scalar(a, r, 2 * quad + 1)

        @block.vector
        def _(d):
            def picks(r, quad):
                if quad % 2 == 0:
                    d.wait_ge(half_in[(quad // 2) % 2], r * 48 + 48 * (1 + quad // QUADS))
                d.wait_ge(q_done, r * CH + (quad + 1) * QUAD)
                at = (quad % 2) * QUAD * P
                d.tensor_scalar(pick[:, quad % 2, :], row[:, (quad // 2) % 2, at:at + QUAD * P],
                                lane_at[:, bass.ds(r * QUADS + quad, 1)], None, ALU.is_equal).then_inc(pick_ready, 1)

            def scores(r, quad):
                for pair in range(QUAD // 2 + 1):
                    n = quad * QUAD + 2 * pair
                    slot = n % SLOTS
                    if pair < QUAD // 2:
                        for k in range(2):
                            d.wait_ge(rows_in[slot + k], r * 32 + 16 * (1 + n // SLOTS))
                        d.wait_ge(q_done, r * CH + (n + 2 + Q0))
                        d.tensor_tensor(prod[:, 2 * pair:2 * pair + 2, :], banks[2 + pair][:, :].rearrange("p (a c) -> p a c", a=2),
                                        kv[:, slot:slot + 2, 0:D], ALU.mult).then_inc(prod_done, 1)
                    if pair:
                        d.wait_ge(prod_done, r * (CH // 2) + (n // 2 + PROD0))
                        d.wait_ge(silu_done, r * CH + (n + SILU0))
                        for j in (2 * pair - 2, 2 * pair - 1):
                            last = d.tensor_tensor_reduce(out=prod[:, j, :], in0=prod[:, j, :],
                                                          in1=dkv[:, (quad * QUAD + j) % SLOTS, 0:D], scale=1.0, scalar=0.0,
                                                          op0=ALU.mult, op1=ALU.add, accum_out=score[:, quad % 2, j:j + 1])
                last.then_inc(score_ready, 1)

            with d.If(d.value_load(v["near_flag"][0:1, 0:1], min_val=0, max_val=1)):
                d.memset(total[:, :, :], 0.0).then_inc(zero_made, 1)
                d.sem_inc(msg_done, MSG0)
                d.sem_inc(q_done, Q0)
                d.sem_inc(prod_done, PROD0)
                d.sem_inc(sum_done, SUM0)
                first = Own(d, d_own)
                d.memset(half_pi[:, :], math.pi / 2).then_inc(clamped, 1)
                d.wait_ge(once, 48)
                d.wait_ge(made, 2)
                d.tensor_scalar(cut[:, :], weight[:, :], CUTOFF, None, ALU.min).then_inc(clamped, 1)
                first.link(d.tensor_tensor(rel[:, :].rearrange("p (g c) -> p g c", c=QUAD),
                                           dst_i[:, :].rearrange("p (g c) -> p g c", c=QUAD),
                                           base_all[:, :].unsqueeze(2).to_broadcast([P, GROUPS, QUAD]), ALU.subtract))
                first.link(d.tensor_scalar(lane_at[:, :], base_all[:, :], lane[:, 0:1], None, ALU.add))
                first.link(d.tensor_scalar(near[:, :], weight[:, :], CUTOFF, None, ALU.is_lt))
                d.wait_ge(sine, 1)
                first.link(d.tensor_scalar(cut[:, :], cut[:, :], 0.5, 0.5, ALU.mult, ALU.add))
                first.link(d.tensor_tensor(cut[:, :], cut[:, :], near[:, :], ALU.mult))
                picks(0, 0)
                scores(0, 0)
                picks(0, 1)
                mixer.prepare(d)
                with d.Fori(0, ROUNDS) as r:
                    own = Own(d, d_own, 5, QUADS + Mixer.OWN, r)
                    for quad in range(QUADS):
                        par = quad % 2
                        d.wait_ge(gate_ready, r * QUADS + (quad + 1))
                        own.link(d.tensor_tensor(gate[:, par, :], gate[:, par, :],
                                                 cut[:, bass.ds(r * CH + quad * QUAD, QUAD)], ALU.mult))
                        d.wait_ge(sum_done, r * QUADS + (quad + 1))
                        for j in range(QUAD):
                            slot = (quad * QUAD + j) % SLOTS
                            d.tensor_scalar(give[:, slot, :], count[:, :], rel[:, bass.ds(r * CH + (quad * QUAD + j), 1)],
                                            gate[:, par, j:j + 1], ALU.is_equal, ALU.mult)
                            d.tensor_tensor(msg[:, slot, :], kv[:, slot, D:2 * D], dkv[:, slot, D:2 * D], ALU.mult)\
                             .then_inc(msg_done, 1)
                        if quad % 2 == 0:
                            mixer.vector(d, r, 2 * quad, own)
                            scores(r, quad + 1)
                        else:
                            scores(r, quad + 1)
                            mixer.vector(d, r, 2 * quad, own)
                        picks(r, quad + 2)
                        mixer.vector(d, r, 2 * quad + 1, own)
                    own.closed()


def build_edges(nc, sem, sb, banks, v):
    q_table, kv_table, acc, before = v["q_table"], v["kv_table"], v["acc"], v["before"]
    ALLC = (ROUNDS + 1) * CH
    ctx = ExitStack()
    with ctx:
        def s(name): return sem("e_" + name, ctx)

        def b(name, shape, dt=fp32): return sb("e_" + name, shape, dt, ctx)

        w = b("w", [KE, 2 * D])
        idx = b("idx", [P, 2, 2, HALF], i32)
        attr = b("attr", [KE, 2, HALF * P])
        row = b("row", [P, 2, HALF * P], i32)
        dst_i, dst_f, weight = b("dst_i", [P, ALLC], i32), b("dst_f", [P, ALLC]), b("weight", [P, ALLC])
        spare, cut, near = b("spare", [P, ALLC]), b("cut", [P, ALLC]), b("near", [P, ALLC])
        lane, half_pi = b("lane", [P, 1]), b("half_pi", [P, 1])
        kv, q, dkv = b("kv", [P, SLOTS, 2 * D]), b("q", [P, SLOTS, D]), b("dkv", [P, SLOTS, 2 * D])
        msg, total = b("msg", [P, SLOTS, D]), b("total", [P, SLOTS, D])
        same = b("same", [P, SLOTS, P])
        prod, earlier = b("prod", [P, 2, D]), b("earlier", [P, 2, P])
        score, gate, cnt = b("score", [P, 2, QUAD]), b("gate", [P, 2, QUAD]), b("cnt", [P, 2, QUAD])
        away, target = b("away", [P, 2, QUAD]), b("target", [P, 2, QUAD], i32)
        dq = b("dq", [P, 2, QUAD])

        once, half_in = s("once"), [s("half_in0"), s("half_in1")]
        rows_in = [s(f"rows_in{k}") for k in range(SLOTS)]
        scattered = [s(f"scattered{k}") for k in range(NACC)]
        proj_done, silu_done, msg_done, sum_done, total_ready, total_free = (
            s(n) for n in "proj_done silu_done msg_done sum_done total_ready total_free".split())
        score_ready, gate_ready, d_own, clamped, sine, tick, lane_made, zero_made, score_parts = (
            s(n) for n in "score_ready gate_ready d_own clamped sine tick lane_made zero_made score_parts".split())
        block = ctx.enter_context(nc.Block())

        MSG0, SILU0, TOT0, SUM0, FREE0 = SLOTS, 2, 2, SLOTS, SLOTS - NACC

        @block.sync
        def _(sp):
            with sp.If(sp.value_load(v["far_flag"][0:1, 0:1], min_val=0, max_val=1)):
                def load(i, half):
                    one_ = bass.ds(i, 1)
                    at = half * HALF
                    sp.dma_start(idx[:, half, 0, :], v["src"][one_, :, at:at + HALF].rearrange("a p c -> (a p) c"))\
                      .then_inc(half_in[half], 16)
                    sp.dma_start(attr[:, half, :], v["attr"][:, one_, at * P:(at + HALF) * P]
                                 .rearrange("k a c -> k (a c)"))\
                      .then_inc(half_in[half], 16)
                    sp.dma_start(idx[:, half, 1, :], v["dst"][one_, :, at:at + HALF].rearrange("a p c -> (a p) c"))\
                      .then_inc(half_in[half], 16)
                    sp.dma_start(row[:, half, :],
                                 v["dst_row"][one_, at * P:(at + HALF) * P].to_broadcast([P, HALF * P]))\
                      .then_inc(half_in[half], 16)

                for half in range(2):
                    load(0, half)
                sp.dma_start(w[:, :], v["w_edge"]).then_inc(once, 16)
                sp.dma_start(dst_i[:, :].rearrange("p (i c) -> p i c", c=CH), v["dst"].rearrange("i p c -> p i c")).then_inc(once, 16)
                sp.dma_start(weight[:, :].rearrange("p (i c) -> p i c", c=CH), v["weight"].rearrange("i p c -> p i c")).then_inc(once, 16)
                with sp.Fori(0, ROUNDS) as r:
                    for half in range(2):
                        sp.wait_ge(msg_done, r * CH + ((half + 1) * HALF + MSG0))
                        load(r + 1, half)
                for half in range(2):
                    sp.wait_ge(half_in[half], 64 * (ROUNDS + 1))

        @block.gpsimd
        def _(g):
            with g.If(g.value_load(v["far_flag"][0:1, 0:1], min_val=0, max_val=1)):
                g.iota(lane[:, :], [[1, 1]], base=ROWS, channel_multiplier=1,
                       allow_small_or_imprecise_dtypes=True).then_inc(lane_made, 1)
                g.sem_inc(total_free, FREE0)

                def gather(quad, j):
                    slot = (quad % 2) * QUAD + j
                    half, at = (quad // 2) % 2, (quad % 2) * QUAD + j
                    g.indirect_dma_start(kv[:, slot, :], None, kv_table,
                                         bass.IndirectOffsetOnAxis(ap=idx[:, half, 0, at:at + 1], axis=0))\
                     .then_inc(rows_in[slot], 16)
                    g.indirect_dma_start(q[:, slot, :], None, q_table,
                                         bass.IndirectOffsetOnAxis(ap=idx[:, half, 1, at:at + 1], axis=0))\
                     .then_inc(rows_in[slot], 16)

                g.wait_ge(zero_made, 1)
                for k in range(NACC):
                    g.dma_start(acc[k][0:P, :], total[:, k, :], accum_op=ALU.add).then_inc(scattered[k], 16)
                g.wait_ge(half_in[0], 64)
                for quad in range(2):
                    for j in range(QUAD):
                        gather(quad, j)
                with g.Fori(0, ROUNDS) as r:
                    for quad in range(QUADS):
                        if quad == 0:
                            g.wait_ge(half_in[1], r * 64 + 64)
                            g.sem_inc(tick, 1)
                        if quad == 2:
                            g.wait_ge(half_in[0], r * 64 + 128)
                            g.sem_inc(tick, 1)
                        for j in range(QUAD):
                            n = quad * QUAD + j
                            g.wait_ge(msg_done, r * CH + (n + 1 + MSG0))
                            g.sem_inc(tick, 1)
                            gather(quad + 2, j)
                            g.wait_ge(total_ready, r * CH + (n + 1 + TOT0))
                            g.wait_ge(scattered[j % NACC], r * (16 * CH // NACC) + 16 * (n // NACC + 1))
                            g.sem_inc(total_free, 1)
                            slot = (quad % 2) * QUAD + j
                            g.indirect_dma_start(acc[j % NACC], bass.IndirectOffsetOnAxis(
                                ap=target[:, quad % 2, j:j + 1], axis=0), total[:, slot, :], None, compute_op=ALU.add)\
                             .then_inc(scattered[j % NACC], 16)
                for k in range(NACC):
                    g.wait_ge(scattered[k], 16 + 16 * ROUNDS * CH // NACC)
                for k in range(SLOTS):
                    g.wait_ge(rows_in[k], 32 * (2 * ROUNDS + 1))

        @block.tensor
        def _(t):
            with t.If(t.value_load(v["far_flag"][0:1, 0:1], min_val=0, max_val=1)):
                def project(r, n):
                    half = (n // HALF) % 2
                    if n % HALF == 0:
                        t.wait_ge(half_in[half], r * 64 + 64 * (1 + n // CH))
                    t.wait_ge(silu_done, r * CH + (n + 1))
                    at = (n % HALF) * P
                    nc.tensor.matmul(banks[n % 2][:, :], attr[:, half, at:at + P], w[:, :], start=True, stop=True)\
                     .then_inc(proj_done, 1)

                t.wait_ge(once, 48)
                for n in range(QUAD):
                    project(0, n)
                with t.Fori(0, ROUNDS) as r:
                    for quad in range(QUADS):
                        for j in range(QUAD):
                            project(r, (quad + 1) * QUAD + j)
                        for j in range(QUAD):
                            n = quad * QUAD + j
                            t.wait_ge(msg_done, r * CH + (n + 1 + MSG0))
                            t.wait_ge(total_ready, r * CH + (n + 1))
                            nc.tensor.matmul(banks[2 + n % 2][:, 0:D], same[:, n % SLOTS, :], msg[:, n % SLOTS, :],
                                             start=True, stop=True).then_inc(sum_done, 1)

        @block.scalar
        def _(a):
            with a.If(a.value_load(v["far_flag"][0:1, 0:1], min_val=0, max_val=1)):
                def silus(r, quad):
                    for j in range(QUAD):
                        n = quad * QUAD + j
                        a.wait_ge(proj_done, r * CH + (n + 1))
                        a.wait_ge(msg_done, r * CH + (n + 1))
                        a.activation(dkv[:, n % SLOTS, :], banks[n % 2][:, :], ACT.Silu).then_inc(silu_done, 1)

                a.sem_inc(silu_done, SILU0)
                a.sem_inc(total_ready, TOT0)
                a.wait_ge(clamped, 2)
                a.activation(cut[:, :], cut[:, :], ACT.Sin, bias=half_pi[:, 0:1], scale=-math.pi / CUTOFF).then_inc(sine, 1)
                silus(0, 0)
                with a.Fori(0, ROUNDS) as r:
                    for quad in range(QUADS):
                        a.wait_ge(score_ready, r * QUADS + (quad + 1))
                        a.activation(gate[:, quad % 2, :], score[:, quad % 2, :], ACT.Silu).then_inc(gate_ready, 1)
                        silus(r, quad + 1)
                        for j in range(QUAD):
                            n = quad * QUAD + j
                            a.wait_ge(sum_done, r * CH + (n + 1 + SUM0))
                            a.wait_ge(total_free, r * CH + (n + 1))
                            a.activation(total[:, n % SLOTS, :], banks[2 + n % 2][:, 0:D], ACT.Copy).then_inc(total_ready, 1)

        @block.vector
        def _(d):
            with d.If(d.value_load(v["far_flag"][0:1, 0:1], min_val=0, max_val=1)):
                d.memset(total[:, 0:NACC, :], 0.0).then_inc(zero_made, 1)
                d.sem_inc(msg_done, MSG0)
                d.sem_inc(sum_done, SUM0)
                first = Own(d, d_own)
                d.memset(half_pi[:, :], math.pi / 2).then_inc(clamped, 1)
                d.wait_ge(once, 48)
                d.wait_ge(lane_made, 1)
                d.tensor_scalar(cut[:, :], weight[:, :], CUTOFF, None, ALU.min).then_inc(clamped, 1)
                first.link(d.tensor_copy(dst_f[:, :], dst_i[:, :]))
                first.link(d.tensor_scalar(spare[:, :], dst_f[:, :], -1.0, lane[:, 0:1], ALU.mult, ALU.add))
                first.link(d.tensor_scalar(near[:, :], weight[:, :], CUTOFF, None, ALU.is_lt))
                d.wait_ge(sine, 1)
                first.link(d.tensor_scalar(cut[:, :], cut[:, :], 0.5, 0.5, ALU.mult, ALU.add))
                first.link(d.tensor_tensor(cut[:, :], cut[:, :], near[:, :], ALU.mult))

                def front(r, quad, own):
                    par = quad % 2
                    chunks = bass.ds(r * CH + quad * QUAD, QUAD)
                    if quad % 2 == 0:
                        d.wait_ge(half_in[(quad // 2) % 2], r * 64 + 64 * (1 + quad // QUADS))
                    d.wait_ge(total_free, r * CH + (quad + 1) * QUAD)
                    own.link(d.tensor_copy(dq[:, par, :], dst_f[:, chunks]))
                    for j in range(QUAD):
                        n = quad * QUAD + j
                        slot = n % SLOTS
                        d.wait_ge(rows_in[slot], r * 64 + 32 * (1 + n // SLOTS))
                        d.wait_ge(silu_done, r * CH + (n + 1 + SILU0))
                        own.link(d.tensor_tensor(prod[:, j % 2, :], q[:, slot, :], kv[:, slot, 0:D], ALU.mult))
                        d.tensor_tensor_reduce(out=prod[:, j % 2, :], in0=prod[:, j % 2, :], in1=dkv[:, slot, 0:D],
                                               scale=1.0, scalar=0.0, op0=ALU.mult, op1=ALU.add,
                                               accum_out=score[:, par, j:j + 1]).then_inc(score_parts, 1)
                        d.wait_ge(sum_done, r * CH + (n + 1))
                        own.link(d.tensor_scalar(same[:, slot, :], row[:, (n // HALF) % 2, (n % HALF) * P:(n % HALF + 1) * P],
                                                 dq[:, par, j:j + 1], None, ALU.is_equal))
                        own.link(d.tensor_tensor_reduce(out=earlier[:, j % 2, :], in0=same[:, slot, :], in1=before[:, :],
                                                        scale=1.0, scalar=0.0, op0=ALU.mult, op1=ALU.add,
                                                        accum_out=cnt[:, par, j:j + 1]))
                    own.link(d.tensor_scalar(cnt[:, par, :], cnt[:, par, :], 0.0, None, ALU.is_gt))
                    own.link(d.tensor_tensor(away[:, par, :], cnt[:, par, :], spare[:, chunks], ALU.mult))
                    d.tensor_tensor(target[:, par, :], away[:, par, :], dq[:, par, :], ALU.add).then_inc(score_ready, 1)

                FRONT = 1 + 3 * QUAD + 2
                opening = Own(d, d_own, 5)
                front(0, 0, opening)
                with d.Fori(0, ROUNDS) as r:
                    own = Own(d, d_own, 5 + FRONT, QUADS * (FRONT + 1), r)
                    for quad in range(QUADS):
                        par = quad % 2
                        d.wait_ge(gate_ready, r * QUADS + (quad + 1))
                        own.link(d.tensor_tensor(gate[:, par, :], gate[:, par, :],
                                                 cut[:, bass.ds(r * CH + quad * QUAD, QUAD)], ALU.mult))
                        for j in range(QUAD):
                            slot = (quad * QUAD + j) % SLOTS
                            d.scalar_tensor_tensor(out=msg[:, slot, :], in0=kv[:, slot, D:2 * D], scalar=gate[:, par, j:j + 1],
                                                   in1=dkv[:, slot, D:2 * D], op0=ALU.mult, op1=ALU.mult).then_inc(msg_done, 1)
                        front(r, quad + 1, own)
                    own.closed()


def build_routing(nc, sem, sb, banks, v):
    x_all, rows_all, ident, acc, logits = v["x_all"], v["rows_all"], v["ident"], v["acc"], v["logits"]
    a_banks, o_banks, h_banks, l_banks = banks[0:2], banks[2:4], banks[4:6], banks[6:8]
    ctx = ExitStack()
    with ctx:
        def s(name): return sem("r_" + name, ctx)

        def b(name, shape, dt=fp32): return sb("r_" + name, shape, dt, ctx)

        wo, gw = b("wo", [P, KB, D]), b("gw", [P, KB, EXPERTS])
        gbias = b("gbias", [P, EXPERTS])
        part, at_ = b("part", [P, 2, NACC, D]), b("at", [P, 2, D])
        hn, ht = b("hn", [P, 2, D]), b("ht", [P, 2, D])
        stats, mv, rs = b("stats", [P, 2, 6]), b("mv", [P, 2, 2]), b("rs", [P, 2])
        w_in, part_in = s("w_in"), [s("part_in0"), s("part_in1")]
        (d_own, e_own, a_turned, a_copied, o_done, var, std, h_ready, h_turned, h_copied, rows_kept,
         l_done, l_added, idle) = (s(n) for n in ("d_own e_own a_turned a_copied o_done var std h_ready "
                                                  "h_turned h_copied rows_kept l_done l_added idle").split())
        block = ctx.enter_context(nc.Block())
        TURN0, KEPT0, ADDED0 = 2, 2, 3

        def rounds(eng, body):
            body(0, first=True)
            with eng.Fori(1, PAIRS - 1) as r:
                body(r)
            body(PAIRS - 1, last=True)

        @block.sync
        def _(sp):
            sp.dma_start(wo[:, :, :], v["wo"].rearrange("(k p) c -> p k c", p=P)).then_inc(w_in, 16)
            sp.dma_start(gw[:, :, :], v["gate_w"].rearrange("(k p) c -> p k c", p=P)).then_inc(w_in, 16)
            sp.dma_start(gbias[:, :], v["gate_b"]).then_inc(w_in, 16)
            with sp.Fori(0, PAIRS) as r:
                for h in range(2):
                    sp.wait_ge(a_turned, r * 2 + (h + 1))
                    for k in range(NACC):
                        sp.dma_start(part[:, h, k, :], rows_of(acc[k][0:ROWS, :], r * 2 + h)).then_inc(part_in[h], 16)

        @block.vector
        def _(d):
            def add(r, c):
                h = c % 2
                own = Own(d, d_own, 3 * c, 6, r)
                res = tile_of(x_all, r * 2 + c)
                d.wait_ge(o_done, r * 2 + (c + 1))
                own.link(d.tensor_tensor(res, res, o_banks[h][:, 0:D], ALU.add))
                own.rest(idle)
                own.link(d.bn_stats(stats[:, h, :], res))
                own.rest(idle)
                own.link(d.bn_aggr(mv[:, h, :], stats[:, h, :]))
                d.tensor_scalar(rs[:, h:h + 1], mv[:, h, 1:2], LN_EPS, None, ALU.add).then_inc(var, 1)

            def norm(r, c):
                h = c % 2
                own = Own(d, e_own, c, 2, r)
                d.wait_ge(std, r * 2 + (c + 1))
                own.link(d.reciprocal(rs[:, h:h + 1], rs[:, h:h + 1]))
                if not (isinstance(r, int) and r * 2 + c + 1 == 0):
                    d.wait_ge(rows_kept, r * 2 + (c - 1 + KEPT0))
                d.tensor_scalar(hn[:, h, :], tile_of(x_all, r * 2 + c), mv[:, h, 0:1], rs[:, h:h + 1],
                                ALU.subtract, ALU.mult).then_inc(h_ready, 1)

            def logit(r, c):
                h = c % 2
                d.wait_ge(l_done, r * 2 + (c + 1))
                d.tensor_tensor(tile_of(logits, r * 2 + c), l_banks[h][:, 0:EXPERTS], gbias[:, :], ALU.add).then_inc(l_added, 1)

            def body(r, first=False, last=False):
                for h in range(2):
                    if not (first and h == 0):
                        norm(r, h - 1)
                    add(r, h)
                    if not first:
                        logit(r, h - 2)

            d.sem_inc(l_added, ADDED0)
            d.wait_ge(w_in, 48)
            rounds(d, body)
            norm(PAIRS - 1, 1)
            for h in range(2):
                logit(PAIRS - 1, h)

        @block.scalar
        def _(a):
            def turned(r, c):
                h = c % 2
                a.wait_ge(a_turned, r * 2 + (c + 1 + TURN0))
                a.activation(at_[:, h, :], a_banks[h][:, 0:D], ACT.Copy).then_inc(a_copied, 1)

            def keep(r, c):
                h = c % 2
                a.wait_ge(h_turned, r * 2 + (c + 1))
                a.activation(ht[:, h, :], h_banks[h][:, 0:D], ACT.Copy).then_inc(h_copied, 1)
                a.activation(tile_of(rows_all, r * 2 + c), hn[:, h, :], ACT.Copy).then_inc(rows_kept, 1)

            def body(r, first=False, last=False):
                for h in range(2):
                    if not (last and h):
                        turned(r, h + 1)
                    if not (first and h == 0):
                        keep(r, h - 1)
                    a.wait_ge(var, r * 2 + (h + 1))
                    a.activation(rs[:, h:h + 1], rs[:, h:h + 1], ACT.Sqrt).then_inc(std, 1)

            a.sem_inc(rows_kept, KEPT0)
            turned(0, 0)
            rounds(a, body)
            keep(PAIRS - 1, 1)

        @block.tensor
        def _(t):
            def turn(bank, rows, signal, ready, r, c):
                h = c % 2
                t.wait_ge(ready, r * 2 + (c + 1))
                for k in range(KB):
                    last = nc.tensor.transpose(bank[h][:, k * P:(k + 1) * P], rows[:, h, k * P:(k + 1) * P], ident[:, :])
                last.then_inc(signal, 1)

            def product(bank, cols, rows, w, ready, signal, r, c):
                h = c % 2
                t.wait_ge(ready, r * 2 + (c + 1))
                for k in range(KB):
                    last = nc.tensor.matmul(bank[h][:, 0:cols], rows[:, h, k * P:(k + 1) * P], w[:, k, :],
                                            start=(k == 0), stop=(k == KB - 1))
                last.then_inc(signal, 1)

            def messages(r, c):
                if not (isinstance(r, int) and r * 2 + c < 2):
                    t.wait_ge(a_copied, r * 2 + (c - 1))
                h = c % 2
                t.wait_ge(part_in[h], r * (16 * NACC) + 16 * NACC * (1 + c // 2))
                for k in range(KB):
                    for n in range(NACC):
                        last = nc.tensor.matmul(a_banks[h][:, k * P:(k + 1) * P], part[:, h, n, k * P:(k + 1) * P], ident[:, :],
                                                start=(n == 0), stop=(n == NACC - 1))
                last.then_inc(a_turned, 1)

            def logit(r, c):
                t.wait_ge(l_added, r * 2 + (c - 1 + ADDED0))
                product(l_banks, EXPERTS, ht, gw, h_copied, l_done, r, c)

            def body(r, first=False, last=False):
                for h in range(2):
                    if not first:
                        t.wait_ge(var, r * 2 + (h - 1))
                    product(o_banks, D, at_, wo, a_copied, o_done, r, h)
                    if not first:
                        logit(r, h - 2)
                    if not (last and h):
                        messages(r, h + 1)
                    if not (first and h == 0):
                        turn(h_banks, hn, h_turned, h_ready, r, h - 1)

            t.sem_inc(a_turned, TURN0)
            t.wait_ge(w_in, 48)
            messages(0, 0)
            rounds(t, body)
            for h in range(2):
                if h:
                    turn(h_banks, hn, h_turned, h_ready, PAIRS - 1, 1)
                logit(PAIRS - 1, h)


def build_experts(nc, sem, sb, banks, v):
    x_all, send_all, ident, logits = v["x_all"], v["send_all"], v["ident"], v["logits"]
    upto, ones, slots, out_rows = v["upto"], v["ones"], v["slots"], v["out"]
    LIVE = REAL_TILES
    ctx = ExitStack()
    with ctx:
        def s(name): return sem("x_" + name, ctx)

        idle = s("idle")

        def b(name, shape, dt=fp32): return sb("x_" + name, shape, dt, ctx)

        TE = [P, TILES, EXPERTS]
        number, best, shown, hot = b("number", TE), b("best", [P, TILES]), b("shown", TE), b("hot", TE)
        probs, sums, pick, place = b("probs", TE), b("sums", [P, TILES]), b("pick", [P, TILES]), b("place", TE)
        carry, pos, kept = b("carry", TE), b("pos", [P, TILES]), b("kept", [P, TILES])
        base, running = b("base", [P, TILES]), b("running", TE)
        put, node = b("put", [P, TILES], i32), b("node", [P, TILES])
        w1, w2 = b("w1", [P, 2, KB, FF]), b("w2", [P, 2, FC, D])
        b1s, b2 = b("b1s", [P, 2, FC]), b("b2", [P, 2, D])
        rows, cols = b("rows", [P, 2, CT, DS]), b("cols", [P, KB, CPAD])
        mid, ans = b("mid", [P, FC, CPAD]), b("ans", [P, 2, CT, D])
        over = b("over", [P, D], u32)
        zero_row, top_row, low_row = b("zero_row", [P, D]), b("top_row", [P, D]), b("low_row", [P, D])
        spare, empty, target = b("spare", [P, 1]), b("empty", [P, 2, CT]), b("target", [P, 2, CT], i32)

        (d_own, numbered, shifted, exped, hot_ready, place_done, put_ready, moved, turned, c_copied, m_done,
         m_ready, y_done, ans_ready, guarded, ans_free, tick) = (
            s(n) for n in ("d_own numbered shifted exped hot_ready place_done put_ready moved turned c_copied "
                           "m_done m_ready y_done ans_ready guarded ans_free tick").split())
        load_in, added = [s("load_in0"), s("load_in1")], s("added")
        block = ctx.enter_context(nc.Block())

        @block.sync
        def _(sp):
            def weights(e, h):
                one = bass.ds(e, 1)
                sp.dma_start(w1[:, h, :, :], v["e_w1"][one, :, :].rearrange("a (k p) f -> p (a k) f", p=P)).then_inc(load_in[h], 16)
                sp.dma_start(w2[:, h, :, :], v["e_w2"][one, :, :].rearrange("a (k p) c -> p (a k) c", p=P)).then_inc(load_in[h], 16)
                sp.dma_start(b1s[:, h, :], v["e_b1"][one, :, :].rearrange("a p f -> (a p) f")).then_inc(load_in[h], 16)
                sp.dma_start(b2[:, h, :], v["e_b2"][one, :].to_broadcast([P, D])).then_inc(load_in[h], 16)

            def tokens(e, h):
                sp.dma_start(rows[:, h, :, :], slots.rearrange("(e t p) c -> e p t c", p=P, t=CT)[bass.ds(e, 1), :, :, :]
                             .rearrange("a p t c -> (a p) t c")).then_inc(load_in[h], 16)

            weights(0, 0)
            weights(1, 1)
            sp.wait_ge(moved, 16 * LIVE)
            tokens(0, 0)
            tokens(1, 1)
            with sp.Fori(0, EXPERTS // 2 - 1) as r:
                for h in range(2):
                    sp.wait_ge(guarded, r * (2 * CT) + CT * (h + 1))
                    nxt = r * 2 + (2 + h)
                    weights(nxt, h)
                    tokens(nxt, h)
            for h in range(2):
                sp.wait_ge(load_in[h], 80 * (EXPERTS // 2))

        @block.gpsimd
        def _(g):
            g.iota(number[:, :, :], [[0, TILES], [1, EXPERTS]], base=0, channel_multiplier=0,
                   allow_small_or_imprecise_dtypes=True).then_inc(numbered, 1)
            g.iota(node[:, :], [[P, TILES]], base=1, channel_multiplier=1,
                   allow_small_or_imprecise_dtypes=True).then_inc(numbered, 1)
            g.iota(spare[:, :], [[1, 1]], base=REAL_TILES * P + 1, channel_multiplier=1,
                   allow_small_or_imprecise_dtypes=True).then_inc(numbered, 1)
            g.dma_start(out_rows.rearrange("(t p) c -> p t c", p=P), x_all[:, :, :]).then_inc(added, 16)
            g.wait_ge(put_ready, 1)
            for t in range(LIVE):
                g.indirect_dma_start(slots, bass.IndirectOffsetOnAxis(ap=put[:, t:t + 1], axis=0), send_all[:, t, :], None,
                                     bounds_check=EXPERTS * CPAD - 1, oob_is_err=False).then_inc(moved, 16)
            with g.Fori(0, EXPERTS // 2) as r:
                for h in range(2):
                    for c in range(CT):
                        g.wait_ge(guarded, r * (2 * CT) + (CT * h + c + 1))
                        g.wait_ge(added, r * (32 * CT) + 16 * (CT * h + c + 1))
                        g.sem_inc(tick, 1)
                        if c == 0:
                            g.sem_inc(ans_free, 1)
                        g.indirect_dma_start(out_rows, bass.IndirectOffsetOnAxis(ap=target[:, h, c:c + 1], axis=0),
                                             ans[:, h, c, :], None, compute_op=ALU.add).then_inc(added, 16)
            g.wait_ge(added, 16 * (CT * EXPERTS + 1))

        @block.vector
        def _(d):
            own = Own(d, d_own)
            wide = TE

            def over_experts(a): return a.unsqueeze(2).to_broadcast(wide)

            own.link(d.memset(zero_row[:, :], 0.0))
            own.link(d.memset(top_row[:, :], 10000.0))
            own.link(d.memset(low_row[:, :], -10000.0))
            own.link(d.tensor_reduce(best[:, :], logits[:, :, :], AX.X, ALU.max))
            d.tensor_tensor(shown[:, :, :], logits[:, :, :], over_experts(best[:, :]), ALU.subtract).then_inc(shifted, 1)
            d.wait_ge(exped, 1)
            own.link(d.tensor_reduce(sums[:, :], probs[:, :, :], AX.X, ALU.add))
            own.link(d.reciprocal(sums[:, :], sums[:, :]))
            own.link(d.tensor_tensor(probs[:, :, :], probs[:, :, :], over_experts(sums[:, :]), ALU.mult))
            own.link(d.tensor_reduce(best[:, :], probs[:, :, :], AX.X, ALU.max))
            own.link(d.tensor_tensor(shown[:, :, :], probs[:, :, :], over_experts(best[:, :]), ALU.is_lt))
            d.wait_ge(numbered, 3)
            own.link(d.scalar_tensor_tensor(out=shown[:, :, :], in0=shown[:, :, :], scalar=float(EXPERTS),
                                            in1=number[:, :, :], op0=ALU.mult, op1=ALU.add))
            own.link(d.tensor_reduce(pick[:, :], shown[:, :, :], AX.X, ALU.min))
            own.link(d.tensor_tensor(hot[:, :, :], number[:, :, :], over_experts(pick[:, :]), ALU.is_equal))
            own.link(d.memset(carry[:, 0, :], 0.0))
            own.link(d.tensor_copy(carry[:, 1:TILES, :], hot[:, 0:TILES - 1, :]))
            step, a_, b_ = 1, carry, place
            while step < TILES:
                own.link(d.tensor_copy(b_[:, 0:step, :], a_[:, 0:step, :]))
                own.link(d.tensor_tensor(b_[:, step:TILES, :], a_[:, step:TILES, :], a_[:, 0:TILES - step, :], ALU.add))
                step, a_, b_ = 2 * step, b_, a_
            own.link(d.tensor_copy(running[:, :, :], a_[:, :, :]))
            d.sem_inc(hot_ready, 1)
            d.wait_ge(place_done, 1)
            own.link(d.tensor_tensor(place[:, :, :], hot[:, :, :],
                                     banks[0][:, 0:TILES * EXPERTS].rearrange("p (t e) -> p t e", e=EXPERTS), ALU.mult))
            own.link(d.tensor_reduce(pos[:, :], place[:, :, :], AX.X, ALU.add))
            own.link(d.tensor_scalar(pos[:, :], pos[:, :], -1.0, None, ALU.add))
            own.link(d.tensor_scalar(kept[:, :], pos[:, :], float(CAP), None, ALU.is_lt))
            own.link(d.tensor_copy(send_all[:, :, D:D + 1], best[:, :].unsqueeze(2)))
            own.link(d.tensor_copy(send_all[:, :, D + 1:DS], node[:, :].unsqueeze(2)))
            own.link(d.tensor_scalar(base[:, :], pick[:, :], float(CPAD), None, ALU.mult))
            own.link(d.tensor_scalar(kept[:, :], kept[:, :], float(-FAR), float(FAR), ALU.mult, ALU.add))
            own.link(d.tensor_tensor(kept[:, :], kept[:, :], pos[:, :], ALU.add))
            d.tensor_tensor(put[:, :], kept[:, :], base[:, :], ALU.add).then_inc(put_ready, 1)
            d.sem_inc(ans_free, 1)
            d.sem_inc(ans_ready, 2)
            first, LINKS = own.n, 2 + 7 * CT
            with d.Fori(0, EXPERTS // 2) as r:
                for h in range(2):
                    mine = Own(d, d_own, first + LINKS * h, 2 * LINKS, r)
                    d.wait_ge(ans_free, r * 2 + (h + 1))
                    d.wait_ge(load_in[h], r * 80 + 80)
                    number_ = rows[:, h, :, D + 1]
                    mine.link(d.tensor_scalar(empty[:, h, :], number_, 0.0, spare[:, 0:1], ALU.is_equal, ALU.mult))
                    mine.link(d.scalar_tensor_tensor(out=target[:, h, :], in0=number_, scalar=-1.0, in1=empty[:, h, :],
                                                     op0=ALU.add, op1=ALU.add))
                    for c in range(CT):
                        d.wait_ge(y_done, r * (2 * CT) + (CT * h + c + 1))
                        one = ans[:, h, c, :]
                        d.tensor_tensor(one, banks[4 + c % 2][:, 0:D], b2[:, h, :], ALU.add).then_inc(ans_ready, 1)
                        d.wait_ge(ans_ready, r * (2 * CT) + (CT * h + c + 3))
                        mine.link(d.tensor_scalar(one, one, rows[:, h, c, D:D + 1], None, ALU.mult))
                        mine.link(d.tensor_tensor(over[:, :], one, one, ALU.not_equal))
                        mine.rest(idle)
                        mine.link(d.copy_predicated(one, over[:, :], zero_row[:, :]))
                        for row, limit, op in ((top_row, BIG, ALU.is_gt), (low_row, -BIG, ALU.is_lt)):
                            mine.link(d.tensor_scalar(over[:, :], one, limit, None, op))
                            mine.rest(idle)
                            mine.link(d.copy_predicated(one, over[:, :], row[:, :]))
                        d.sem_inc(guarded, 1)
                    assert mine.n - mine.start == LINKS

        @block.scalar
        def _(a):
            a.wait_ge(shifted, 1)
            a.activation(probs[:, :, :].rearrange("p t e -> p (t e)"), shown[:, :, :].rearrange("p t e -> p (t e)"),
                         ACT.Exp).then_inc(exped, 1)
            with a.Fori(0, EXPERTS // 2) as r:
                for h in range(2):
                    for k in range(KB):
                        a.wait_ge(turned, r * (2 * KB) + (KB * h + k + 1))
                        a.activation(cols[:, k, :], banks[k][:, :], ACT.Copy).then_inc(c_copied, 1)
                    for f in range(FC):
                        a.wait_ge(m_done, r * (2 * FC) + (FC * h + f + 1))
                        a.activation(mid[:, f, :], banks[2 + f % 2][:, :], ACT.Relu, bias=b1s[:, h, f:f + 1])\
                         .then_inc(m_ready, 1)

        @block.tensor
        def _(t_):
            t_.wait_ge(hot_ready, 1)
            n = TILES * EXPERTS
            nc.tensor.matmul(banks[0][:, 0:n], upto[:, :], hot[:, :, :].rearrange("p t e -> p (t e)"), start=True, stop=False)
            nc.tensor.matmul(banks[0][:, 0:n], ones[:, :], running[:, :, :].rearrange("p t e -> p (t e)"), start=False, stop=True)\
              .then_inc(place_done, 1)
            t_.wait_ge(put_ready, 1)
            with t_.Fori(0, EXPERTS // 2) as r:
                for h in range(2):
                    t_.wait_ge(load_in[h], r * 80 + 80)
                    for k in range(KB):
                        for c in range(CT):
                            last = nc.tensor.transpose(banks[k][:, c * P:(c + 1) * P], rows[:, h, c, k * P:(k + 1) * P], ident[:, :])
                        last.then_inc(turned, 1)
                    t_.wait_ge(c_copied, r * (2 * KB) + KB * (h + 1))
                    for f in range(FC):
                        if f >= 2:
                            t_.wait_ge(m_ready, r * (2 * FC) + (FC * h + f - 1))
                        for k in range(KB):
                            last = nc.tensor.matmul(banks[2 + f % 2][:, :], w1[:, h, k, f * P:(f + 1) * P], cols[:, k, :],
                                                    start=(k == 0), stop=(k == KB - 1))
                        last.then_inc(m_done, 1)
                    t_.wait_ge(m_ready, r * (2 * FC) + FC * (h + 1))
                    for c in range(CT):
                        t_.wait_ge(ans_ready, r * (2 * CT) + (CT * h + c + 1))
                        for f in range(FC):
                            last = nc.tensor.matmul(banks[4 + c % 2][:, 0:D], mid[:, f, c * P:(c + 1) * P], w2[:, h, f, :],
                                                    start=(f == 0), stop=(f == FC - 1))
                        last.then_inc(y_done, 1)


def build(nc, *arrays):
    v = dict(zip(ARRAYS, arrays))
    top = ExitStack()
    with top:
        def sem(name, ctx=top): return ctx.enter_context(nc.semaphore(name))

        def sb(name, shape, dt=fp32, ctx=top): return ctx.enter_context(nc.sbuf_tensor(name, shape, dt))

        def dram(name, rows, cols):
            return nc.dram_tensor(name, [rows, cols], fp32, kind="Internal").ap()

        v["kv_table"], v["q_table"] = dram("kv_table", ROWS, 2 * D), dram("q_table", ROWS, D)
        v["parts_table"] = nc.dram_tensor("parts_table", [ROWS, 3 * D], bf16, kind="Internal").ap()
        v["acc"] = [dram(f"acc{k}", ROWS + P, D) for k in range(NACC)]
        v["slots"] = dram("slots", EXPERTS * CPAD, DS)
        banks = [top.enter_context(nc.psum_tensor(f"bank{k}", [P, 512], fp32)) for k in range(8)]
        v["x_all"] = sb("x_all", [P, TILES, D])
        v["send_all"] = sb("send_all", [P, TILES, DS])
        v["rows_all"] = v["send_all"][:, :, 0:D]
        v["ident"], v["ones"] = sb("ident", [P, P]), sb("ones", [P, P])
        v["before"], v["upto"] = sb("before", [P, P]), sb("upto", [P, P])
        v["kv_sum"] = sb("kv_sum", [P, KB, P + 1])
        v["base_i"], v["base_all"] = sb("base_i", [P, GROUPS], i32), sb("base_all", [P, GROUPS])
        v["near_flag"], v["far_flag"] = sb("near_flag", [P, 1], i32), sb("far_flag", [P, 1], i32)
        v["mix_q"] = sb("mix_q", [P, TILES + 1, D])
        v["logits"] = sb("logits", [P, TILES, EXPERTS])
        v["consts_made"] = sem("consts_made")
        v["mixer_signals"] = [sem("mix_" + name) for name in Mixer.SIGNALS]
        build_nodes(nc, sem, sb, banks, v)
        build_near_edges(nc, sem, sb, banks, v)
        build_mixer(nc, sem, sb, banks, v)
        build_edges(nc, sem, sb, banks, v)
        build_routing(nc, sem, sb, banks, v)
        build_experts(nc, sem, sb, banks, v)


ARRAYS = ("x", "row_mask", "head_mask", "src", "dst", "dst_row", "weight", "attr", "ln_gb", "w_gnn", "b_gnn", "wo", "bo",
          "w_edge", "w_mix", "wm", "w1m", "w2m", "gb_mix", "gate_w", "gate_b", "e_w1", "e_b1", "e_w2", "e_b2", "out")


def kernel(**inputs):
    import numpy as np
    import concourse.bacc as bacc
    from concourse.bass_utils import run_bass_kernel_spmd

    a = {k: np.asarray(x) for k, x in inputs.items()}
    g = {k[7:]: x for k, x in a.items() if k.startswith("L0_gnn_")}
    m = {k[7:]: x for k, x in a.items() if k.startswith("L0_mix_")}
    f = {k[7:]: x for k, x in a.items() if k.startswith("L0_ffn_")}
    slots_all = (ROUNDS + 1) * CH * P
    more = slots_all - EDGES

    def to_chunks(e, fill):
        return np.pad(e, (0, more), constant_values=fill).reshape(ROUNDS + 1, CH, P)

    def spread(row):
        return np.broadcast_to(row, (P,) + row.shape)

    attr = np.concatenate([np.pad(a["edge_attr_64"], ((0, more), (0, 0))).T, np.ones((1, slots_all), np.float32)])
    arrays = {
        "x": np.pad(a["x"], ((0, ROWS - NODES), (0, 0))),
        "row_mask": (np.arange(ROWS) < NODES).astype(np.float32).reshape(TILES, P).T,
        "head_mask": (np.arange(P)[:, None] // HD == np.arange(HB)).astype(np.float32),
        "src": to_chunks(a["src"], 0).transpose(0, 2, 1),
        "dst": to_chunks(a["dst"], NODES).transpose(0, 2, 1),
        "dst_row": to_chunks(a["dst"], NODES).reshape(ROUNDS + 1, CH * P),
        "weight": to_chunks(a["edge_weight"], 0).transpose(0, 2, 1),
        "attr": attr.reshape(KE, ROUNDS + 1, CH * P),
        "ln_gb": spread(np.stack([g["ln_g"], g["ln_b"]])),
        "w_gnn": np.concatenate([g["Wq"].T, g["Wk"].T, g["Wv"].T], 1),
        "b_gnn": spread(np.concatenate([g["bq"], g["bk"], g["bv"]])),
        "wo": g["Wo"].T, "bo": spread(g["bo"]),
        "w_edge": np.concatenate([np.concatenate([g["Wdk"].T, g["Wdv"].T], 1), np.concatenate([g["bdk"], g["bdv"]])[None]]),
        "w_mix": np.concatenate([m["Wq"], m["Wk"], m["Wv"]], 1),
        "wm": m["Wm"], "w1m": m["W1"], "w2m": m["W2"],
        "gb_mix": spread(np.stack([m["g1"], m["b1"], m["g2"], m["b2"]])),
        "gate_w": f["gate_w"], "gate_b": spread(f["gate_b"]),
        "e_w1": f["w1"], "e_b1": f["b1"].reshape(EXPERTS, FC, P).transpose(0, 2, 1), "e_w2": f["w2"], "e_b2": f["b2"],
    }
    arrays = {f"in_{k}": np.ascontiguousarray(arrays[k]) for k in ARRAYS[:-1]}
    nc = bacc.Bacc("TRN2", target_bir_lowering=False, num_devices=1)
    args = [nc.dram_tensor(k, x.shape, mybir.dt.from_np(x.dtype), kind="ExternalInput").ap() for k, x in arrays.items()]
    args.append(nc.dram_tensor("out_rows", [ROWS, D], fp32, kind="ExternalOutput").ap())
    build(nc, *args)
    r = run_bass_kernel_spmd(nc, [arrays], core_ids=[0])
    return r.results[0]["out_rows"][:NODES]
```
